# Optimizing a Trainium2 kernel written in Bass

```python
import numpy as np
import jax
import jax.numpy as jnp

def _softmax(x, axis=-1):
    return jax.nn.softmax(x, axis=axis)

def _gelu(x):
    return jax.nn.gelu(x, approximate=True)

def _silu(x):
    return jax.nn.silu(x)

def _sigmoid(x):
    return jax.nn.sigmoid(x)

def _layernorm(x, axis=-1, eps=1e-05):
    m = jnp.mean(x, axis=axis, keepdims=True)
    v = jnp.var(x, axis=axis, keepdims=True)
    return (x - m) / jnp.sqrt(v + eps)

def _scatter_add(tgt, idx, src, axis=0):
    return tgt.at[idx].add(src)

def _segment_sum(src, seg, n):
    return jax.ops.segment_sum(src, seg, n)
kernel_name = 'mk_flamingo_gated_d2_seqx_r4_fdfbdc'

def setup_inputs(seed: int=0):
    np.random.seed(seed)
    _w = jnp.asarray

    def _rec_inputs():
        import jax
        import jax.numpy as jnp
        _rk = jax.random.key(seed)
        x = -0.0003929 + 0.9999 * jax.random.normal(jax.random.fold_in(_rk, 1), (32, 128, 256), jnp.float32)
        _lenS = 128 - jax.random.randint(jax.random.fold_in(_rk, 7), (32,), 0, max(1, 128 // 4) + 1, jnp.int32)
        _lenS2 = 128 - jax.random.randint(jax.random.fold_in(_rk, 8), (32,), 0, max(1, 128 // 4) + 1, jnp.int32)
        _ctx_1024P = jax.random.normal(jax.random.fold_in(_rk, 11), (32, 16, 256), jnp.float32)
        _ctx_1024c = jax.random.dirichlet(jax.random.fold_in(_rk, 511), 0.3 * jnp.ones((16,), jnp.float32), (32, 128))
        _ctx_1024t = jnp.einsum('bsk,bkd->bsd', _ctx_1024c, _ctx_1024P)
        _ctx_1024t = _ctx_1024t * jax.lax.rsqrt(jnp.mean(jnp.square(_ctx_1024t)) + 1e-12) * 0.953939
        ctx_1024 = 2.81802e-05 + 1.00001 * (_ctx_1024t + 0.3 * jax.random.normal(jax.random.fold_in(_rk, 611), (32, 128, 256), jnp.float32))
        _g = jax.random.normal(jax.random.fold_in(_rk, 9001), (2, 2), jnp.float32)
        _g = jnp.sign(_g) * jnp.maximum(jnp.abs(_g), 1.0) + (_g == 0) * 1.0
        g_xattn = _g[0]
        g_ffn = _g[1]
        return (x, ctx_1024, g_xattn, g_ffn)
    x, ctx_1024, g_xattn, g_ffn = _rec_inputs()

    def _L0_xattn_setup():
        import jax, jax.numpy as jnp
        import numpy as np
        NUM_HEADS = 8
        BLOCK_SIZE = 128

        def _split_blocks(x, H, nb, bs, d):
            B, S, E = x.shape
            return x.reshape(B, S, H, d).transpose(0, 2, 1, 3).reshape(B, H, nb, bs, d)
        key = jax.random.key(seed)
        kq, kk, kv = jax.random.split(key, 3)
        B, S, E = (4, 1024, 256)
        return {'query': jax.random.normal(kq, (B, S, E), dtype=jnp.float32), 'key': jax.random.normal(kk, (B, S, E), dtype=jnp.float32), 'value': jax.random.normal(kv, (B, S, E), dtype=jnp.float32)}
    _L0_xattn_all = _L0_xattn_setup()
    _L0_xattn_in = {k: v for k, v in _L0_xattn_all.items() if k in ()}
    del _L0_xattn_all

    def _L0_ffn_setup():
        import jax, jax.numpy as jnp
        import numpy as np
        D_MODEL = 256
        M = 64
        INNER = 16
        key = jax.random.key(seed)
        ks = jax.random.split(key, 9)

        def init(k, shape, fan_in):
            bound = 1.0 / np.sqrt(fan_in)
            return jax.random.uniform(k, shape, jnp.float32, -bound, bound)
        x = jax.random.normal(ks[0], (16, 1024, D_MODEL), dtype=jnp.float32)
        Win = init(ks[1], (D_MODEL, M), D_MODEL)
        bin_ = init(ks[2], (M,), D_MODEL)
        W1 = init(ks[3], (M, INNER), 1)
        b1 = init(ks[4], (M, INNER), 1)
        W2 = init(ks[5], (M, INNER), INNER)
        b2 = init(ks[6], (M,), INNER)
        Wout = init(ks[7], (M, D_MODEL), M)
        bout = init(ks[8], (D_MODEL,), M)
        return {'x': x, 'Win': Win, 'bin_': bin_, 'W1': W1, 'b1': b1, 'W2': W2, 'b2': b2, 'Wout': Wout, 'bout': bout}
    _L0_ffn_all = _L0_ffn_setup()
    _L0_ffn_in = {k: v for k, v in _L0_ffn_all.items() if k in ('Win', 'bin_', 'W1', 'b1', 'W2', 'b2', 'Wout', 'bout')}
    del _L0_ffn_all

    def _L1_xattn_setup():
        import jax, jax.numpy as jnp
        import numpy as np
        DIM = 256
        NUM_HEADS = 16
        DIM_HEAD = 64
        INNER = NUM_HEADS * DIM_HEAD
        SCALE = DIM_HEAD ** (-0.5)

        def _layernorm(x, gamma, beta, eps=1e-05):
            mu = jnp.mean(x, axis=-1, keepdims=True)
            var = jnp.mean(jnp.square(x - mu), axis=-1, keepdims=True)
            return (x - mu) * jax.lax.rsqrt(var + eps) * gamma + beta
        key = jax.random.key(seed)
        ks = jax.random.split(key, 8)
        B, SQ, SK = (2, 512, 1024)
        x = jax.random.normal(ks[0], (B, SQ, DIM), dtype=jnp.float32)
        context = jax.random.normal(ks[1], (B, SK, DIM), dtype=jnp.float32)
        ln_gamma = jnp.ones((DIM,), jnp.float32)
        ln_beta = jnp.zeros((DIM,), jnp.float32)
        w_q = jax.random.normal(ks[2], (DIM, INNER), dtype=jnp.float32) / np.sqrt(DIM)
        w_kv = jax.random.normal(ks[3], (DIM, 2 * INNER), dtype=jnp.float32) / np.sqrt(DIM)
        w_out = jax.random.normal(ks[4], (INNER, DIM), dtype=jnp.float32) / np.sqrt(INNER)
        b_out = jnp.zeros((DIM,), jnp.float32)
        gate = jnp.array([0.5], jnp.float32)
        return {'x': x, 'context': context, 'ln_gamma': ln_gamma, 'ln_beta': ln_beta, 'w_q': w_q, 'w_kv': w_kv, 'w_out': w_out, 'b_out': b_out, 'gate': gate}
    _L1_xattn_all = _L1_xattn_setup()
    _L1_xattn_in = {k: v for k, v in _L1_xattn_all.items() if k in ('ln_gamma', 'ln_beta', 'w_q', 'w_kv', 'w_out', 'b_out', 'gate')}
    del _L1_xattn_all

    def _L1_ffn_setup():
        import jax, jax.numpy as jnp
        import numpy as np
        E = 32
        H = 256
        I = 128
        G = 8
        TKG = 4
        TOPK = 8
        NSH = 2
        SCALE = 2.5
        key = jax.random.key(seed)
        ks = jax.random.split(key, 10)
        s = 0.02
        return {'hidden_states': jax.random.normal(ks[0], (2, 256, H), jnp.float32), 'gate_w': jax.random.normal(ks[1], (E, H), jnp.float32) * s, 'gate_bias': jax.random.normal(ks[2], (E,), jnp.float32) * s, 'w_gate': jax.random.normal(ks[3], (E, I, H), jnp.float32) * s, 'w_up': jax.random.normal(ks[4], (E, I, H), jnp.float32) * s, 'w_down': jax.random.normal(ks[5], (E, H, I), jnp.float32) * s, 'sh_gate': jax.random.normal(ks[6], (I * NSH, H), jnp.float32) * s, 'sh_up': jax.random.normal(ks[7], (I * NSH, H), jnp.float32) * s, 'sh_down': jax.random.normal(ks[8], (H, I * NSH), jnp.float32) * s}
    _L1_ffn_all = _L1_ffn_setup()
    _L1_ffn_in = {k: v for k, v in _L1_ffn_all.items() if k in ('gate_w', 'gate_bias', 'w_gate', 'w_up', 'w_down', 'sh_gate', 'sh_up', 'sh_down')}
    del _L1_ffn_all
    return {'x': x, 'ctx_1024': ctx_1024, 'g_xattn': g_xattn, 'g_ffn': g_ffn, 'L0_ffn_Win': _L0_ffn_in['Win'], 'L0_ffn_bin_': _L0_ffn_in['bin_'], 'L0_ffn_W1': _L0_ffn_in['W1'], 'L0_ffn_b1': _L0_ffn_in['b1'], 'L0_ffn_W2': _L0_ffn_in['W2'], 'L0_ffn_b2': _L0_ffn_in['b2'], 'L0_ffn_Wout': _L0_ffn_in['Wout'], 'L0_ffn_bout': _L0_ffn_in['bout'], 'L1_xattn_ln_gamma': _L1_xattn_in['ln_gamma'], 'L1_xattn_ln_beta': _L1_xattn_in['ln_beta'], 'L1_xattn_w_q': _L1_xattn_in['w_q'], 'L1_xattn_w_kv': _L1_xattn_in['w_kv'], 'L1_xattn_w_out': _L1_xattn_in['w_out'], 'L1_xattn_b_out': _L1_xattn_in['b_out'], 'L1_xattn_gate': _L1_xattn_in['gate'], 'L1_ffn_gate_w': _L1_ffn_in['gate_w'], 'L1_ffn_gate_bias': _L1_ffn_in['gate_bias'], 'L1_ffn_w_gate': _L1_ffn_in['w_gate'], 'L1_ffn_w_up': _L1_ffn_in['w_up'], 'L1_ffn_w_down': _L1_ffn_in['w_down'], 'L1_ffn_sh_gate': _L1_ffn_in['sh_gate'], 'L1_ffn_sh_up': _L1_ffn_in['sh_up'], 'L1_ffn_sh_down': _L1_ffn_in['sh_down']}

def reference(x, ctx_1024, g_xattn, g_ffn, L0_ffn_Win, L0_ffn_bin_, L0_ffn_W1, L0_ffn_b1, L0_ffn_W2, L0_ffn_b2, L0_ffn_Wout, L0_ffn_bout, L1_xattn_ln_gamma, L1_xattn_ln_beta, L1_xattn_w_q, L1_xattn_w_kv, L1_xattn_w_out, L1_xattn_b_out, L1_xattn_gate, L1_ffn_gate_w, L1_ffn_gate_bias, L1_ffn_w_gate, L1_ffn_w_up, L1_ffn_w_down, L1_ffn_sh_gate, L1_ffn_sh_up, L1_ffn_sh_down):
    import jax
    import jax.numpy as jnp

    def _L0_xattn_ref(query, key, value):
        import jax, jax.numpy as jnp
        import numpy as np
        NUM_HEADS = 8
        BLOCK_SIZE = 128

        def _split_blocks(x, H, nb, bs, d):
            B, S, E = x.shape
            return x.reshape(B, S, H, d).transpose(0, 2, 1, 3).reshape(B, H, nb, bs, d)
        B, S, E = query.shape
        H, bs = (NUM_HEADS, BLOCK_SIZE)
        d = E // H
        nb = S // bs
        q = _split_blocks(query, H, nb, bs, d)
        k = _split_blocks(key, H, nb, bs, d)
        v = _split_blocks(value, H, nb, bs, d)
        scale = 1.0 / d ** 0.5
        scores = jnp.einsum('bhnqd,bhnkd->bhnqk', q, k) * scale
        weights = jax.nn.softmax(scores, axis=-1)
        out = jnp.einsum('bhnqk,bhnkd->bhnqd', weights, v)
        return out.reshape(B, H, S, d).transpose(0, 2, 1, 3).reshape(B, S, E)

    def _L0_ffn_ref(x, Win, bin_, W1, b1, W2, b2, Wout, bout):
        import jax, jax.numpy as jnp
        import numpy as np
        D_MODEL = 256
        M = 64
        INNER = 16
        s = jnp.einsum('btd,dm->btm', x, Win) + bin_
        h = jax.nn.relu(s[..., None] * W1 + b1)
        g = jnp.einsum('btmh,mh->btm', h, W2) + b2
        out = jnp.einsum('btm,md->btd', g, Wout) + bout
        return out

    def _L1_xattn_ref(x, context, ln_gamma, ln_beta, w_q, w_kv, w_out, b_out, gate):
        import jax, jax.numpy as jnp
        import numpy as np
        DIM = 256
        NUM_HEADS = 16
        DIM_HEAD = 64
        INNER = NUM_HEADS * DIM_HEAD
        SCALE = DIM_HEAD ** (-0.5)

        def _layernorm(x, gamma, beta, eps=1e-05):
            mu = jnp.mean(x, axis=-1, keepdims=True)
            var = jnp.mean(jnp.square(x - mu), axis=-1, keepdims=True)
            return (x - mu) * jax.lax.rsqrt(var + eps) * gamma + beta
        B, SQ, _ = x.shape
        SK = context.shape[1]
        xn = _layernorm(x, ln_gamma, ln_beta)
        q = (xn @ w_q).reshape(B, SQ, NUM_HEADS, DIM_HEAD)
        kv = context @ w_kv
        k, v = jnp.split(kv, 2, axis=-1)
        k = k.reshape(B, SK, NUM_HEADS, DIM_HEAD)
        v = v.reshape(B, SK, NUM_HEADS, DIM_HEAD)
        scores = jnp.einsum('bqhd,bkhd->bhqk', q * SCALE, k)
        attn = jax.nn.softmax(scores, axis=-1)
        out = jnp.einsum('bhqk,bkhd->bqhd', attn, v).reshape(B, SQ, INNER)
        out = out @ w_out + b_out
        return out * jnp.tanh(gate[0])

    def _L1_ffn_ref(hidden_states, gate_w, gate_bias, w_gate, w_up, w_down, sh_gate, sh_up, sh_down):
        import jax, jax.numpy as jnp
        import numpy as np
        E = 32
        H = 256
        I = 128
        G = 8
        TKG = 4
        TOPK = 8
        NSH = 2
        SCALE = 2.5
        B, S, Hd = hidden_states.shape
        h = hidden_states.reshape(-1, Hd)
        logits = h.astype(jnp.float32) @ gate_w.T
        scores = jax.nn.sigmoid(logits)
        sc = scores + gate_bias
        grp = sc.reshape(-1, G, E // G)
        group_scores = jax.lax.top_k(grp, 2)[0].sum(-1)
        gidx = jax.lax.top_k(group_scores, TKG)[1]
        gmask = jnp.sum(jax.nn.one_hot(gidx, G, dtype=sc.dtype), axis=1)
        smask = jnp.repeat(gmask, E // G, axis=1)
        masked = jnp.where(smask > 0, sc, jnp.zeros_like(sc))
        tki = jax.lax.top_k(masked, TOPK)[1]
        tkw = jnp.take_along_axis(scores, tki, axis=1)
        tkw = tkw / (tkw.sum(-1, keepdims=True) + 1e-20)
        tkw = tkw * SCALE
        combine = (jax.nn.one_hot(tki, E, dtype=tkw.dtype) * tkw[..., None]).sum(1)
        g = jax.nn.silu(jnp.einsum('th,eih->tei', h, w_gate))
        u = jnp.einsum('th,eih->tei', h, w_up)
        routed = jnp.einsum('tei,ehi->th', g * u * combine[:, :, None], w_down)
        sg = jax.nn.silu(h @ sh_gate.T)
        shared = sg * (h @ sh_up.T) @ sh_down.T
        return (routed + shared).reshape(B, S, Hd)
    x = x + jnp.tanh(g_xattn[0]) * _L0_xattn_ref(_layernorm(x, axis=-1), ctx_1024, ctx_1024)
    x = x + jnp.tanh(g_ffn[0]) * _L0_ffn_ref(_layernorm(x, axis=-1), L0_ffn_Win, L0_ffn_bin_, L0_ffn_W1, L0_ffn_b1, L0_ffn_W2, L0_ffn_b2, L0_ffn_Wout, L0_ffn_bout)
    x = x + jnp.tanh(g_xattn[1]) * _L1_xattn_ref(_layernorm(x, axis=-1), ctx_1024, L1_xattn_ln_gamma, L1_xattn_ln_beta, L1_xattn_w_q, L1_xattn_w_kv, L1_xattn_w_out, L1_xattn_b_out, L1_xattn_gate)
    x = x + jnp.tanh(g_ffn[1]) * _L1_ffn_ref(_layernorm(x, axis=-1), L1_ffn_gate_w, L1_ffn_gate_bias, L1_ffn_w_gate, L1_ffn_w_up, L1_ffn_w_down, L1_ffn_sh_gate, L1_ffn_sh_up, L1_ffn_sh_down)
    return x

_drawn_inputs = setup_inputs


def setup_inputs(seed=0):
    import zlib

    import numpy as np

    out = dict(_drawn_inputs(seed))
    spreads = {'g_ffn': (-1.0, 0.6),
     'L1_xattn_ln_gamma': (1.0, 0.6),
     'L1_xattn_ln_beta': (0.0, 0.8),
     'L1_xattn_b_out': (0.0, 0.1)}
    factors = {'L0_ffn_bin_': 8.0,
     'L1_ffn_gate_w': 8.0,
     'L1_ffn_gate_bias': 8.0,
     'L1_ffn_w_gate': 7.944,
     'L1_ffn_w_up': 7.806,
     'L1_ffn_w_down': 7.811,
     'L1_ffn_sh_gate': 4.972,
     'L1_ffn_sh_up': 4.956,
     'L1_ffn_sh_down': 4.933}
    for name, (base, spread) in spreads.items():
        noise = np.random.default_rng([zlib.crc32(name.encode()), seed]).standard_normal(out[name].shape)
        drawn = base * np.exp(spread * noise) if base else spread * noise
        out[name] = jnp.asarray(drawn.astype(out[name].dtype))
    for name, factor in factors.items():
        out[name] = (out[name] * factor).astype(out[name].dtype)
    return out
```

```python
from contextlib import ExitStack

import concourse.bass as bass
from concourse import mybir

F32 = mybir.dt.float32
F32R = mybir.dt.float32r
ALU = mybir.AluOpType
ACT = mybir.ActivationFunctionType
X = mybir.AxisListType.X

P = 128
D = 256
K2 = D // P
BANK = 512
EPS = 1e-5


class Chain:

    def __init__(self, eng, sem):
        self.eng, self.sem, self.base, self.n = eng, sem, 0, 0

    def step(self, ins):
        ins.then_inc(self.sem, 1)
        self.n += 1
        return ins

    def settle(self):
        self.eng.wait_ge(self.sem, self.base + self.n)

    def enter_loop(self, it, per):
        self.before, self.base, self.n = self.base + self.n, self.base + self.n + it * per, 0
        self.per = per

    def leave_loop(self, trips):
        assert self.n == self.per, (self.n, self.per)
        self.base, self.n = self.before + trips * self.per, 0


def build(nc, a):
    NB = a["x"].shape[0]
    NT = NB * P
    with ExitStack() as ctx:
        k = Kernel(nc, a, NB, ctx)
        constants(k)
        attention0(k)
        with ExitStack() as inner:
            k.awh = inner.enter_context(nc.sbuf_tensor("attn_w_high", [P, a["attn_w"].shape[1]], F32R))
            k.awl = inner.enter_context(nc.sbuf_tensor("attn_w_low", [P, a["attn_w"].shape[1]], F32R))
            relu_ffn(k)
            attention1(k)
        with ExitStack() as inner:
            k.hTh = inner.enter_context(nc.sbuf_tensor("hT_high", [P, K2, NT], F32R))
            k.hTl = inner.enter_context(nc.sbuf_tensor("hT_low", [P, K2, NT], F32R))
            router(k)
            experts(k)
        store(k)


class Kernel:
    def __init__(self, nc, a, NB, ctx):
        self.nc, self.a, self.NB = nc, a, NB

        def sb(name, shape, dt=F32):
            return ctx.enter_context(nc.sbuf_tensor(name, shape, dt))

        self.bank = [ctx.enter_context(nc.psum_tensor(f"bank{i}", [P, BANK], F32)) for i in range(8)]
        self.xs = sb("x_resident", [P, NB, D])
        self.ident = sb("identity", [P, P])
        self.gates = sb("gates_raw", [P, 5])
        self.tg = sb("gates_tanh", [P, 6])
        self.minus_half, self.eps, self.zero = sb("minus_half", [P, 1]), sb("eps", [P, 1]), sb("zero", [P, 1])
        self.diag = sb("w2_diagonals", [P, 8, 64])
        self.w1 = sb("w1_columns", [P, 8])
        self.negb1 = sb("minus_b1", [P, 8])
        self.bin = sb("bin_column", [P, 1])
        self.gbias = sb("g_bias", [64, 1])
        self.win = sb("win", [P, K2, P])
        self.wout0 = sb("wout_and_bout", [65, D])
        self.comb = sb("combine", [P, NB, 34])


TG_X0, TG_X1, TG_F0, TG_F1, TG_GATE, TG_X1GATE = range(6)


def rstd_steps(pool, k, n, mv, veps, rstd, stats_ready, veps_done, rstd_ready):
    pool.wait_ge(stats_ready, n + 1)
    pool.tensor_tensor(veps, mv[:, 1:2], k.eps[:], ALU.add).then_inc(veps_done, 1)
    pool.wait_ge(veps_done, n + 1)
    pool.tensor_tensor(rstd, veps, k.minus_half[:], ALU.pow).then_inc(rstd_ready, 1)


def three_passes(pe, out, ah, al, bh, bl, first, last):
    pe.matmul(out, ah, bh, start=first, stop=False)
    pe.matmul(out, al, bh, start=False, stop=False)
    return pe.matmul(out, ah, bl, start=False, stop=last)


def constants(k):
    nc, a = k.nc, k.a
    with ExitStack() as c:
        sem = lambda n: c.enter_context(nc.semaphore(n))
        sb = lambda n, s: c.enter_context(nc.sbuf_tensor(n, s, F32))
        loaded, tanh_done, chain_sem, half_done = sem("c_loaded"), sem("c_tanh"), sem("c_chain"), sem("c_half")
        eye2, w2, w2row, b1row, prod, b1c, b2c = (sb("eye2", [P, 64]), sb("w2c", [P, 8]), sb("w2row", [64, 16]),
                                                  sb("b1row", [64, 16]), sb("prod", [64, 16]),
                                                  sb("b1c", [P, 8]), sb("b2c", [64, 1]))
        psum_b = sb("w2b1", [64, 1])
        block = c.enter_context(nc.Block())
        loads = [(k.ident, "ident"), (k.gates, "gates"), (eye2, "eye2"), (k.w1, "w1c"), (b1c, "b1c"),
                 (w2, "w2c"), (w2row, "w2row"), (b1row, "b1row"), (b2c, "b2c"), (k.bin, "binc"),
                 (k.win, "win"), (k.wout0, "wout0")]

        @block.sync
        def _(sp):
            for dst, name in loads:
                sp.dma_start(dst[:], a[name]).then_inc(loaded, 16)

        @block.gpsimd
        def _(pool):
            pool.memset(k.minus_half[:], -0.5).then_inc(half_done, 1)
            pool.memset(k.eps[:], EPS).then_inc(half_done, 1)
            pool.memset(k.zero[:], 0.0).then_inc(half_done, 1)

        @block.scalar
        def _(act):
            act.wait_ge(loaded, 16 * len(loads))
            act.activation(k.tg[:, 0:5], k.gates[:], ACT.Tanh).then_inc(tanh_done, 1)

        @block.vector
        def _(dve):
            chain = Chain(dve, chain_sem)
            dve.wait_ge(loaded, 16 * len(loads))
            for j in range(8):
                chain.step(dve.tensor_scalar(k.diag[:, j, :], eye2[:], w2[:, j:j + 1], None, ALU.mult))
            chain.step(dve.tensor_scalar(k.negb1[:], b1c[:], -1.0, None, ALU.mult))
            chain.step(dve.tensor_tensor(prod[:], w2row[:], b1row[:], ALU.mult))
            chain.settle()
            chain.step(dve.tensor_reduce(psum_b[:], prod[:], X, ALU.add))
            chain.settle()
            chain.step(dve.tensor_tensor(k.gbias[:], psum_b[:], b2c[:], ALU.add))
            dve.wait_ge(tanh_done, 1)
            chain.step(dve.tensor_tensor(k.tg[:, 5:6], k.tg[:, TG_X1:TG_X1 + 1],
                                         k.tg[:, TG_GATE:TG_GATE + 1], ALU.mult))



def moments(dve, src, stats, mv, stats_ready):
    dve.bn_stats(stats, src)
    dve.drain()
    dve.bn_aggr(mv, stats).then_inc(stats_ready, 1)


def apply_norm(dve, src, dst, mv, rstd, rstd_ready, n):
    dve.wait_ge(rstd_ready, n + 1)
    return dve.tensor_scalar(dst, src, mv[:, 0:1], rstd, ALU.subtract, ALU.mult)


def attention0(k):
    nc, a, NB = k.nc, k.a, k.NB
    H, DH = 8, 32
    SCALE = DH ** -0.5
    U = 4
    trips = NB // U - 1
    with ExitStack() as c:
        sem = lambda n: c.enter_context(nc.semaphore("a0_" + n))
        sb = lambda n, s, dt=F32: c.enter_context(nc.sbuf_tensor("a0_" + n, s, dt))
        x_loaded, rows_loaded = sem("x_loaded"), sem("rows_loaded")
        ctx_loaded = [sem(f"ctx_loaded{i}") for i in range(U)]
        stats_ready, veps_done, rstd_ready = sem("stats_ready"), sem("veps_done"), sem("rstd_ready")
        xn_ready, t_ready, q_copied = sem("xn_ready"), sem("t_ready"), sem("q_copied")
        s_ready, max_ready, exp_done = sem("s_ready"), sem("max_ready"), sem("exp_done")
        pt_ready, pt_copied = sem("pt_ready"), sem("pt_copied")
        ov_ready, ov_copied, added = sem("ov_ready"), sem("ov_copied"), sem("added")
        dve_chain = sem("dve_chain")
        ctxT = sb("ctxT", [P, U, K2, P])
        cv = sb("ctx", [P, U, D])
        xn = sb("xn", [P, 2, D])
        qT = sb("qT", [P, 2, K2, 4, P])
        head_rows = sb("head_rows", [P, 4])
        pr = sb("probs", [P, 2, H, P])
        pT = sb("probsT", [P, 2, H, P])
        stats, mv, veps, rstd = sb("stats", [P, 6]), sb("mv", [P, 2]), sb("veps", [P, 1]), sb("rstd", [P, 1])
        nmax, rsum = sb("minus_max", [P, 2, H]), sb("row_sum", [P, 2, H])
        rinv = sb("inverse_sum", [P, 2, H])
        upd = sb("update", [P, 2, D])
        S, BT, BP0, BP1, BO = k.bank[0:4], k.bank[4], k.bank[5], k.bank[6], k.bank[7]
        block = c.enter_context(nc.Block())

        @block.sync
        def _(sp):
            def x_chunk(n):
                sp.dma_start(k.xs[:, bass.ds(n * U, U), :],
                             a["x"][bass.ds(n * U, U)].rearrange("b p d -> p b d")).then_inc(x_loaded, 16)

            def context(pair, half, slot):
                sp.dma_start(ctxT[:, slot], a["ctxT"][pair, :, :, half, :]).then_inc(ctx_loaded[slot], 16)
                sp.dma_start(cv[:, slot], a["ctx"][pair, half]).then_inc(ctx_loaded[slot], 16)

            x_chunk(0)
            sp.dma_start(head_rows[:], a["head_rows"]).then_inc(rows_loaded, 16)
            for j in range(U):
                context(j // 2, j % 2, j)
            sp.wait_ge(x_loaded, 16)
            x_chunk(1)

            def body(it, more_x):
                if more_x:
                    sp.wait_ge(x_loaded, it * 16 + 32)
                    x_chunk(it + 2)
                for j in range(U):
                    sp.wait_ge(ov_ready, it * U + j + 1)
                    context(it * 2 + 2 + j // 2, j % 2, j)

            with sp.Fori(0, trips - 1) as it:
                body(it, True)
            body(trips - 1, False)

        @block.gpsimd
        def _(pool):
            def inverse_deviation(n):
                rstd_steps(pool, k, n, mv, veps[:], rstd[:], stats_ready, veps_done, rstd_ready)

            pool.sem_inc(added, 1)
            for n in range(4):
                inverse_deviation(n)

            def body(it, last):
                for j in range(U):
                    b = it * U + j
                    if not last:
                        inverse_deviation(b + 4)
                    pool.wait_ge(ov_copied, b + 2)
                    xb = k.xs[:, b, :]
                    pool.tensor_tensor(xb, xb, upd[:, j % 2, :], ALU.add).then_inc(added, 1)

            with pool.Fori(0, trips) as it:
                body(it, False)
            body(trips, True)

        @block.vector
        def _(dve):
            chain = Chain(dve, dve_chain)

            def measure(b, x_count):
                dve.wait_ge(x_loaded, x_count)
                moments(dve, k.xs[:, b, :], stats[:], mv[:], stats_ready)

            def apply(b, par):
                apply_norm(dve, k.xs[:, b, :], xn[:, par, :], mv, rstd[:], rstd_ready, b).then_inc(xn_ready, 1)

            def norm(b, par, x_count):
                measure(b, x_count)
                apply(b, par)

            def queries(b, par):
                dve.wait_ge(t_ready, b + 1)
                for kk in range(K2):
                    ins = dve.tensor_tensor(qT[:, par, kk],
                                            BT[:, kk * P:kk * P + P].unsqueeze(1).broadcast_to([P, 4, P]),
                                            head_rows[:].unsqueeze(2).broadcast_to([P, 4, P]), ALU.mult)
                ins.then_inc(q_copied, 1)

            def maxima(b, par):
                dve.wait_ge(s_ready, b + 1)
                for kk in range(K2):
                    ins = dve.tensor_reduce(nmax[:, par, kk * 4:kk * 4 + 4],
                                            S[par * 2 + kk][:].rearrange("p (j t) -> p j t", j=4),
                                            X, ALU.max, negate=True)
                ins.then_inc(max_ready, 1)

            def inverse_sums(b, par):
                dve.wait_ge(exp_done, b + 1)
                chain.step(dve.reciprocal(rinv[:, par, :], rsum[:, par, :]))

            def output(b, par):
                chain.settle()
                dve.wait_ge(ov_ready, b + 1)
                dve.wait_ge(added, b + 1)
                dve.scalar_tensor_tensor(upd[:, par, :].rearrange("p (h e) -> p h e", h=H),
                                         BO[:, 0:D].rearrange("p (h e) -> p h e", h=H), k.tg[:, TG_X0:TG_X0 + 1],
                                         rinv[:, par, :].unsqueeze(2).broadcast_to([P, H, DH]),
                                         ALU.mult, ALU.mult).then_inc(ov_copied, 1)

            dve.sem_inc(ov_copied, 1)
            norm(0, 0, 16)
            norm(1, 1, 16)
            dve.wait_ge(rows_loaded, 16)
            queries(0, 0)
            norm(2, 0, 16)
            queries(1, 1)
            norm(3, 1, 16)
            maxima(0, 0)
            queries(2, 0)
            maxima(1, 1)

            def body(it, last):
                for j in range(U):
                    b, par = it * U + j, j % 2
                    if not last:
                        measure(b + 4, it * 16 + 32)
                    inverse_sums(b, par)
                    if not last or j + 2 < U:
                        maxima(b + 2, par)
                    if not last:
                        apply(b + 4, par)
                    if not last or j + 3 < U:
                        queries(b + 3, 1 - par)
                    output(b, par)

            with dve.Fori(0, trips) as it:
                chain.enter_loop(it, U)
                body(it, False)
            chain.leave_loop(trips)
            body(trips, True)

        @block.scalar
        def _(act):
            def exponentials(b, par, heads):
                act.wait_ge(max_ready, b + 1)
                for h in heads:
                    kk, j = divmod(h, 4)
                    ins = act.activation(pr[:, par, h, :], S[par * 2 + kk][:, j * P:j * P + P], ACT.Exp,
                                         bias=nmax[:, par, h:h + 1], accum_out=rsum[:, par, h:h + 1])
                return ins

            exponentials(0, 0, range(H)).then_inc(exp_done, 1)

            def body(it, last):
                for j in range(U):
                    b, par = it * U + j, j % 2
                    for n in range(2):
                        if not last or j + 1 < U:
                            ins = exponentials(b + 1, 1 - par, range(4 * n, 4 * n + 4))
                            if n == 1:
                                ins.then_inc(exp_done, 1)
                        act.wait_ge(pt_ready, b * 2 + 1 + n)
                        act.activation(pT[:, par, 4 * n:4 * n + 4, :], (BP0, BP1)[n][:], ACT.Copy)\
                           .then_inc(pt_copied, 1)

            with act.Fori(0, trips) as it:
                body(it, False)
            body(trips, True)

        @block.tensor
        def _(pe):
            def transposed_queries(b, par):
                pe.wait_ge(xn_ready, b + 1)
                pe.wait_ge(q_copied, b)
                for kk in range(K2):
                    ins = pe.transpose(BT[:, kk * P:kk * P + P],
                                       xn[:, par, kk * P:kk * P + P], k.ident[:])
                ins.then_inc(t_ready, 1)

            def scores(b, par, slot, loads):
                pe.wait_ge(ctx_loaded[slot], loads)
                pe.wait_ge(q_copied, b + 1)
                for kk in range(K2):
                    for j in range(4):
                        ins = pe.matmul(S[par * 2 + kk][:, j * P:j * P + P], qT[:, par, kk, j, :],
                                        ctxT[:, slot, kk, :], start=True, stop=True)
                ins.then_inc(s_ready, 1)

            transposed_queries(0, 0)
            transposed_queries(1, 1)
            scores(0, 0, 0, 32)
            transposed_queries(2, 0)
            scores(1, 1, 1, 32)

            def body(it, last):
                for j in range(U):
                    b, par = it * U + j, j % 2
                    pe.wait_ge(exp_done, b + 1)
                    for h in range(H):
                        bank = (BP0, BP1)[h // 4]
                        ins = pe.transpose(bank[:, h % 4 * P:h % 4 * P + P], pr[:, par, h, :], k.ident[:])
                        if h % 4 == 3:
                            ins.then_inc(pt_ready, 1)
                    if not last or j + 2 < U:
                        scores(b + 2, par, (j + 2) % U, (it + (j + 2) // U) * 32 + 32)
                    if not last or j + 3 < U:
                        transposed_queries(b + 3, 1 - par)
                    pe.wait_ge(pt_copied, b * 2 + 2)
                    pe.wait_ge(ov_copied, b + 1)
                    for h in range(H):
                        ins = pe.matmul(BO[:, h * DH:h * DH + DH],
                                        pT[:, par, h, :], cv[:, j, h * DH:h * DH + DH], start=True, stop=True)
                    ins.then_inc(ov_ready, 1)

            with pe.Fori(0, trips) as it:
                body(it, False)
            body(trips, True)


def relu_ffn(k):
    nc, NB = k.nc, k.NB
    G = BANK // P
    NBLK, M = NB // G, 64
    LOOPED = NBLK - 3
    with ExitStack() as c:
        sem = lambda n: c.enter_context(nc.semaphore("f0_" + n))
        sb = lambda n, s: c.enter_context(nc.sbuf_tensor("f0_" + n, s, F32))
        stats_ready, veps_done, rstd_ready = sem("stats_ready"), sem("veps_done"), sem("rstd_ready")
        xn_ready, xt_ready, xt_copied = sem("xn_ready"), sem("xt_ready"), sem("xt_copied")
        s_ready, s_copied, h_ready, g_step = sem("s_ready"), sem("s_copied"), sem("h_ready"), sem("g_step")
        g_copied, o_ready, o_added = sem("g_copied"), sem("o_ready"), sem("o_added")
        ones_set = sem("ones_set")
        xn, xT = sb("xn", [P, G, D]), sb("xT", [P, K2, BANK])
        s, h = sb("s", [P, BANK]), sb("h", [P, 8, BANK])
        gT = sb("gT", [M + 1, BANK])
        stats, mv = sb("stats", [P, G, 6]), sb("mv", [P, G, 2])
        veps, rstd = sb("veps", [P, G]), sb("rstd", [P, G])
        half = sb("half", [P, G])
        half_set = sem("half_set")
        w_loaded, w_high, w_split = [sem("w_loaded0"), sem("w_loaded1")], sem("w_high"), sem("w_split")
        WCH = k.a["attn_w"].shape[1] // NBLK
        raw = sb("w_raw", [P, 2, WCH])
        BX, BS, BG, BOUT = k.bank[0:2], k.bank[2], k.bank[3], k.bank[4:6]
        block = c.enter_context(nc.Block())

        def steps(eng, body):
            with eng.Fori(0, LOOPED) as t:
                body(t, 0)
            for t in range(LOOPED, NBLK):
                body(t, t - LOOPED + 1)

        @block.gpsimd
        def _(pool):
            pool.memset(gT[M:M + 1, :], 1.0).then_inc(ones_set, 1)
            pool.wait_ge(ones_set, 1)
            pool.memset(half[:], -0.5).then_inc(half_set, 1)
            pool.wait_ge(half_set, 1)

            def split(t, par, loads):
                at = bass.ds(t * WCH, WCH)
                pool.wait_ge(w_loaded[par], loads * 16)
                pool.tensor_copy(k.awh[:, at], raw[:, par, :]).then_inc(w_high, 1)
                pool.wait_ge(w_high, t + 1)
                pool.tensor_tensor(k.awl[:, at], raw[:, par, :], k.awh[:, at].bitcast(F32),
                                   ALU.subtract).then_inc(w_split, 1)

            def inverse_deviations(t):
                pool.wait_ge(stats_ready, t + 1)
                pool.tensor_tensor(veps[:], mv[:, :, 1], k.eps[:].broadcast_to([P, G]), ALU.add).then_inc(veps_done, 1)
                pool.wait_ge(veps_done, t + 1)
                pool.tensor_tensor(rstd[:], veps[:], half[:], ALU.pow).then_inc(rstd_ready, 1)

            with pool.Fori(0, NBLK // 2) as it:
                for par in range(2):
                    inverse_deviations(it * 2 + par)
                    split(it * 2 + par, par, it + 1)

        @block.sync
        def _(sp):
            def load(t, par):
                sp.dma_start(raw[:, par, :], k.a["attn_w"][:, bass.ds(t * WCH, WCH)]).then_inc(w_loaded[par], 16)

            load(0, 0)
            load(1, 1)
            with sp.Fori(0, NBLK // 2 - 1) as it:
                for par in range(2):
                    sp.wait_ge(w_split, it * 2 + par + 1)
                    load(it * 2 + par + 2, par)

        @block.vector
        def _(dve):
            def norm(t):
                for j in range(G):
                    dve.bn_stats(stats[:, j, :], k.xs[:, t * G + j, :])
                dve.drain()
                for j in range(G):
                    ins = dve.bn_aggr(mv[:, j, :], stats[:, j, :])
                ins.then_inc(stats_ready, 1)
                dve.wait_ge(rstd_ready, t + 1)
                for j in range(G):
                    ins = dve.tensor_scalar(xn[:, j, :], k.xs[:, t * G + j, :], mv[:, j, 0:1], rstd[:, j:j + 1],
                                            ALU.subtract, ALU.mult)
                ins.then_inc(xn_ready, 1)

            def hidden(t, used):
                dve.wait_ge(s_ready, t + 1)
                dve.wait_ge(h_ready, t * 8)
                dve.tensor_scalar(s[:], BS[:], k.bin[:], None, ALU.add).then_inc(s_copied, 1)
                dve.wait_ge(s_copied, t + 1)
                for j in range(8):
                    if used is not None:
                        dve.wait_ge(g_step, used + j + 1)
                    dve.tensor_scalar(h[:, j, :], s[:], k.w1[:, j:j + 1], k.negb1[:, j:j + 1],
                                      ALU.mult, ALU.max).then_inc(h_ready, 1)

            dve.sem_inc(o_added, 1)
            norm(0)
            dve.wait_ge(xt_ready, 1)
            norm(1)
            hidden(0, None)
            dve.wait_ge(xt_ready, 2)
            norm(2)

            def body(t, tail):
                if tail < 3:
                    hidden(t + 1, t * 8)
                if tail < 1:
                    dve.wait_ge(xt_ready, t + 3)
                    norm(t + 3)
                dve.wait_ge(o_ready, t + 1)
                for j in range(G):
                    xb = k.xs[:, t * G + j, :]
                    ins = dve.scalar_tensor_tensor(xb, BOUT[j // 2][:, j % 2 * D:j % 2 * D + D],
                                                   k.tg[:, TG_F0:TG_F0 + 1], xb, ALU.mult, ALU.add)
                ins.then_inc(o_added, 1)

            steps(dve, body)

        @block.scalar
        def _(act):
            def xt_copy(t):
                act.wait_ge(xt_ready, t + 1)
                for kk in range(K2):
                    ins = act.activation(xT[:, kk, :], BX[kk][:], ACT.Copy)
                ins.then_inc(xt_copied, 1)

            xt_copy(0)
            xt_copy(1)

            def body(t, tail):
                act.wait_ge(g_step, t * 8 + 8)
                act.activation(gT[0:M, :], BG[0:M, :], ACT.Identity, bias=k.gbias[:]).then_inc(g_copied, 1)
                if tail < 2:
                    xt_copy(t + 2)

            steps(act, body)

        @block.tensor
        def _(pe):
            def transposes(t):
                pe.wait_ge(xn_ready, t + 1)
                for kk in range(K2):
                    for j in range(G):
                        ins = pe.transpose(BX[kk][:, j * P:j * P + P], xn[:, j, kk * P:kk * P + P], k.ident[:])
                ins.then_inc(xt_ready, 1)

            def first_product(t):
                pe.wait_ge(xt_copied, t + 1)
                pe.wait_ge(s_copied, t)
                for kk in range(K2):
                    ins = pe.matmul(BS[:], k.win[:, kk, :], xT[:, kk, :], start=kk == 0, stop=kk == K2 - 1)
                ins.then_inc(s_ready, 1)

            transposes(0)
            first_product(0)
            transposes(1)
            pe.wait_ge(ones_set, 1)

            def body(t, tail):
                if tail < 3:
                    first_product(t + 1)
                for j in range(8):
                    pe.wait_ge(h_ready, t * 8 + j + 1)
                    pe.matmul(BG[0:M, :], k.diag[:, j, :], h[:, j, :], start=j == 0, stop=j == 7).then_inc(g_step, 1)
                if tail < 2:
                    transposes(t + 2)
                pe.wait_ge(g_copied, t + 1)
                pe.wait_ge(o_added, t + 1)
                for j in range(G):
                    ins = pe.matmul(BOUT[j // 2][:, j % 2 * D:j % 2 * D + D], gT[:, j * P:j * P + P], k.wout0[:],
                                    start=True, stop=True)
                ins.then_inc(o_ready, 1)

            steps(pe, body)


def attention1(k):
    nc, a, NB = k.nc, k.a, k.NB
    H, DH = 16, 64
    SCALE = DH ** -0.5
    NP = NB // 2
    trips = NP // 2 - 1
    INNER = H * DH
    KC = INNER // P
    FILL = ["XT", "K0", "K1", "Q0", "Q1", "K2", "K3", "Q2", "Q3", "V0", "V1", "V2", "V3"]
    NF = len(FILL)
    PER6, PER7 = (NF + 1) // 2, NF // 2
    with ExitStack() as c:
        sem = lambda n: c.enter_context(nc.semaphore("a1_" + n))
        sb = lambda n, s, dt=F32: c.enter_context(nc.sbuf_tensor("a1_" + n, s, dt))
        w_loaded, boadd_ready = sem("w_loaded"), sem("boadd_ready")
        ctx_loaded = [sem("ctx_loaded0"), sem("ctx_loaded1")]
        stats_ready, veps_done, rstd_ready = sem("stats_ready"), sem("veps_done"), sem("rstd_ready")
        xn_ready, proj_ready = sem("xn_ready"), sem("proj_ready")
        copied = [sem("copied6"), sem("copied7")]
        s_ready, max_ready, exp_done = sem("s_ready"), sem("max_ready"), sem("exp_done")
        pt_ready, pt0_copied, pt1_copied = sem("pt_ready"), sem("pt0_copied"), sem("pt1_copied")
        ov_ready, ov_copied, ot_ready, ot_copied = sem("ov_ready"), sem("ov_copied"), sem("ot_ready"), sem("ot_copied")
        w_ready, w_copied, biased, dve_chain = sem("w_ready"), sem("w_copied"), sem("biased"), sem("dve_chain")
        at_q, at_out = K2 * 2 * INNER, K2 * 3 * INNER
        wkv, wq, wout = ([w[:, lo:hi].rearrange("p (k n) -> p k n", k=kc) for w in (k.awh, k.awl)]
                         for lo, hi, kc in ((0, at_q, K2), (at_q, at_out, K2), (at_out, at_out + KC * D, KC)))
        gam, bet, bo = sb("gammaT", [P, K2]), sb("betaT", [P, K2]), sb("b_out", [P, D])
        raw = sb("ctxT", [P, 2, K2, 2, P])
        ctxT = [sb(n, [P, 2, K2, 2, P], F32R) for n in ("ctxT_high", "ctxT_low")]
        x1, xn, xTf = sb("x1", [P, D]), sb("xn", [P, 2, D]), sb("xT", [P, K2, 2 * P])
        xT = [sb(n, [P, K2, 2 * P], F32R) for n in ("xT_high", "xT_low")]
        qT, kT = sb("qT", [P, 2, KC, 2 * P]), sb("kT", [P, 2, KC, 2 * P])
        v = sb("v", [P, 2, 2, INNER])
        pr, pT = sb("probs", [P, 2, 8, P]), sb("probsT", [P, 2, 8, P])
        o = sb("o", [P, 2, BANK])
        oT = [sb(n, [P, KC, P], F32R) for n in ("oT_high", "oT_low")]
        ctx_high, ctx_split, xt_written, xt_high, xt_split, ot_high = (
            sem("ctx_high"), sem("ctx_split"), sem("xt_written"), sem("xt_high"), sem("xt_split"), sem("ot_high"))
        stats, mv, veps, rstd = sb("stats", [P, 6]), sb("mv", [P, 2]), sb("veps", [P, 1]), sb("rstd", [P, 1])
        nmax, rsum, rinv = sb("minus_max", [P, 2, 4, 2]), sb("row_sum", [P, 2, 8]), sb("inverse_sum", [P, 2, 8])
        block = c.enter_context(nc.Block())
        weights = [(gam, "gammaT"), (bet, "betaT"), (bo, "b_out")]

        def pairs(eng, body, enter=None, leave=None):
            with eng.Fori(0, trips) as it:
                if enter:
                    enter(it)
                for half in range(2):
                    body(it * 2 + half, it, half, 2)
            if leave:
                leave()
            for half in range(2):
                body(2 * trips + half, trips, half, 1 - half)

        @block.sync
        def _(sp):
            def context(p, half):
                sp.dma_start(raw[:, half], a["ctxT"][p]).then_inc(ctx_loaded[half], 16)

            context(0, 0)
            for dst, name in weights:
                sp.dma_start(dst[:], a[name]).then_inc(w_loaded, 16)
            context(1, 1)
            with sp.Fori(0, trips) as it:
                for half in range(2):
                    sp.wait_ge(ctx_split, it * 2 + half + 1)
                    context(it * 2 + half + 2, half)

        @block.gpsimd
        def _(pool):
            def inverse_deviation(n):
                rstd_steps(pool, k, n, mv, veps[:], rstd[:], stats_ready, veps_done, rstd_ready)

            pool.wait_ge(w_loaded, 16 * len(weights))
            pool.tensor_tensor(bo[:], bo[:], k.tg[:, TG_X1GATE:TG_X1GATE + 1].broadcast_to([P, D]),
                               ALU.mult).then_inc(boadd_ready, 1)
            pool.wait_ge(boadd_ready, 1)

            zeros = k.zero[:].unsqueeze(2).unsqueeze(3).broadcast_to([P, K2, 2, P])

            def split_context(q, half, loads):
                pool.wait_ge(ctx_loaded[half], loads * 16)
                pool.tensor_tensor(ctxT[0][:, half], raw[:, half], zeros, ALU.add).then_inc(ctx_high, 1)
                pool.wait_ge(ctx_high, q + 1)
                pool.tensor_tensor(ctxT[1][:, half], raw[:, half], ctxT[0][:, half].bitcast(F32),
                                   ALU.subtract).then_inc(ctx_split, 1)

            def low_input(q):
                pool.wait_ge(xt_high, q + 1)
                pool.tensor_tensor(xT[1][:], xTf[:], xT[0][:].bitcast(F32), ALU.subtract).then_inc(xt_split, 1)

            split_context(0, 0, 1)
            for n in range(4):
                inverse_deviation(n)
            low_input(0)
            for n in range(4, 8):
                inverse_deviation(n)
            split_context(1, 1, 1)

            def body(p, it, half, ahead):
                if ahead >= 1:
                    low_input(p + 1)
                if ahead >= 2:
                    pool.wait_ge(proj_ready, (p + 1) * NF)
                    split_context(p + 2, half, it + 2)
                    for n in range(4):
                        inverse_deviation(p * 4 + 8 + n)
                for j in range(2):
                    b = p * 2 + j
                    pool.wait_ge(w_copied, b + 2)
                    xb = k.xs[:, b, :]
                    pool.tensor_tensor(xb, xb, bo[:], ALU.add).then_inc(biased, 1)

            pairs(pool, body)

        def copy_projection(eng, is_act, half, i):
            bank = k.bank[6 + i % 2]
            kind, n = FILL[i][:-1], FILL[i][-1]
            if kind in "KQ":
                n = int(n)
                dst = (kT if kind == "K" else qT)[:, half, 2 * n:2 * n + 2, :]
                scale = SCALE if kind == "Q" else 1.0
                src = bank[:].rearrange("p (c t) -> p c t", c=2)
            else:
                n = int(n)
                dst, src, scale = v[:, half, n // 2, n % 2 * BANK:n % 2 * BANK + BANK], bank[:], 1.0
            if is_act:
                ins = eng.activation(dst, src, ACT.Copy, scale=scale)
            elif scale != 1.0:
                ins = eng.tensor_scalar(dst, src, scale, None, ALU.mult)
            else:
                ins = eng.tensor_copy(dst, src)
            ins.then_inc(copied[i % 2], 1)

        @block.vector
        def _(dve):
            chain = Chain(dve, dve_chain)

            def measure_x(b):
                moments(dve, k.xs[:, b, :], stats[:], mv[:], stats_ready)

            def measure_normed(b):
                chain.step(apply_norm(dve, k.xs[:, b, :], x1[:], mv, rstd[:], rstd_ready, b * 2))
                chain.settle()
                moments(dve, x1[:], stats[:], mv[:], stats_ready)

            def normed_input(b, par):
                apply_norm(dve, x1[:], xn[:, par, :], mv, rstd[:], rstd_ready, b * 2 + 1).then_inc(xn_ready, 1)

            def norm(b, par):
                measure_x(b)
                measure_normed(b)
                normed_input(b, par)

            def proj(q, half, i):
                if i % 2 == 1:
                    dve.wait_ge(proj_ready, q * NF + i + 1)
                    copy_projection(dve, False, half, i)

            def maxima(u, par):
                dve.wait_ge(s_ready, u + 1)
                for e in range(2):
                    ins = dve.tensor_reduce(nmax[:, par, :, e],
                                            k.bank[2 * par + e][:].rearrange("p (m t) -> p m t", m=4),
                                            X, ALU.max, negate=True)
                ins.then_inc(max_ready, 1)

            dve.sem_inc(ov_copied, 1)
            dve.sem_inc(ot_copied, 1)
            dve.sem_inc(w_copied, 1)
            norm(0, 0)
            norm(1, 1)
            for i in range(NF):
                proj(0, 0, i)
                if i == 3:
                    dve.wait_ge(proj_ready, 1)
                    norm(2, 0)
                    norm(3, 1)
            maxima(0, 0)
            maxima(1, 1)

            def body(p, it, half, ahead):
                for uu in range(4):
                    u, par = p * 4 + uu, uu % 2
                    normed = p * 2 + 4 + uu - 1 if ahead >= 2 and uu in (1, 2) else None
                    dve.wait_ge(pt_ready, u * 2 + 1)
                    dve.tensor_copy(pT[:, par, 0:4, :], k.bank[4][:]).then_inc(pt0_copied, 1)
                    if normed is not None:
                        measure_x(normed)
                    dve.wait_ge(exp_done, u + 1)
                    chain.step(dve.reciprocal(rinv[:, par, :], rsum[:, par, :]))
                    if ahead >= 1 or uu < 2:
                        maxima(u + 2, par)
                    if uu == 2:
                        residual(p * 2)
                    chain.settle()
                    dve.wait_ge(ov_ready, u + 1)
                    dve.tensor_tensor(o[:, par, :].rearrange("p (h e) -> p h e", h=8),
                                      k.bank[4][:].rearrange("p (h e) -> p h e", h=8),
                                      rinv[:, par, :].unsqueeze(2).broadcast_to([P, 8, DH]), ALU.mult)\
                       .then_inc(ov_copied, 1)
                    if normed is not None:
                        measure_normed(normed)
                    if ahead >= 1:
                        proj(p + 1, 1 - half, 3 * uu)
                        proj(p + 1, 1 - half, 3 * uu + 1)
                    if normed is not None:
                        if uu == 1:
                            dve.wait_ge(proj_ready, (p + 1) * NF + 1)
                        normed_input(normed, uu - 1)
                    low_output(u, uu)
                    if ahead >= 1:
                        proj(p + 1, 1 - half, 3 * uu + 2)
                        if uu == 3:
                            proj(p + 1, 1 - half, 12)
                residual(p * 2 + 1)

            def low_output(u, uu):
                at = slice(uu % 2 * 4, uu % 2 * 4 + 4)
                dve.wait_ge(ot_high, u + 1)
                dve.tensor_tensor(oT[1][:, at, :], k.bank[5][:].rearrange("p (c t) -> p c t", c=4),
                                  oT[0][:, at, :].bitcast(F32), ALU.subtract).then_inc(ot_copied, 1)

            def residual(b):
                dve.wait_ge(w_ready, b + 1)
                xb = k.xs[:, b, :]
                dve.scalar_tensor_tensor(xb, k.bank[5][:, 0:D], k.tg[:, TG_X1GATE:TG_X1GATE + 1], xb,
                                         ALU.mult, ALU.add).then_inc(w_copied, 1)

            pairs(dve, body, lambda it: chain.enter_loop(it, 2 * (4 + 2)), lambda: chain.leave_loop(trips))

        @block.scalar
        def _(act):
            act.wait_ge(w_loaded, 16 * len(weights))

            def proj(q, half, i):
                if i % 2 == 0:
                    act.wait_ge(proj_ready, q * NF + i + 1)
                    if i == 0:
                        for kk in range(K2):
                            ins = act.activation(xTf[:, kk, :], k.bank[6][:, kk * 2 * P:(kk + 1) * 2 * P], ACT.Identity,
                                                 bias=bet[:, kk:kk + 1], scale=gam[:, kk:kk + 1])
                        ins.then_inc(copied[0], 1)
                        act.wait_ge(copied[0], q * PER6 + 1)
                        act.activation(xT[0][:], xTf[:], ACT.Copy).then_inc(xt_high, 1)
                    else:
                        copy_projection(act, True, half, i)

            def exponentials(par, hs):
                for hh in hs:
                    m, e = divmod(hh, 2)
                    ins = act.activation(pr[:, par, hh, :], k.bank[2 * par + e][:, m * P:m * P + P], ACT.Exp,
                                         bias=nmax[:, par, m, e:e + 1], accum_out=rsum[:, par, hh:hh + 1])
                return ins

            for i in range(NF):
                proj(0, 0, i)
            act.wait_ge(max_ready, 1)
            exponentials(0, range(8)).then_inc(exp_done, 1)

            def body(p, it, half, ahead):
                for uu in range(4):
                    u, par, octet = p * 4 + uu, uu % 2, uu % 2
                    act.wait_ge(pt_ready, u * 2 + 2)
                    act.activation(pT[:, par, 4:8, :], k.bank[5][:], ACT.Copy).then_inc(pt1_copied, 1)
                    if ahead >= 1 or uu < 3:
                        act.wait_ge(max_ready, u + 2)
                        exponentials(1 - par, range(8)).then_inc(exp_done, 1)
                    if ahead >= 1:
                        proj(p + 1, 1 - half, 3 * uu)
                        proj(p + 1, 1 - half, 3 * uu + 1)
                    act.wait_ge(ot_ready, u + 1)
                    act.activation(oT[0][:, octet * 4:octet * 4 + 4, :], k.bank[5][:], ACT.Copy)\
                       .then_inc(ot_high, 1)
                    if ahead >= 1:
                        proj(p + 1, 1 - half, 3 * uu + 2)
                        if uu == 3:
                            proj(p + 1, 1 - half, 12)

            pairs(act, body)

        @block.tensor
        def _(pe):
            def proj(q, it, half, i):
                bank = k.bank[6 + i % 2]
                pe.wait_ge(copied[i % 2], q * (PER6, PER7)[i % 2] + i // 2)
                if i == 0:
                    pe.wait_ge(xn_ready, q * 2 + 2)
                    for kk in range(K2):
                        for j in range(2):
                            ins = pe.transpose(bank[:, kk * 2 * P + j * P:kk * 2 * P + j * P + P],
                                               xn[:, j, kk * P:kk * P + P], k.ident[:])
                    ins.then_inc(proj_ready, 1)
                    return
                kind, n = FILL[i][:-1], int(FILL[i][-1])
                if i == 1:
                    pe.wait_ge(ctx_split, q + 1)
                if kind == "Q" and n == 0:
                    pe.wait_ge(xt_split, q + 1)
                if kind == "K":
                    moving = [x[:, half].rearrange("p k b t -> p k (b t)") for x in ctxT]
                else:
                    moving = xT
                if kind in "KQ":
                    w = wkv if kind == "K" else wq
                    for j in range(2):
                        cols = slice((2 * n + j) * P, (2 * n + j + 1) * P)
                        for kk in range(K2):
                            ins = three_passes(pe, bank[:, j * 2 * P:(j + 1) * 2 * P], w[0][:, kk, cols],
                                               w[1][:, kk, cols], moving[0][:, kk, :], moving[1][:, kk, :],
                                               kk == 0, kk == K2 - 1)
                else:
                    cols = slice(INNER + n % 2 * BANK, INNER + (n % 2 + 1) * BANK)
                    for kk in range(K2):
                        ins = three_passes(pe, bank[:], ctxT[0][:, half, kk, n // 2, :],
                                           ctxT[1][:, half, kk, n // 2, :], wkv[0][:, kk, cols],
                                           wkv[1][:, kk, cols], kk == 0, kk == K2 - 1)
                ins.then_inc(proj_ready, 1)

            def scores(half, uu):
                b, octet = uu // 2, uu % 2
                for m in range(4):
                    for e in range(2):
                        r = slice(DH * e, DH * e + DH)
                        ins = pe.matmul(k.bank[2 * (uu % 2) + e][:, m * P:m * P + P],
                                        qT[r, half, octet * 4 + m, b * P:b * P + P],
                                        kT[r, half, octet * 4 + m, b * P:b * P + P], start=True, stop=True)
                ins.then_inc(s_ready, 1)

            def await_projected(q, name):
                upto = FILL.index(name) + 1
                pe.wait_ge(copied[0], q * PER6 + (upto + 1) // 2)
                pe.wait_ge(copied[1], q * PER7 + upto // 2)

            def projected(b):
                for cc in range(KC):
                    ins = three_passes(pe, k.bank[5][:, 0:D], oT[0][:, cc, :], oT[1][:, cc, :],
                                       wout[0][:, cc, :], wout[1][:, cc, :], cc == 0, cc == KC - 1)
                ins.then_inc(w_ready, 1)

            pe.wait_ge(w_loaded, 16 * len(weights))
            for i in range(NF):
                proj(0, 0, 0, i)
            await_projected(0, "Q3")
            scores(0, 0)
            scores(0, 1)

            def body(p, it, half, ahead):
                nxt = (p + 1, it + half, 1 - half)
                for uu in range(4):
                    u, par = p * 4 + uu, uu % 2
                    b, octet = uu // 2, uu % 2
                    pe.wait_ge(exp_done, u + 1)
                    pe.wait_ge(ov_copied, u + 1)
                    for hh in range(8):
                        if hh == 4:
                            pe.wait_ge(ot_copied, u + 1)
                            if uu == 0:
                                pe.wait_ge(w_copied, p * 2 + 1)
                        ins = pe.transpose(k.bank[4 + hh // 4][:, hh % 4 * P:hh % 4 * P + P],
                                           pr[:, par, hh, :], k.ident[:])
                        if hh % 4 == 3:
                            ins.then_inc(pt_ready, 1)
                    if uu < 2:
                        scores(half, uu + 2)
                    elif ahead >= 1:
                        await_projected(p + 1, "Q1" if uu == 2 else "Q3")
                        scores(1 - half, uu - 2)
                    pe.wait_ge(pt0_copied, u + 1)
                    pe.wait_ge(pt1_copied, u + 1)
                    if uu == 2:
                        projected(p * 2)
                    if uu == 0:
                        await_projected(p, "V3")
                    for hh in range(8):
                        g = octet * 8 + hh
                        ins = pe.matmul(k.bank[4][:, hh * DH:hh * DH + DH], pT[:, par, hh, :],
                                        v[:, half, b, g * DH:g * DH + DH], start=True, stop=True)
                    ins.then_inc(ov_ready, 1)
                    if ahead >= 1:
                        proj(*nxt, 3 * uu)
                        proj(*nxt, 3 * uu + 1)
                    pe.wait_ge(ov_copied, u + 2)
                    if uu == 2:
                        pe.wait_ge(w_copied, p * 2 + 2)
                    for cc in range(4):
                        ins = pe.transpose(k.bank[5][:, cc * P:cc * P + P],
                                           o[:, par, cc * P:cc * P + P], k.ident[:])
                    ins.then_inc(ot_ready, 1)
                    if ahead >= 1:
                        proj(*nxt, 3 * uu + 2)
                        if uu == 3:
                            proj(*nxt, 12)
                pe.wait_ge(ot_copied, p * 4 + 5)
                projected(p * 2 + 1)

            pairs(pe, body)


def router(k):
    nc, a, NB = k.nc, k.a, k.NB
    E, GR, TOPG = 32, 8, 4
    EG = E // GR
    with ExitStack() as c:
        sem = lambda n: c.enter_context(nc.semaphore("r_" + n))
        sb = lambda n, s: c.enter_context(nc.sbuf_tensor("r_" + n, s, F32))
        loaded, xn_ready, t_ready, hf_copied = sem("loaded"), sem("xn_ready"), sem("t_ready"), sem("hf_copied")
        hi_copied, lo_done, l_ready, sig_done = sem("hi_copied"), sem("lo_done"), sem("l_ready"), sem("sig_done")
        stats_ready, veps_done, rstd_ready = sem("stats_ready"), sem("veps_done"), sem("rstd_ready")
        dve_chain, route_chain = sem("dve_chain"), sem("route_chain")
        gw, bias, tri = sb("gate_wT", [P, K2, E]), sb("gate_bias", [P, E]), sb("earlier", [P, GR * GR])
        xn, hf = sb("xn", [P, 2, D]), sb("hT", [P, 2, K2, P])
        sc = sb("scores", [P, NB, E])
        stats, mv, veps, rstd = sb("stats", [P, 6]), sb("mv", [P, 2]), sb("veps", [P, 1]), sb("rstd", [P, 1])
        loads = [(gw, "gate_wT"), (bias, "gate_bias"), (tri, "earlier")]

        with nc.Block() as block:
            @block.sync
            def _(sp):
                for dst, name in loads:
                    sp.dma_start(dst[:], a[name]).then_inc(loaded, 16)

            @block.vector
            def _(dve):
                def measure(b):
                    moments(dve, k.xs[:, b, :], stats[:], mv[:], stats_ready)

                def apply(b, par):
                    apply_norm(dve, k.xs[:, b, :], xn[:, par, :], mv, rstd[:], rstd_ready, b).then_inc(xn_ready, 1)

                def copy(b, par):
                    dve.wait_ge(t_ready, b + 1)
                    dve.wait_ge(lo_done, b + 1)
                    dve.tensor_copy(hf[:, par], k.bank[par][:, 0:D].rearrange("p (k t) -> p k t", k=K2))\
                       .then_inc(hf_copied, 1)

                trips = NB // 2 - 1
                measure(0)
                apply(0, 0)
                measure(1)
                apply(1, 1)
                with dve.Fori(0, trips) as it:
                    for par in range(2):
                        measure(it * 2 + par + 2)
                        copy(it * 2 + par, par)
                        apply(it * 2 + par + 2, par)
                copy(NB - 2, 0)
                copy(NB - 1, 1)

            @block.gpsimd
            def _(pool):
                pool.sem_inc(lo_done, 2)

                def inverse_deviation(b):
                    rstd_steps(pool, k, b, mv, veps[:], rstd[:], stats_ready, veps_done, rstd_ready)

                def low(b, par):
                    pool.wait_ge(hf_copied, b + 1)
                    pool.wait_ge(hi_copied, b + 1)
                    at = bass.ds(b * P, P)
                    pool.tensor_tensor(k.hTl[:, :, at], hf[:, par], k.hTh[:, :, at].bitcast(F32),
                                       ALU.subtract).then_inc(lo_done, 1)

                inverse_deviation(0)
                inverse_deviation(1)
                trips = NB // 2 - 1
                with pool.Fori(0, trips) as it:
                    for par in range(2):
                        inverse_deviation(it * 2 + par + 2)
                        low(it * 2 + par, par)
                low(NB - 2, 0)
                low(NB - 1, 1)

            @block.scalar
            def _(act):
                act.sem_inc(sig_done, 2)

                def high(b, par):
                    act.wait_ge(hf_copied, b + 1)
                    act.activation(k.hTh[:, :, bass.ds(b * P, P)], hf[:, par], ACT.Copy).then_inc(hi_copied, 1)

                def sigmoid(b, par):
                    act.wait_ge(l_ready, b + 1)
                    act.activation(sc[:, b, :], k.bank[2 + par][:, 0:E], ACT.Sigmoid).then_inc(sig_done, 1)

                with act.Fori(0, NB // 2) as it:
                    for par in range(2):
                        high(it * 2 + par, par)
                        sigmoid(it * 2 + par, par)

            @block.tensor
            def _(pe):
                def transposed(b, par):
                    pe.wait_ge(xn_ready, b + 1)
                    for kk in range(K2):
                        ins = pe.transpose(k.bank[par][:, kk * P:kk * P + P], xn[:, par, kk * P:kk * P + P], k.ident[:])
                    ins.then_inc(t_ready, 1)

                def logits(b, par):
                    pe.wait_ge(hf_copied, b + 1)
                    pe.wait_ge(sig_done, b + 1)
                    for kk in range(K2):
                        ins = pe.matmul(k.bank[2 + par][:, 0:E], hf[:, par, kk, :], gw[:, kk, :],
                                        start=kk == 0, stop=kk == K2 - 1)
                    ins.then_inc(l_ready, 1)

                pe.wait_ge(loaded, 16 * len(loads))
                transposed(0, 0)
                transposed(1, 1)
                with pe.Fori(0, NB // 2 - 1) as it:
                    for par in range(2):
                        logits(it * 2 + par, par)
                        transposed(it * 2 + par + 2, par)
                for par in range(2):
                    logits(NB - 2 + par, par)

        tmp = [sb(f"t{i}", [P, NB, GR]) for i in range(5)]
        pair_gt, pair_eq = sb("greater", [P, NB, GR, GR]), sb("equal", [P, NB, GR, GR])
        rank, biased, masked, rest = (sb("rank", [P, NB, GR]), sb("biased", [P, NB, E]),
                                      sb("masked", [P, NB, E]), sb("rest", [P, NB, E]))
        top8, wsum = sb("top8", [P, NB, 8]), sb("wsum", [P, NB])

        with nc.Block() as block:
            @block.vector
            def _(dve):
                chain = Chain(dve, route_chain)

                def tt(out, x, y, op):
                    chain.step(dve.tensor_tensor(out, x, y, op))

                def then():
                    chain.settle()

                tt(biased[:], sc[:], bias[:].unsqueeze(1).broadcast_to([P, NB, E]), ALU.add)
                then()
                el = biased[:].rearrange("p b (g e) -> p b g e", e=EG)
                e0, e1, e2, e3 = (el[:, :, :, i] for i in range(4))
                tt(tmp[0][:], e0, e1, ALU.max)
                tt(tmp[1][:], e0, e1, ALU.min)
                tt(tmp[2][:], e2, e3, ALU.max)
                tt(tmp[3][:], e2, e3, ALU.min)
                then()
                tt(tmp[4][:], tmp[0][:], tmp[2][:], ALU.add)
                tt(tmp[1][:], tmp[0][:], tmp[1][:], ALU.add)
                tt(tmp[3][:], tmp[2][:], tmp[3][:], ALU.add)
                then()
                tt(tmp[1][:], tmp[1][:], tmp[3][:], ALU.max)
                then()
                gs = tmp[4]
                tt(gs[:], gs[:], tmp[1][:], ALU.max)
                then()
                other = gs[:].unsqueeze(2).broadcast_to([P, NB, GR, GR])
                own = gs[:].unsqueeze(3).broadcast_to([P, NB, GR, GR])
                earlier = tri[:].rearrange("p (g h) -> p g h", h=GR).unsqueeze(1).broadcast_to([P, NB, GR, GR])
                tt(pair_gt[:], other, own, ALU.is_gt)
                tt(pair_eq[:], other, own, ALU.is_equal)
                then()
                tt(pair_eq[:], pair_eq[:], earlier, ALU.mult)
                then()
                tt(pair_gt[:], pair_gt[:], pair_eq[:], ALU.add)
                then()
                chain.step(dve.tensor_reduce(rank[:], pair_gt[:], X, ALU.add))
                then()
                chain.step(dve.tensor_scalar(rank[:], rank[:], float(TOPG), None, ALU.is_lt))
                then()
                tt(masked[:].rearrange("p b (g e) -> p b g e", e=EG), el,
                   rank[:].unsqueeze(3).broadcast_to([P, NB, GR, EG]), ALU.mult)
                then()
                for b in range(NB):
                    chain.step(dve.max(top8[:, b, :], masked[:, b, :]))
                then()
                for b in range(NB):
                    chain.step(dve.match_replace(rest[:, b, :], top8[:, b, :], masked[:, b, :], -3.0e38))
                then()
                tt(rest[:], rest[:], masked[:], ALU.not_equal)
                then()
                tt(rest[:], rest[:], sc[:], ALU.mult)
                then()
                chain.step(dve.tensor_reduce(wsum[:], rest[:], X, ALU.add))
                then()
                chain.step(dve.tensor_scalar(wsum[:], wsum[:], 1e-20, None, ALU.add))
                then()
                chain.step(dve.reciprocal(wsum[:], wsum[:]))
                then()
                chain.step(dve.tensor_scalar(wsum[:], wsum[:], 2.5, k.tg[:, TG_F1:TG_F1 + 1], ALU.mult, ALU.mult))
                then()
                tt(k.comb[:, :, 0:E], rest[:], wsum[:].unsqueeze(2).broadcast_to([P, NB, E]), ALU.mult)
                chain.step(dve.tensor_copy(k.comb[:, :, E:E + 2],
                                           k.tg[:, TG_F1:TG_F1 + 1].unsqueeze(1).broadcast_to([P, NB, 2])))


def experts(k):
    nc, a, NB = k.nc, k.a, k.NB
    NE = a["experts"].shape[0]
    G = BANK // P
    BL = NB // G
    trips = NE // 2 - 1
    WG, WU, WD, WN = 0, D, 2 * D, 3 * D
    with ExitStack() as c:
        sem = lambda n: c.enter_context(nc.semaphore("e_" + n))
        sb = lambda n, s, dt=F32: c.enter_context(nc.sbuf_tensor("e_" + n, s, dt))
        w_loaded = [sem("w_loaded0"), sem("w_loaded1")]
        w_high, w_split, pool_copied = sem("w_high"), sem("w_split"), sem("weights_of_tokens")
        g_ready, u_ready, y_ready = sem("g_ready"), sem("u_ready"), sem("y_ready")
        silu_done, gu_done, hi_done, lo_done, acc_done = (sem("silu_done"), sem("gu_done"), sem("hi_done"),
                                                          sem("lo_done"), sem("acc_done"))
        raw = sb("w_raw", [P, 2, WN])
        wh, wl = sb("w_high", [P, 2, WN], F32R), sb("w_low", [P, 2, WN], F32R)
        ce = sb("token_weight", [P, 2, NB])
        silu, gu = sb("silu", [P, 2, BANK]), sb("gu", [P, 2, BANK])
        guh, gul = sb("gu_high", [P, 2, BANK], F32R), sb("gu_low", [P, 2, BANK], F32R)
        block = c.enter_context(nc.Block())

        def sweep(eng, body):
            with eng.Fori(0, trips) as it:
                for ep in range(2):
                    body(it * 2 + ep, ep, False)
            body(NE - 2, 0, False)
            body(NE - 1, 1, True)

        @block.sync
        def _(sp):
            def load(e, ep):
                sp.dma_start(raw[:, ep], a["experts"][e]).then_inc(w_loaded[ep], 16)

            load(0, 0)
            load(1, 1)
            with sp.Fori(0, trips) as it:
                for ep in range(2):
                    sp.wait_ge(w_split, it * 2 + ep + 1)
                    load(it * 2 + ep + 2, ep)

        @block.gpsimd
        def _(pool):
            def split(e, ep, loads):
                pool.wait_ge(w_loaded[ep], loads * 16)
                pool.tensor_copy(ce[:, ep, :], k.comb[:, :, e]).then_inc(pool_copied, 1)
                pool.tensor_copy(wh[:, ep], raw[:, ep]).then_inc(w_high, 1)
                pool.wait_ge(w_high, e + 1)
                pool.tensor_tensor(wl[:, ep], raw[:, ep], wh[:, ep].bitcast(F32), ALU.subtract).then_inc(w_split, 1)

            def low(s, par):
                pool.wait_ge(hi_done, s + 1)
                pool.tensor_tensor(gul[:, par], gu[:, par], guh[:, par].bitcast(F32), ALU.subtract)\
                    .then_inc(lo_done, 1)

            pool.sem_inc(lo_done, 2)
            split(0, 0, 1)

            def body(it, last):
                for ep in range(2):
                    e = it * 2 + ep
                    for blk in range(BL):
                        low(e * BL + blk, blk % 2)
                        if blk == 1 and not (last and ep == 1):
                            pool.wait_ge(acc_done, e * BL + 2)
                            split(e + 1, 1 - ep, it + 1 + ep)

            with pool.Fori(0, trips) as it:
                body(it, False)
            body(trips, True)

        @block.scalar
        def _(act):
            act.sem_inc(silu_done, 2)

            def step(s, par):
                act.wait_ge(g_ready, s + 1)
                act.wait_ge(gu_done, s + 1)
                act.activation(silu[:, par], k.bank[par][:], ACT.Silu).then_inc(silu_done, 1)
                act.wait_ge(gu_done, s + 3)
                act.activation(guh[:, par], gu[:, par], ACT.Copy).then_inc(hi_done, 1)

            sweep(act, lambda e, ep, last: [step(e * BL + blk, blk % 2) for blk in range(BL)])

        @block.vector
        def _(dve):
            dve.sem_inc(gu_done, 2)
            dve.sem_inc(acc_done, 2)

            def gated(s, par):
                dve.wait_ge(silu_done, s + 3)
                dve.wait_ge(u_ready, s + 1)
                dve.wait_ge(lo_done, s + 1)
                dve.tensor_tensor(gu[:, par], silu[:, par], k.bank[2 + par][:], ALU.mult).then_inc(gu_done, 1)

            def add(e, ep, blk):
                dve.wait_ge(y_ready, e * BL + blk + 1)
                for j in range(G):
                    b = blk * G + j
                    xb = k.xs[:, b, :]
                    bank = k.bank[4 + blk % 2 * 2 + j // 2]
                    ins = dve.scalar_tensor_tensor(xb, bank[:, j % 2 * D:j % 2 * D + D], ce[:, ep, b:b + 1], xb,
                                                   ALU.mult, ALU.add)
                ins.then_inc(acc_done, 1)

            gated(0, 0)

            def body(e, ep, last):
                for blk in range(BL):
                    if not (last and blk == BL - 1):
                        gated(e * BL + blk + 1, 1 - blk % 2)
                    add(e, ep, blk)

            sweep(dve, body)

        @block.tensor
        def _(pe):
            def gate_and_up(e, ep, blk):
                s, par = e * BL + blk, blk % 2
                if blk == 0:
                    pe.wait_ge(w_split, e + 1)
                at = slice(blk * BANK, blk * BANK + BANK)
                for w0, bank, free, ready in ((WG, k.bank[par], silu_done, g_ready),
                                              (WU, k.bank[2 + par], gu_done, u_ready)):
                    pe.wait_ge(free, s + 1)
                    for kk in range(K2):
                        w = slice(w0 + kk * P, w0 + kk * P + P)
                        ins = three_passes(pe, bank[:], wh[:, ep, w], wl[:, ep, w], k.hTh[:, kk, at], k.hTl[:, kk, at],
                                           kk == 0, kk == K2 - 1)
                    ins.then_inc(ready, 1)

            def down(e, ep, blk):
                s, par = e * BL + blk, blk % 2
                pe.wait_ge(hi_done, s + 1)
                pe.wait_ge(lo_done, s + 3)
                pe.wait_ge(acc_done, s + 1)
                for j in range(G):
                    out = k.bank[4 + par * 2 + j // 2][:, j % 2 * D:j % 2 * D + D]
                    t = slice(j * P, j * P + P)
                    ins = three_passes(pe, out, guh[:, par, t], gul[:, par, t], wh[:, ep, WD:WN], wl[:, ep, WD:WN],
                                       True, True)
                ins.then_inc(y_ready, 1)

            gate_and_up(0, 0, 0)

            def body(e, ep, last):
                for blk in range(BL):
                    if blk < BL - 1:
                        gate_and_up(e, ep, blk + 1)
                    elif not last:
                        gate_and_up(e + 1, 1 - ep, 0)
                    down(e, ep, blk)

            sweep(pe, body)


def store(k):
    nc = k.nc
    with ExitStack() as c:
        stored = c.enter_context(nc.semaphore("stored"))
        block = c.enter_context(nc.Block())

        @block.sync
        def _(sp):
            sp.dma_start(k.a["out"].rearrange("b p d -> p b d"), k.xs[:]).then_inc(stored, 16)
            sp.wait_ge(stored, 16)


def layouts(i):
    import numpy as np

    f = {n: np.asarray(v) for n, v in i.items()}
    B = f["x"].shape[0]
    col = lambda v, p: np.ascontiguousarray(v.reshape(-1, p).T)
    rows = lambda v: np.ascontiguousarray(np.broadcast_to(v, (P, v.size)))
    halves = lambda v: v.reshape(64, 2, 8).transpose(1, 0, 2).reshape(P, 8)
    chunks = lambda v: v.reshape(-1, P, v.shape[-1]).transpose(1, 0, 2)
    per_expert = lambda w: w.transpose(0, 2, 1).reshape(w.shape[0], K2, P, P).transpose(0, 2, 1, 3).reshape(-1, P, D)
    gate = np.concatenate([f["L1_ffn_w_gate"], f["L1_ffn_sh_gate"].reshape(2, P, D)])
    up = np.concatenate([f["L1_ffn_w_up"], f["L1_ffn_sh_up"].reshape(2, P, D)])
    down = np.concatenate([f["L1_ffn_w_down"].transpose(0, 2, 1), f["L1_ffn_sh_down"].T.reshape(2, P, D)])
    tri = np.tril(np.ones((8, 8), np.float32), -1).reshape(-1)
    eye64 = np.eye(64, dtype=np.float32)
    win = chunks(f["L0_ffn_Win"])
    return {
        "x": f["x"],
        "ctx": f["ctx_1024"].reshape(B // 2, 2, P, D),
        "ctxT": f["ctx_1024"].reshape(B // 2, 2, P, K2, P).transpose(0, 4, 3, 1, 2),
        "ident": np.eye(P, dtype=np.float32),
        "eye2": np.concatenate([eye64, eye64]),
        "head_rows": np.repeat(np.eye(4, dtype=np.float32), 32, axis=0) * np.float32(32 ** -0.5),
        "gates": rows(np.concatenate([f["g_xattn"], f["g_ffn"], f["L1_xattn_gate"]])),
        "w1c": halves(f["L0_ffn_W1"]), "b1c": halves(f["L0_ffn_b1"]), "w2c": halves(f["L0_ffn_W2"]),
        "w2row": f["L0_ffn_W2"], "b1row": f["L0_ffn_b1"], "b2c": f["L0_ffn_b2"].reshape(64, 1),
        "binc": np.tile(f["L0_ffn_bin_"], 2).reshape(P, 1),
        "win": np.concatenate([win, win], axis=2),
        "wout0": np.concatenate([f["L0_ffn_Wout"], f["L0_ffn_bout"].reshape(1, D)]),
        "attn_w": np.concatenate([chunks(f["L1_xattn_" + n]).reshape(P, -1) for n in ("w_kv", "w_q", "w_out")], axis=1),
        "gammaT": col(f["L1_xattn_ln_gamma"], P), "betaT": col(f["L1_xattn_ln_beta"], P),
        "b_out": rows(f["L1_xattn_b_out"]),
        "gate_wT": chunks(f["L1_ffn_gate_w"].T), "gate_bias": rows(f["L1_ffn_gate_bias"]), "earlier": rows(tri),
        "experts": np.concatenate([per_expert(gate), per_expert(up), down], axis=2),
    }


def kernel(**inputs):
    import numpy as np
    import concourse.bacc as bacc
    from concourse.bass_utils import run_bass_kernel_spmd

    nc = bacc.Bacc("TRN2", target_bir_lowering=False, num_devices=1)
    arrays, aps = {}, {}
    for name, v in layouts(inputs).items():
        v = np.ascontiguousarray(v)
        arrays["in_" + name] = v
        aps[name] = nc.dram_tensor("in_" + name, v.shape, mybir.dt.from_np(v.dtype), kind="ExternalInput").ap()
    aps["out"] = nc.dram_tensor("out_x", inputs["x"].shape, F32, kind="ExternalOutput").ap()
    build(nc, aps)
    return run_bass_kernel_spmd(nc, [arrays], core_ids=[0]).results[0]["out_x"]
```

```python
from contextlib import ExitStack

import concourse.bass as bass
from concourse import mybir

F32 = mybir.dt.float32
F32R = mybir.dt.float32r
ALU = mybir.AluOpType
ACT = mybir.ActivationFunctionType
X = mybir.AxisListType.X

P = 128
D = 256
K2 = D // P
BANK = 512
EPS = 1e-5
E, GR, TOPG, SHARED = 32, 8, 4, 2
EG = E // GR
ROUTED_SCALE = 2.5


class Chain:

    def __init__(self, eng, sem):
        self.eng, self.sem, self.base, self.n = eng, sem, 0, 0

    def step(self, ins):
        ins.then_inc(self.sem, 1)
        self.n += 1
        return ins

    def settle(self):
        self.eng.wait_ge(self.sem, self.base + self.n)

    def enter_loop(self, it, per):
        self.before, self.base, self.n = self.base + self.n, self.base + self.n + it * per, 0
        self.per = per

    def leave_loop(self, trips):
        assert self.n == self.per, (self.n, self.per)
        self.base, self.n = self.before + trips * self.per, 0


def build(nc, a):
    NB = a["x"].shape[0]
    NT = NB * P
    with ExitStack() as ctx:
        k = Kernel(nc, a, NB, ctx)
        with ExitStack() as inner:
            k.folding = Folding(k, lambda n: inner.enter_context(nc.semaphore(n)),
                                lambda n, s: inner.enter_context(nc.sbuf_tensor(n, s, F32)))
            attention0(k)
            k.awh = inner.enter_context(nc.sbuf_tensor("attn_w_high", [P, a["attn_w"].shape[1]], F32R))
            k.awl = inner.enter_context(nc.sbuf_tensor("attn_w_low", [P, a["attn_w"].shape[1]], F32R))
            relu_ffn(k)
            attention1(k)
        with ExitStack() as inner:
            k.hTh = inner.enter_context(nc.sbuf_tensor("hT_high", [P, K2, NT], F32R))
            k.hTl = inner.enter_context(nc.sbuf_tensor("hT_low", [P, K2, NT], F32R))
            k.sc = inner.enter_context(nc.sbuf_tensor("scores", [P, NB, E], F32))
            k.bias = inner.enter_context(nc.sbuf_tensor("gate_bias", [P, E], F32))
            k.earlier = inner.enter_context(nc.sbuf_tensor("earlier", [P, GR * GR], F32))
            router(k)
            experts(k)


class Kernel:
    def __init__(self, nc, a, NB, ctx):
        self.nc, self.a, self.NB = nc, a, NB

        def sb(name, shape, dt=F32):
            return ctx.enter_context(nc.sbuf_tensor(name, shape, dt))

        self.bank = [ctx.enter_context(nc.psum_tensor(f"bank{i}", [P, BANK], F32)) for i in range(8)]
        self.xs = sb("x_resident", [P, NB, D])
        self.ident = sb("identity", [P, P])
        self.gates = sb("gates_raw", [P, 5])
        self.tg = sb("gates_tanh", [P, 6])
        self.minus_half, self.eps, self.zero = sb("minus_half", [P, 1]), sb("eps", [P, 1]), sb("zero", [P, 1])
        self.diag = sb("w2_diagonals", [P, 8, 64])
        self.w1 = sb("w1_columns", [P, 8])
        self.negb1 = sb("minus_b1", [P, 8])
        self.bin = sb("bin_column", [P, 1])
        self.gbias = sb("g_bias", [64, 1])
        self.win = sb("win", [P, K2, P])
        self.wout0 = sb("wout_and_bout", [65, D])
        self.comb = sb("combine", [P, NB, SHARED + E])


TG_X0, TG_X1, TG_F0, TG_F1, TG_GATE, TG_X1GATE = range(6)


def rstd_steps(pool, k, n, mv, veps, rstd, stats_ready, veps_done, rstd_ready):
    pool.wait_ge(stats_ready, n + 1)
    pool.tensor_tensor(veps, mv[:, 1:2], k.eps[:], ALU.add).then_inc(veps_done, 1)
    pool.wait_ge(veps_done, n + 1)
    pool.tensor_tensor(rstd, veps, k.minus_half[:], ALU.pow).then_inc(rstd_ready, 1)


def three_passes(pe, out, ah, al, bh, bl, first, last):
    pe.matmul(out, ah, bh, start=first, stop=False)
    pe.matmul(out, al, bh, start=False, stop=False)
    return pe.matmul(out, ah, bl, start=False, stop=last)


class Folding:

    def __init__(self, k, sem, sb):
        self.k, self.loaded, self.done = k, sem("const_loaded"), sem("folded")
        self.eye2, self.w2, self.b1c = sb("eye2", [P, 64]), sb("w2c", [P, 8]), sb("b1c", [P, 8])
        self.w2row, self.b1row, self.prod = sb("w2row", [64, 16]), sb("b1row", [64, 16]), sb("prod", [64, 16])
        self.b2c, self.w2b1 = sb("b2c", [64, 1]), sb("w2b1", [64, 1])
        self.loads = [(self.eye2, "eye2"), (k.w1, "w1c"), (self.b1c, "b1c"), (self.w2, "w2c"),
                      (self.w2row, "w2row"), (self.b1row, "b1row"), (self.b2c, "b2c"), (k.bin, "binc"),
                      (k.win, "win"), (k.wout0, "wout0")]
        self.steps = 8 + 5

    def load(self, sp):
        for dst, name in self.loads:
            sp.dma_start(dst[:], self.k.a[name]).then_inc(self.loaded, 16)

    def fold(self, dve):
        k, chain = self.k, Chain(dve, self.done)
        dve.wait_ge(self.loaded, 16 * len(self.loads))
        for j in range(8):
            chain.step(dve.tensor_scalar(k.diag[:, j, :], self.eye2[:], self.w2[:, j:j + 1], None, ALU.mult))
        chain.step(dve.tensor_scalar(k.negb1[:], self.b1c[:], -1.0, None, ALU.mult))
        chain.step(dve.tensor_tensor(self.prod[:], self.w2row[:], self.b1row[:], ALU.mult))
        chain.settle()
        chain.step(dve.tensor_reduce(self.w2b1[:], self.prod[:], X, ALU.add))
        chain.settle()
        chain.step(dve.tensor_tensor(k.gbias[:], self.w2b1[:], self.b2c[:], ALU.add))
        chain.step(dve.tensor_tensor(k.tg[:, TG_X1GATE:TG_X1GATE + 1], k.tg[:, TG_X1:TG_X1 + 1],
                                     k.tg[:, TG_GATE:TG_GATE + 1], ALU.mult))
        chain.settle()
        assert chain.n == self.steps


def moments(dve, src, stats, mv, stats_ready):
    dve.bn_stats(stats, src)
    dve.drain()
    dve.bn_aggr(mv, stats).then_inc(stats_ready, 1)


def apply_norm(dve, src, dst, mv, rstd, rstd_ready, n):
    dve.wait_ge(rstd_ready, n + 1)
    return dve.tensor_scalar(dst, src, mv[:, 0:1], rstd, ALU.subtract, ALU.mult)


def attention0(k):
    nc, a, NB = k.nc, k.a, k.NB
    H, DH = 8, 32
    SCALE = DH ** -0.5
    U = 4
    trips = NB // U - 1
    with ExitStack() as c:
        sem = lambda n: c.enter_context(nc.semaphore("a0_" + n))
        sb = lambda n, s, dt=F32: c.enter_context(nc.sbuf_tensor("a0_" + n, s, dt))
        x_loaded, consts_loaded, tanh_done, consts_set = (sem("x_loaded"), sem("consts_loaded"), sem("tanh_done"),
                                                          sem("consts_set"))
        ctx_loaded = [sem(f"ctx_loaded{i}") for i in range(U)]
        stats_ready, veps_done, rstd_ready = sem("stats_ready"), sem("veps_done"), sem("rstd_ready")
        xn_ready, t_ready, q_copied = sem("xn_ready"), sem("t_ready"), sem("q_copied")
        s_ready, max_ready, exp_done = sem("s_ready"), sem("max_ready"), sem("exp_done")
        pt_ready, pt_copied = sem("pt_ready"), sem("pt_copied")
        ov_ready, ov_copied, added = sem("ov_ready"), sem("ov_copied"), sem("added")
        dve_chain = sem("dve_chain")
        ctxT = sb("ctxT", [P, U, K2, P])
        cv = sb("ctx", [P, U, D])
        xn = sb("xn", [P, 2, D])
        qT = sb("qT", [P, 2, K2, 4, P])
        head_rows = sb("head_rows", [P, 4])
        pr = sb("probs", [P, 2, H, P])
        pT = sb("probsT", [P, 2, H, P])
        stats, mv, veps, rstd = sb("stats", [P, 6]), sb("mv", [P, 2]), sb("veps", [P, 1]), sb("rstd", [P, 1])
        nmax, rsum = sb("minus_max", [P, 2, H]), sb("row_sum", [P, 2, H])
        rinv = sb("inverse_sum", [P, 2, H])
        upd = sb("update", [P, 2, D])
        consts = [(k.ident, "ident"), (head_rows, "head_rows"), (k.gates, "gates")]
        S, BT, BP0, BP1, BO = k.bank[0:4], k.bank[4], k.bank[5], k.bank[6], k.bank[7]
        block = c.enter_context(nc.Block())

        @block.sync
        def _(sp):
            def x_chunk(n):
                sp.dma_start(k.xs[:, bass.ds(n * U, U), :],
                             a["x"][bass.ds(n * U, U)].rearrange("b p d -> p b d")).then_inc(x_loaded, 16)

            def context(pair, half, slot):
                sp.dma_start(ctxT[:, slot], a["ctxT"][pair, :, :, half, :]).then_inc(ctx_loaded[slot], 16)
                sp.dma_start(cv[:, slot], a["ctx"][pair, half]).then_inc(ctx_loaded[slot], 16)

            x_chunk(0)
            for dst, name in consts:
                sp.dma_start(dst[:], a[name]).then_inc(consts_loaded, 16)
            for j in range(U):
                context(j // 2, j % 2, j)
            sp.wait_ge(x_loaded, 16)
            x_chunk(1)
            k.folding.load(sp)

            def body(it, more_x):
                if more_x:
                    sp.wait_ge(x_loaded, it * 16 + 32)
                    x_chunk(it + 2)
                for j in range(U):
                    sp.wait_ge(ov_ready, it * U + j + 1)
                    context(it * 2 + 2 + j // 2, j % 2, j)

            with sp.Fori(0, trips - 1) as it:
                body(it, True)
            body(trips - 1, False)

        @block.gpsimd
        def _(pool):
            def inverse_deviation(n):
                rstd_steps(pool, k, n, mv, veps[:], rstd[:], stats_ready, veps_done, rstd_ready)

            pool.memset(k.minus_half[:], -0.5).then_inc(consts_set, 1)
            pool.memset(k.eps[:], EPS).then_inc(consts_set, 1)
            pool.memset(k.zero[:], 0.0).then_inc(consts_set, 1)
            pool.wait_ge(consts_set, 3)
            pool.sem_inc(added, 1)
            for n in range(4):
                inverse_deviation(n)

            def body(it, last):
                for j in range(U):
                    b = it * U + j
                    if not last:
                        inverse_deviation(b + 4)
                    pool.wait_ge(ov_copied, b + 2)
                    xb = k.xs[:, b, :]
                    pool.tensor_tensor(xb, xb, upd[:, j % 2, :], ALU.add).then_inc(added, 1)

            with pool.Fori(0, trips) as it:
                body(it, False)
            body(trips, True)

        @block.vector
        def _(dve):
            chain = Chain(dve, dve_chain)

            def measure(b, x_count):
                dve.wait_ge(x_loaded, x_count)
                moments(dve, k.xs[:, b, :], stats[:], mv[:], stats_ready)

            def apply(b, par):
                apply_norm(dve, k.xs[:, b, :], xn[:, par, :], mv, rstd[:], rstd_ready, b).then_inc(xn_ready, 1)

            def norm(b, par, x_count):
                measure(b, x_count)
                apply(b, par)

            def queries(b, par):
                dve.wait_ge(t_ready, b + 1)
                for kk in range(K2):
                    ins = dve.tensor_tensor(qT[:, par, kk],
                                            BT[:, kk * P:kk * P + P].unsqueeze(1).broadcast_to([P, 4, P]),
                                            head_rows[:].unsqueeze(2).broadcast_to([P, 4, P]), ALU.mult)
                ins.then_inc(q_copied, 1)

            def maxima(b, par):
                for kk in range(K2):
                    dve.wait_ge(s_ready, b * K2 + kk + 1)
                    dve.tensor_reduce(nmax[:, par, kk * 4:kk * 4 + 4],
                                      S[par * 2 + kk][:].rearrange("p (j t) -> p j t", j=4),
                                      X, ALU.max, negate=True).then_inc(max_ready, 1)

            def inverse_sums(b, par):
                dve.wait_ge(exp_done, b + 1)
                chain.step(dve.reciprocal(rinv[:, par, :], rsum[:, par, :]))

            def output(b, par):
                chain.settle()
                dve.wait_ge(ov_ready, b + 1)
                dve.wait_ge(added, b + 1)
                dve.scalar_tensor_tensor(upd[:, par, :].rearrange("p (h e) -> p h e", h=H),
                                         BO[:, 0:D].rearrange("p (h e) -> p h e", h=H), k.tg[:, TG_X0:TG_X0 + 1],
                                         rinv[:, par, :].unsqueeze(2).broadcast_to([P, H, DH]),
                                         ALU.mult, ALU.mult).then_inc(ov_copied, 1)

            dve.sem_inc(ov_copied, 1)
            norm(0, 0, 16)
            norm(1, 1, 16)
            dve.wait_ge(consts_loaded, 16 * len(consts))
            queries(0, 0)
            norm(2, 0, 16)
            queries(1, 1)
            norm(3, 1, 16)
            maxima(0, 0)
            queries(2, 0)
            maxima(1, 1)
            dve.wait_ge(tanh_done, 1)

            def body(it, last):
                for j in range(U):
                    b, par = it * U + j, j % 2
                    if not last or j + 3 < U:
                        queries(b + 3, 1 - par)
                    if not last:
                        measure(b + 4, it * 16 + 32)
                    inverse_sums(b, par)
                    if not last or j + 2 < U:
                        maxima(b + 2, par)
                    if not last:
                        apply(b + 4, par)
                    output(b, par)

            with dve.Fori(0, trips) as it:
                chain.enter_loop(it, U)
                body(it, False)
            chain.leave_loop(trips)
            body(trips, True)

        @block.scalar
        def _(act):
            def exponentials(b, par, heads):
                act.wait_ge(max_ready, b * K2 + heads[0] // 4 + 1)
                for h in heads:
                    kk, j = divmod(h, 4)
                    ins = act.activation(pr[:, par, h, :], S[par * 2 + kk][:, j * P:j * P + P], ACT.Exp,
                                         bias=nmax[:, par, h:h + 1], accum_out=rsum[:, par, h:h + 1])
                return ins

            act.wait_ge(consts_loaded, 16 * len(consts))
            act.activation(k.tg[:, 0:5], k.gates[:], ACT.Tanh).then_inc(tanh_done, 1)
            exponentials(0, 0, range(4))
            exponentials(0, 0, range(4, H)).then_inc(exp_done, 1)

            def body(it, last):
                for j in range(U):
                    b, par = it * U + j, j % 2
                    if not last or j + 1 < U:
                        exponentials(b + 1, 1 - par, range(4))
                        exponentials(b + 1, 1 - par, range(4, H)).then_inc(exp_done, 1)
                    for n in range(2):
                        act.wait_ge(pt_ready, b * 2 + 1 + n)
                        act.activation(pT[:, par, 4 * n:4 * n + 4, :], (BP0, BP1)[n][:], ACT.Copy)\
                           .then_inc(pt_copied, 1)

            with act.Fori(0, trips) as it:
                body(it, False)
            body(trips, True)

        @block.tensor
        def _(pe):
            def transposed_queries(b, par):
                pe.wait_ge(xn_ready, b + 1)
                pe.wait_ge(q_copied, b)
                for kk in range(K2):
                    ins = pe.transpose(BT[:, kk * P:kk * P + P],
                                       xn[:, par, kk * P:kk * P + P], k.ident[:])
                ins.then_inc(t_ready, 1)

            def scores(b, par, slot, loads):
                pe.wait_ge(ctx_loaded[slot], loads)
                pe.wait_ge(q_copied, b + 1)
                for kk in range(K2):
                    for j in range(4):
                        ins = pe.matmul(S[par * 2 + kk][:, j * P:j * P + P], qT[:, par, kk, j, :],
                                        ctxT[:, slot, kk, :], start=True, stop=True)
                    ins.then_inc(s_ready, 1)

            pe.wait_ge(consts_loaded, 16 * len(consts))
            transposed_queries(0, 0)
            transposed_queries(1, 1)
            scores(0, 0, 0, 32)
            transposed_queries(2, 0)
            scores(1, 1, 1, 32)

            def body(it, last):
                for j in range(U):
                    b, par = it * U + j, j % 2
                    if not last or j + 3 < U:
                        transposed_queries(b + 3, 1 - par)
                    pe.wait_ge(exp_done, b + 1)
                    for h in range(H):
                        bank = (BP0, BP1)[h // 4]
                        ins = pe.transpose(bank[:, h % 4 * P:h % 4 * P + P], pr[:, par, h, :], k.ident[:])
                        if h % 4 == 3:
                            ins.then_inc(pt_ready, 1)
                    if not last or j + 2 < U:
                        scores(b + 2, par, (j + 2) % U, (it + (j + 2) // U) * 32 + 32)
                    pe.wait_ge(pt_copied, b * 2 + 2)
                    pe.wait_ge(ov_copied, b + 1)
                    for h in range(H):
                        ins = pe.matmul(BO[:, h * DH:h * DH + DH],
                                        pT[:, par, h, :], cv[:, j, h * DH:h * DH + DH], start=True, stop=True)
                    ins.then_inc(ov_ready, 1)

            with pe.Fori(0, trips) as it:
                body(it, False)
            body(trips, True)


def relu_ffn(k):
    nc, NB = k.nc, k.NB
    G = BANK // P
    NBLK, M = NB // G, 64
    LOOPED = NBLK - 3
    with ExitStack() as c:
        sem = lambda n: c.enter_context(nc.semaphore("f0_" + n))
        sb = lambda n, s: c.enter_context(nc.sbuf_tensor("f0_" + n, s, F32))
        stats_ready, veps_done, rstd_ready = sem("stats_ready"), sem("veps_done"), sem("rstd_ready")
        xn_ready, xt_ready, xt_copied = sem("xn_ready"), sem("xt_ready"), sem("xt_copied")
        s_ready, s_copied, h_ready, g_step = sem("s_ready"), sem("s_copied"), sem("h_ready"), sem("g_step")
        g_copied, o_ready, o_added = sem("g_copied"), sem("o_ready"), sem("o_added")
        ones_set = sem("ones_set")
        xn, xT = sb("xn", [P, G, D]), sb("xT", [P, K2, BANK])
        s, h = sb("s", [P, BANK]), sb("h", [P, 8, BANK])
        gT = sb("gT", [M + 1, BANK])
        stats, mv = sb("stats", [P, G, 6]), sb("mv", [P, G, 2])
        veps, rstd = sb("veps", [P, G]), sb("rstd", [P, G])
        half = sb("half", [P, G])
        half_set = sem("half_set")
        w_loaded, w_high, w_split = [sem("w_loaded0"), sem("w_loaded1")], sem("w_high"), sem("w_split")
        WCH = k.a["attn_w"].shape[1] // NBLK
        raw = sb("w_raw", [P, 2, WCH])
        BX, BS, BG, BOUT = k.bank[0:2], k.bank[2], k.bank[3], k.bank[4:6]
        block = c.enter_context(nc.Block())

        def steps(eng, body):
            with eng.Fori(0, LOOPED) as t:
                body(t, 0)
            for t in range(LOOPED, NBLK):
                body(t, t - LOOPED + 1)

        @block.gpsimd
        def _(pool):
            pool.memset(gT[M:M + 1, :], 1.0).then_inc(ones_set, 1)
            pool.wait_ge(ones_set, 1)
            pool.memset(half[:], -0.5).then_inc(half_set, 1)
            pool.wait_ge(half_set, 1)

            def split(t, par, loads):
                at = bass.ds(t * WCH, WCH)
                pool.wait_ge(w_loaded[par], loads * 16)
                pool.tensor_copy(k.awh[:, at], raw[:, par, :]).then_inc(w_high, 1)
                pool.wait_ge(w_high, t + 1)
                pool.tensor_tensor(k.awl[:, at], raw[:, par, :], k.awh[:, at].bitcast(F32),
                                   ALU.subtract).then_inc(w_split, 1)

            def inverse_deviations(t):
                pool.wait_ge(stats_ready, t + 1)
                pool.tensor_tensor(veps[:], mv[:, :, 1], k.eps[:].broadcast_to([P, G]), ALU.add).then_inc(veps_done, 1)
                pool.wait_ge(veps_done, t + 1)
                pool.tensor_tensor(rstd[:], veps[:], half[:], ALU.pow).then_inc(rstd_ready, 1)

            with pool.Fori(0, NBLK // 2) as it:
                for par in range(2):
                    inverse_deviations(it * 2 + par)
                    split(it * 2 + par, par, it + 1)

        @block.sync
        def _(sp):
            def load(t, par):
                sp.dma_start(raw[:, par, :], k.a["attn_w"][:, bass.ds(t * WCH, WCH)]).then_inc(w_loaded[par], 16)

            load(0, 0)
            load(1, 1)
            with sp.Fori(0, NBLK // 2 - 1) as it:
                for par in range(2):
                    sp.wait_ge(w_split, it * 2 + par + 1)
                    load(it * 2 + par + 2, par)

        @block.vector
        def _(dve):
            def norm(t):
                for j in range(G):
                    dve.bn_stats(stats[:, j, :], k.xs[:, t * G + j, :])
                dve.drain()
                for j in range(G):
                    ins = dve.bn_aggr(mv[:, j, :], stats[:, j, :])
                ins.then_inc(stats_ready, 1)
                dve.wait_ge(rstd_ready, t + 1)
                for j in range(G):
                    ins = dve.tensor_scalar(xn[:, j, :], k.xs[:, t * G + j, :], mv[:, j, 0:1], rstd[:, j:j + 1],
                                            ALU.subtract, ALU.mult)
                ins.then_inc(xn_ready, 1)

            def hidden(t, used):
                dve.wait_ge(s_ready, t + 1)
                dve.wait_ge(h_ready, t * 8)
                dve.tensor_scalar(s[:], BS[:], k.bin[:], None, ALU.add).then_inc(s_copied, 1)
                dve.wait_ge(s_copied, t + 1)
                for j in range(8):
                    if used is not None:
                        dve.wait_ge(g_step, used + j + 1)
                    dve.tensor_scalar(h[:, j, :], s[:], k.w1[:, j:j + 1], k.negb1[:, j:j + 1],
                                      ALU.mult, ALU.max).then_inc(h_ready, 1)

            dve.sem_inc(o_added, 1)
            norm(0)
            k.folding.fold(dve)
            dve.wait_ge(xt_ready, 1)
            norm(1)
            hidden(0, None)
            dve.wait_ge(xt_ready, 2)
            norm(2)

            def body(t, tail):
                if tail < 3:
                    hidden(t + 1, t * 8)
                if tail < 1:
                    dve.wait_ge(xt_ready, t + 3)
                    norm(t + 3)
                dve.wait_ge(o_ready, t + 1)
                for j in range(G):
                    xb = k.xs[:, t * G + j, :]
                    ins = dve.scalar_tensor_tensor(xb, BOUT[j // 2][:, j % 2 * D:j % 2 * D + D],
                                                   k.tg[:, TG_F0:TG_F0 + 1], xb, ALU.mult, ALU.add)
                ins.then_inc(o_added, 1)

            steps(dve, body)

        @block.scalar
        def _(act):
            def xt_copy(t):
                act.wait_ge(xt_ready, t + 1)
                for kk in range(K2):
                    ins = act.activation(xT[:, kk, :], BX[kk][:], ACT.Copy)
                ins.then_inc(xt_copied, 1)

            xt_copy(0)
            xt_copy(1)

            def body(t, tail):
                act.wait_ge(g_step, t * 8 + 8)
                act.activation(gT[0:M, :], BG[0:M, :], ACT.Identity, bias=k.gbias[:]).then_inc(g_copied, 1)
                if tail < 2:
                    xt_copy(t + 2)

            steps(act, body)

        @block.tensor
        def _(pe):
            def transposes(t):
                pe.wait_ge(xn_ready, t + 1)
                for kk in range(K2):
                    for j in range(G):
                        ins = pe.transpose(BX[kk][:, j * P:j * P + P], xn[:, j, kk * P:kk * P + P], k.ident[:])
                ins.then_inc(xt_ready, 1)

            def first_product(t):
                pe.wait_ge(xt_copied, t + 1)
                pe.wait_ge(s_copied, t)
                for kk in range(K2):
                    ins = pe.matmul(BS[:], k.win[:, kk, :], xT[:, kk, :], start=kk == 0, stop=kk == K2 - 1)
                ins.then_inc(s_ready, 1)

            transposes(0)
            first_product(0)
            transposes(1)
            pe.wait_ge(ones_set, 1)
            pe.wait_ge(k.folding.done, k.folding.steps)

            def body(t, tail):
                if tail < 3:
                    first_product(t + 1)
                for j in range(8):
                    pe.wait_ge(h_ready, t * 8 + j + 1)
                    pe.matmul(BG[0:M, :], k.diag[:, j, :], h[:, j, :], start=j == 0, stop=j == 7).then_inc(g_step, 1)
                if tail < 2:
                    transposes(t + 2)
                pe.wait_ge(g_copied, t + 1)
                pe.wait_ge(o_added, t + 1)
                for j in range(G):
                    ins = pe.matmul(BOUT[j // 2][:, j % 2 * D:j % 2 * D + D], gT[:, j * P:j * P + P], k.wout0[:],
                                    start=True, stop=True)
                ins.then_inc(o_ready, 1)

            steps(pe, body)


def attention1(k):
    nc, a, NB = k.nc, k.a, k.NB
    H, DH = 16, 64
    SCALE = DH ** -0.5
    NP = NB // 2
    trips = NP // 2 - 1
    INNER = H * DH
    KC = INNER // P
    FILL = ["XT", "K0", "K1", "Q0", "Q1", "K2", "K3", "Q2", "Q3", "V0", "V1", "V2", "V3"]
    NF = len(FILL)
    PER6, PER7 = (NF + 1) // 2, NF // 2
    fills = lambda uu: range(3 * uu, 3 * uu + 3 + uu // 3)
    with ExitStack() as c:
        sem = lambda n: c.enter_context(nc.semaphore("a1_" + n))
        sb = lambda n, s, dt=F32: c.enter_context(nc.sbuf_tensor("a1_" + n, s, dt))
        w_loaded, boadd_ready = sem("w_loaded"), sem("boadd_ready")
        ctx_loaded = [sem("ctx_loaded0"), sem("ctx_loaded1")]
        stats_ready, veps_done, rstd_ready = sem("stats_ready"), sem("veps_done"), sem("rstd_ready")
        xn_ready, proj_ready = sem("xn_ready"), sem("proj_ready")
        copied = [sem("copied6"), sem("copied7")]
        s_ready, max_ready, exp_done = sem("s_ready"), sem("max_ready"), sem("exp_done")
        pt_ready, pt0_copied, pt1_copied = sem("pt_ready"), sem("pt0_copied"), sem("pt1_copied")
        scaled, ov_ready, ot_copied = sem("scaled"), sem("ov_ready"), sem("ot_copied")
        w_ready, w_copied, biased, dve_chain = sem("w_ready"), sem("w_copied"), sem("biased"), sem("dve_chain")
        at_q, at_out = K2 * 2 * INNER, K2 * 3 * INNER
        wkv, wq, wout = ([w[:, lo:hi].rearrange("p (k n) -> p k n", k=kc) for w in (k.awh, k.awl)]
                         for lo, hi, kc in ((0, at_q, K2), (at_q, at_out, K2), (at_out, at_out + KC * D, KC)))
        gam, bet, bo = sb("gammaT", [P, K2]), sb("betaT", [P, K2]), sb("b_out", [P, D])
        raw = sb("ctxT", [P, 2, K2, 2, P])
        ctxT = [sb(n, [P, 2, K2, 2, P], F32R) for n in ("ctxT_high", "ctxT_low")]
        x1, xn, xTf = sb("x1", [P, D]), sb("xn", [P, 2, D]), sb("xT", [P, K2, 2 * P])
        xT = [sb(n, [P, K2, 2 * P], F32R) for n in ("xT_high", "xT_low")]
        qT, kT = sb("qT", [P, 2, KC, 2 * P]), sb("kT", [P, 2, KC, 2 * P])
        v = sb("v", [P, 2, 2, INNER])
        pr, pT = sb("probs", [P, 2, 8, P]), sb("probsT", [P, 2, 8, P])
        oT = [sb(n, [P, KC, P], F32R) for n in ("oT_high", "oT_low")]
        ctx_high, ctx_split, xt_written, xt_high, xt_split, ot_high = (
            sem("ctx_high"), sem("ctx_split"), sem("xt_written"), sem("xt_high"), sem("xt_split"), sem("ot_high"))
        stats, mv, veps, rstd = sb("stats", [P, 6]), sb("mv", [P, 2]), sb("veps", [P, 1]), sb("rstd", [P, 1])
        nmax, rsum, rinv = sb("minus_max", [P, 2, 4, 2]), sb("row_sum", [P, 2, 8]), sb("inverse_sum", [P, 2, 8])
        block = c.enter_context(nc.Block())
        weights = [(gam, "gammaT"), (bet, "betaT"), (bo, "b_out")]

        def pairs(eng, body, enter=None, leave=None):
            with eng.Fori(0, trips) as it:
                if enter:
                    enter(it)
                for half in range(2):
                    body(it * 2 + half, it, half, 2)
            if leave:
                leave()
            for half in range(2):
                body(2 * trips + half, trips, half, 1 - half)

        @block.sync
        def _(sp):
            def context(p, half):
                sp.dma_start(raw[:, half], a["ctxT"][p]).then_inc(ctx_loaded[half], 16)

            context(0, 0)
            for dst, name in weights:
                sp.dma_start(dst[:], a[name]).then_inc(w_loaded, 16)
            context(1, 1)
            with sp.Fori(0, trips) as it:
                for half in range(2):
                    sp.wait_ge(ctx_split, it * 2 + half + 1)
                    context(it * 2 + half + 2, half)

        @block.gpsimd
        def _(pool):
            def inverse_deviation(n):
                rstd_steps(pool, k, n, mv, veps[:], rstd[:], stats_ready, veps_done, rstd_ready)

            zeros = k.zero[:].unsqueeze(2).unsqueeze(3).broadcast_to([P, K2, 2, P])

            def split_context(q, half, loads):
                pool.wait_ge(ctx_loaded[half], loads * 16)
                pool.tensor_tensor(ctxT[0][:, half], raw[:, half], zeros, ALU.add).then_inc(ctx_high, 1)
                pool.wait_ge(ctx_high, q + 1)
                pool.tensor_tensor(ctxT[1][:, half], raw[:, half], ctxT[0][:, half].bitcast(F32),
                                   ALU.subtract).then_inc(ctx_split, 1)

            def low_input(q):
                pool.wait_ge(xt_high, q + 1)
                pool.tensor_tensor(xT[1][:], xTf[:], xT[0][:].bitcast(F32), ALU.subtract).then_inc(xt_split, 1)

            for n in range(4):
                inverse_deviation(n)
            split_context(0, 0, 1)
            low_input(0)
            for n in range(4, 8):
                inverse_deviation(n)
            pool.wait_ge(w_loaded, 16 * len(weights))
            pool.tensor_tensor(bo[:], bo[:], k.tg[:, TG_X1GATE:TG_X1GATE + 1].broadcast_to([P, D]),
                               ALU.mult).then_inc(boadd_ready, 1)
            pool.wait_ge(boadd_ready, 1)
            split_context(1, 1, 1)

            def body(p, it, half, ahead):
                if ahead >= 2:
                    inverse_deviation(p * 4 + 8)
                if ahead >= 1:
                    low_input(p + 1)
                if ahead >= 2:
                    for n in range(1, 4):
                        inverse_deviation(p * 4 + 8 + n)
                    pool.wait_ge(proj_ready, (p + 1) * NF)
                    split_context(p + 2, half, it + 2)
                for j in range(2):
                    b = p * 2 + j
                    pool.wait_ge(w_copied, b + 2)
                    xb = k.xs[:, b, :]
                    pool.tensor_tensor(xb, xb, bo[:], ALU.add).then_inc(biased, 1)

            pairs(pool, body)

        def copy_projection(eng, is_act, half, i):
            bank = k.bank[6 + i % 2]
            kind, n = FILL[i][:-1], FILL[i][-1]
            if kind in "KQ":
                n = int(n)
                dst = (kT if kind == "K" else qT)[:, half, 2 * n:2 * n + 2, :]
                scale = SCALE if kind == "Q" else 1.0
                src = bank[:].rearrange("p (c t) -> p c t", c=2)
            else:
                n = int(n)
                dst, src, scale = v[:, half, n // 2, n % 2 * BANK:n % 2 * BANK + BANK], bank[:], 1.0
            if is_act:
                ins = eng.activation(dst, src, ACT.Copy, scale=scale)
            elif scale != 1.0:
                ins = eng.tensor_scalar(dst, src, scale, None, ALU.mult)
            else:
                ins = eng.tensor_copy(dst, src)
            ins.then_inc(copied[i % 2], 1)

        @block.vector
        def _(dve):
            chain = Chain(dve, dve_chain)

            def measure_x(b):
                moments(dve, k.xs[:, b, :], stats[:], mv[:], stats_ready)

            def measure_normed(b):
                chain.step(apply_norm(dve, k.xs[:, b, :], x1[:], mv, rstd[:], rstd_ready, b * 2))
                chain.settle()
                moments(dve, x1[:], stats[:], mv[:], stats_ready)

            def normed_input(b, par):
                apply_norm(dve, x1[:], xn[:, par, :], mv, rstd[:], rstd_ready, b * 2 + 1).then_inc(xn_ready, 1)

            def norm(b, par):
                measure_x(b)
                measure_normed(b)
                normed_input(b, par)

            def proj(q, half, i):
                if i % 2 == 1:
                    dve.wait_ge(proj_ready, q * NF + i + 1)
                    copy_projection(dve, False, half, i)

            def maxima(u, par):
                dve.wait_ge(s_ready, u + 1)
                for e in range(2):
                    ins = dve.tensor_reduce(nmax[:, par, :, e],
                                            k.bank[2 * par + e][:].rearrange("p (m t) -> p m t", m=4),
                                            X, ALU.max, negate=True)
                ins.then_inc(max_ready, 1)

            def normalised(u, par):
                dve.wait_ge(exp_done, u + 1)
                chain.step(dve.reciprocal(rinv[:, par, :], rsum[:, par, :]))
                chain.settle()
                dve.tensor_tensor(pr[:, par], pr[:, par], rinv[:, par, :].unsqueeze(2).broadcast_to([P, 8, P]),
                                  ALU.mult).then_inc(scaled, 1)

            dve.sem_inc(ot_copied, 1)
            dve.sem_inc(w_copied, 1)
            norm(0, 0)
            norm(1, 1)
            for i in range(NF):
                proj(0, 0, i)
                if i == 3:
                    dve.wait_ge(proj_ready, 1)
                    norm(2, 0)
                    norm(3, 1)
            maxima(0, 0)
            maxima(1, 1)
            normalised(0, 0)

            def body(p, it, half, ahead):
                for uu in range(4):
                    u, par = p * 4 + uu, uu % 2
                    normed = p * 2 + 4 + uu // 2 if ahead >= 2 and uu % 2 == 0 else None
                    dve.wait_ge(pt_ready, u * 2 + 1)
                    dve.tensor_copy(pT[:, par, 0:4, :], k.bank[4][:]).then_inc(pt0_copied, 1)
                    if normed is not None:
                        measure_x(normed)
                    if ahead >= 1 or uu < 2:
                        maxima(u + 2, par)
                    if uu == 2:
                        residual(p * 2)
                    if ahead >= 2 and uu % 2 == 1:
                        if uu == 1:
                            dve.wait_ge(proj_ready, (p + 1) * NF + 1)
                        normed_input(p * 2 + 4 + uu // 2, uu // 2)
                    low_output(u, uu)
                    if ahead >= 1:
                        proj(p + 1, 1 - half, fills(uu)[0])
                    if ahead >= 1 or uu < 3:
                        normalised(u + 1, 1 - par)
                    if ahead >= 1:
                        for i in fills(uu)[1:]:
                            proj(p + 1, 1 - half, i)
                    if normed is not None:
                        measure_normed(normed)
                residual(p * 2 + 1)

            def low_output(u, uu):
                at = slice(uu % 2 * 4, uu % 2 * 4 + 4)
                dve.wait_ge(ot_high, u + 1)
                dve.tensor_tensor(oT[1][:, at, :], k.bank[4][:].rearrange("p (c t) -> p c t", c=4),
                                  oT[0][:, at, :].bitcast(F32), ALU.subtract).then_inc(ot_copied, 1)

            def residual(b):
                dve.wait_ge(w_ready, b + 1)
                xb = k.xs[:, b, :]
                dve.scalar_tensor_tensor(xb, k.bank[5][:, 0:D], k.tg[:, TG_X1GATE:TG_X1GATE + 1], xb,
                                         ALU.mult, ALU.add).then_inc(w_copied, 1)

            pairs(dve, body, lambda it: chain.enter_loop(it, 2 * (4 + 2)), lambda: chain.leave_loop(trips))

        @block.scalar
        def _(act):
            act.wait_ge(w_loaded, 16 * len(weights))

            def proj(q, half, i):
                if i % 2 == 0:
                    act.wait_ge(proj_ready, q * NF + i + 1)
                    if i == 0:
                        for kk in range(K2):
                            ins = act.activation(xTf[:, kk, :], k.bank[6][:, kk * 2 * P:(kk + 1) * 2 * P], ACT.Identity,
                                                 bias=bet[:, kk:kk + 1], scale=gam[:, kk:kk + 1])
                        ins.then_inc(copied[0], 1)
                        act.wait_ge(copied[0], q * PER6 + 1)
                        act.activation(xT[0][:], xTf[:], ACT.Copy).then_inc(xt_high, 1)
                    else:
                        copy_projection(act, True, half, i)

            def exponentials(par, hs):
                for hh in hs:
                    m, e = divmod(hh, 2)
                    ins = act.activation(pr[:, par, hh, :], k.bank[2 * par + e][:, m * P:m * P + P], ACT.Exp,
                                         bias=nmax[:, par, m, e:e + 1], accum_out=rsum[:, par, hh:hh + 1])
                return ins

            for i in range(NF):
                proj(0, 0, i)
            act.wait_ge(max_ready, 1)
            exponentials(0, range(8)).then_inc(exp_done, 1)

            def body(p, it, half, ahead):
                for uu in range(4):
                    u, par, octet = p * 4 + uu, uu % 2, uu % 2
                    act.wait_ge(pt_ready, u * 2 + 2)
                    act.activation(pT[:, par, 4:8, :], k.bank[5][:], ACT.Copy).then_inc(pt1_copied, 1)
                    if ahead >= 1 or uu < 3:
                        act.wait_ge(max_ready, u + 2)
                        exponentials(1 - par, range(8)).then_inc(exp_done, 1)
                    act.wait_ge(ov_ready, u + 1)
                    act.activation(oT[0][:, octet * 4:octet * 4 + 4, :], k.bank[4][:], ACT.Copy)\
                       .then_inc(ot_high, 1)
                    if ahead >= 1:
                        for i in fills(uu):
                            proj(p + 1, 1 - half, i)

            pairs(act, body)

        @block.tensor
        def _(pe):
            def proj(q, it, half, i):
                bank = k.bank[6 + i % 2]
                pe.wait_ge(copied[i % 2], q * (PER6, PER7)[i % 2] + i // 2)
                if i == 0:
                    pe.wait_ge(xn_ready, q * 2 + 2)
                    for kk in range(K2):
                        for j in range(2):
                            ins = pe.transpose(bank[:, kk * 2 * P + j * P:kk * 2 * P + j * P + P],
                                               xn[:, j, kk * P:kk * P + P], k.ident[:])
                    ins.then_inc(proj_ready, 1)
                    return
                kind, n = FILL[i][:-1], int(FILL[i][-1])
                if i == 1:
                    pe.wait_ge(ctx_split, q + 1)
                if kind == "Q" and n == 0:
                    pe.wait_ge(xt_split, q + 1)
                if kind == "K":
                    moving = [x[:, half].rearrange("p k b t -> p k (b t)") for x in ctxT]
                else:
                    moving = xT
                if kind in "KQ":
                    w = wkv if kind == "K" else wq
                    for j in range(2):
                        cols = slice((2 * n + j) * P, (2 * n + j + 1) * P)
                        for kk in range(K2):
                            ins = three_passes(pe, bank[:, j * 2 * P:(j + 1) * 2 * P], w[0][:, kk, cols],
                                               w[1][:, kk, cols], moving[0][:, kk, :], moving[1][:, kk, :],
                                               kk == 0, kk == K2 - 1)
                else:
                    cols = slice(INNER + n % 2 * BANK, INNER + (n % 2 + 1) * BANK)
                    for kk in range(K2):
                        ins = three_passes(pe, bank[:], ctxT[0][:, half, kk, n // 2, :],
                                           ctxT[1][:, half, kk, n // 2, :], wkv[0][:, kk, cols],
                                           wkv[1][:, kk, cols], kk == 0, kk == K2 - 1)
                ins.then_inc(proj_ready, 1)

            def scores(half, uu):
                b, octet = uu // 2, uu % 2
                for m in range(4):
                    for e in range(2):
                        r = slice(DH * e, DH * e + DH)
                        ins = pe.matmul(k.bank[2 * (uu % 2) + e][:, m * P:m * P + P],
                                        qT[r, half, octet * 4 + m, b * P:b * P + P],
                                        kT[r, half, octet * 4 + m, b * P:b * P + P], start=True, stop=True)
                ins.then_inc(s_ready, 1)

            def await_projected(q, name):
                upto = FILL.index(name) + 1
                pe.wait_ge(copied[0], q * PER6 + (upto + 1) // 2)
                pe.wait_ge(copied[1], q * PER7 + upto // 2)

            def projected(b):
                for cc in range(KC):
                    ins = three_passes(pe, k.bank[5][:, 0:D], oT[0][:, cc, :], oT[1][:, cc, :],
                                       wout[0][:, cc, :], wout[1][:, cc, :], cc == 0, cc == KC - 1)
                ins.then_inc(w_ready, 1)

            pe.wait_ge(w_loaded, 16 * len(weights))
            for i in range(NF):
                proj(0, 0, 0, i)
            await_projected(0, "Q3")
            scores(0, 0)
            scores(0, 1)

            def body(p, it, half, ahead):
                nxt = (p + 1, it + half, 1 - half)
                for uu in range(4):
                    u, par = p * 4 + uu, uu % 2
                    b, octet = uu // 2, uu % 2
                    pe.wait_ge(scaled, u + 1)
                    pe.wait_ge(ot_copied, u + 1)
                    for hh in range(8):
                        if hh == 4 and uu in (0, 3):
                            pe.wait_ge(w_copied, p * 2 + 1 + b)
                        ins = pe.transpose(k.bank[4 + hh // 4][:, hh % 4 * P:hh % 4 * P + P],
                                           pr[:, par, hh, :], k.ident[:])
                        if hh % 4 == 3:
                            ins.then_inc(pt_ready, 1)
                    if uu < 2:
                        scores(half, uu + 2)
                    elif ahead >= 1:
                        await_projected(p + 1, "Q1" if uu == 2 else "Q3")
                        scores(1 - half, uu - 2)
                    pe.wait_ge(pt0_copied, u + 1)
                    pe.wait_ge(pt1_copied, u + 1)
                    if uu == 2:
                        projected(p * 2)
                    if uu == 0:
                        await_projected(p, "V3")
                    for hh in range(8):
                        m, e = divmod(hh, 2)
                        g = octet * 8 + hh
                        ins = pe.matmul(k.bank[4][e * DH:(e + 1) * DH, m * P:(m + 1) * P],
                                        v[:, half, b, g * DH:g * DH + DH], pT[:, par, hh, :], start=True, stop=True)
                    ins.then_inc(ov_ready, 1)
                    if uu == 3:
                        if ahead >= 1:
                            for i in fills(uu)[:-1]:
                                proj(*nxt, i)
                        pe.wait_ge(ot_copied, p * 4 + 5)
                        projected(p * 2 + 1)
                        if ahead >= 1:
                            proj(*nxt, fills(uu)[-1])
                    elif ahead >= 1:
                        for i in fills(uu):
                            proj(*nxt, i)
            pairs(pe, body)


def router(k):
    nc, a, NB = k.nc, k.a, k.NB
    G = BANK // P
    NBLK = NB // G
    trips = NBLK // 2 - 1
    with ExitStack() as c:
        sem = lambda n: c.enter_context(nc.semaphore("r_" + n))
        sb = lambda n, s: c.enter_context(nc.sbuf_tensor("r_" + n, s, F32))
        loaded, xn_ready, t_ready, minus_set = sem("loaded"), sem("xn_ready"), sem("t_ready"), sem("minus_set")
        hf_copied, hi_copied, lo_done, l_ready, l_copied = (sem("hf_copied"), sem("hi_copied"), sem("lo_done"),
                                                                sem("l_ready"), sem("l_copied"))
        stats_ready, veps_done, rstd_ready = sem("stats_ready"), sem("veps_done"), sem("rstd_ready")
        sig_done, shared_set = sem("sig_done"), sem("shared_set")
        gw = sb("gate_wT", [P, K2, E])
        xn, hf = sb("xn", [P, 2, G, D]), sb("hT", [P, 2, K2, BANK])
        lg = sb("logits", [P, NB, E])
        stats, mv = sb("stats", [P, G, 6]), sb("mv", [P, G, 2])
        veps, rstd, minus = sb("veps", [P, G]), sb("rstd", [P, G]), sb("minus_halves", [P, G])
        loads = [(gw, "gate_wT"), (k.bias, "gate_bias"), (k.earlier, "earlier")]

        def sweep(eng, body):
            with eng.Fori(0, trips) as it:
                for par in range(2):
                    body(it * 2 + par, par, True)
            for par in range(2):
                body(trips * 2 + par, par, False)

        with nc.Block() as block:
            @block.sync
            def _(sp):
                for dst, name in loads:
                    sp.dma_start(dst[:], a[name]).then_inc(loaded, 16)

            @block.vector
            def _(dve):
                def norm(t, par):
                    for j in range(G):
                        dve.bn_stats(stats[:, j, :], k.xs[:, t * G + j, :])
                    dve.drain()
                    for j in range(G):
                        ins = dve.bn_aggr(mv[:, j, :], stats[:, j, :])
                    ins.then_inc(stats_ready, 1)
                    dve.wait_ge(rstd_ready, t + 1)
                    for j in range(G):
                        ins = dve.tensor_scalar(xn[:, par, j, :], k.xs[:, t * G + j, :], mv[:, j, 0:1],
                                                rstd[:, j:j + 1], ALU.subtract, ALU.mult)
                    ins.then_inc(xn_ready, 1)

                def low(t, par):
                    dve.wait_ge(hi_copied, t + 1)
                    at = bass.ds(t * BANK, BANK)
                    dve.tensor_tensor(k.hTl[:, :, at], hf[:, par], k.hTh[:, :, at].bitcast(F32), ALU.subtract)\
                        .then_inc(lo_done, 1)

                def take_logits(t, par):
                    dve.wait_ge(l_ready, t + 1)
                    dve.tensor_copy(lg[:, bass.ds(t * G, G), :],
                                    k.bank[4 + par][:, 0:G * E].rearrange("p (g e) -> p g e", e=E)).then_inc(l_copied, 1)

                dve.sem_inc(l_copied, 2)
                dve.sem_inc(lo_done, 2)
                dve.tensor_copy(k.comb[:, :, 0:SHARED],
                                k.tg[:, TG_F1:TG_F1 + 1].unsqueeze(1).broadcast_to([P, NB, SHARED])).then_inc(shared_set, 1)
                norm(0, 0)
                norm(1, 1)

                def body(t, par, ahead):
                    low(t, par)
                    if ahead:
                        norm(t + 2, par)
                    take_logits(t, par)

                sweep(dve, body)

            @block.gpsimd
            def _(pool):
                pool.memset(minus[:], -0.5).then_inc(minus_set, 1)
                pool.wait_ge(minus_set, 1)
                with pool.Fori(0, NBLK) as t:
                    pool.wait_ge(stats_ready, t + 1)
                    pool.tensor_tensor(veps[:], mv[:, :, 1], k.eps[:].broadcast_to([P, G]), ALU.add)\
                        .then_inc(veps_done, 1)
                    pool.wait_ge(veps_done, t + 1)
                    pool.tensor_tensor(rstd[:], veps[:], minus[:], ALU.pow).then_inc(rstd_ready, 1)

            @block.scalar
            def _(act):
                def high(t, par):
                    act.wait_ge(t_ready, t + 1)
                    act.wait_ge(lo_done, t + 1)
                    for kk in range(K2):
                        ins = act.activation(hf[:, par, kk, :], k.bank[par * 2 + kk][:], ACT.Copy)
                    ins.then_inc(hf_copied, 1)
                    act.wait_ge(hf_copied, t + 1)
                    act.activation(k.hTh[:, :, bass.ds(t * BANK, BANK)], hf[:, par], ACT.Copy).then_inc(hi_copied, 1)

                with act.Fori(0, NBLK // 2) as it:
                    for par in range(2):
                        high(it * 2 + par, par)
                act.wait_ge(l_copied, NBLK + 2)
                act.activation(k.sc[:], lg[:], ACT.Sigmoid).then_inc(sig_done, 1)

            @block.tensor
            def _(pe):
                def transposed(t, par):
                    pe.wait_ge(xn_ready, t + 1)
                    for kk in range(K2):
                        for j in range(G):
                            ins = pe.transpose(k.bank[par * 2 + kk][:, j * P:j * P + P],
                                               xn[:, par, j, kk * P:kk * P + P], k.ident[:])
                    ins.then_inc(t_ready, 1)

                def logits(t, par):
                    pe.wait_ge(hf_copied, t + 1)
                    pe.wait_ge(l_copied, t + 1)
                    for j in range(G):
                        for kk in range(K2):
                            ins = pe.matmul(k.bank[4 + par][:, j * E:j * E + E], hf[:, par, kk, j * P:j * P + P],
                                            gw[:, kk, :], start=kk == 0, stop=kk == K2 - 1)
                    ins.then_inc(l_ready, 1)

                pe.wait_ge(loaded, 16 * len(loads))
                transposed(0, 0)
                transposed(1, 1)

                def body(t, par, ahead):
                    logits(t, par)
                    if ahead:
                        transposed(t + 2, par)

                sweep(pe, body)


class Routing:

    def __init__(self, k, dve, chain, routed, sb):
        self.k, self.dve, self.chain, self.routed, NB = k, dve, chain, routed, k.NB
        self.tmp = [sb(f"t{i}", [P, NB, GR]) for i in range(5)]
        self.greater, self.equal = sb("greater", [P, NB, GR, GR]), sb("equal", [P, NB, GR, GR])
        self.rank, self.top8, self.wsum = sb("rank", [P, NB, GR]), sb("top8", [P, NB, 8]), sb("wsum", [P, NB])
        self.biased, self.masked, self.rest = (sb("biased", [P, NB, E]), sb("masked", [P, NB, E]),
                                               sb("rest", [P, NB, E]))
        cut = [NB * i // 3 for i in range(4)]
        self.steps = (self.bias_and_halves, self.group_scores, self.better, self.as_good, self.as_good_earlier,
                      self.ahead, self.keep, self.mask,
                      lambda: self.largest(0, NB // 2), lambda: self.largest(NB // 2, NB),
                      lambda: self.take_out(cut[0], cut[1]), lambda: self.take_out(cut[1], cut[2]),
                      lambda: self.take_out(cut[2], cut[3]), self.chosen, self.normalise, self.weights)

    def tt(self, out, x, y, op):
        self.chain.step(self.dve.tensor_tensor(out, x, y, op))

    def groups(self, t):
        return t[:].rearrange("p b (g e) -> p b g e", e=EG)

    def bias_and_halves(self):
        k, t = self.k, self.tmp
        self.tt(self.biased[:], k.sc[:], k.bias[:].unsqueeze(1).broadcast_to([P, k.NB, E]), ALU.add)
        self.chain.settle()
        e0, e1, e2, e3 = (self.groups(self.biased)[:, :, :, i] for i in range(EG))
        self.tt(t[0][:], e0, e1, ALU.max)
        self.tt(t[1][:], e0, e1, ALU.min)
        self.tt(t[2][:], e2, e3, ALU.max)
        self.tt(t[3][:], e2, e3, ALU.min)
        self.chain.settle()

    def group_scores(self):
        t = self.tmp
        self.tt(t[4][:], t[0][:], t[2][:], ALU.add)
        self.tt(t[1][:], t[0][:], t[1][:], ALU.add)
        self.tt(t[3][:], t[2][:], t[3][:], ALU.add)
        self.chain.settle()
        self.tt(t[1][:], t[1][:], t[3][:], ALU.max)
        self.chain.settle()
        self.tt(t[4][:], t[4][:], t[1][:], ALU.max)
        self.chain.settle()

    def pairs(self):
        shape = [P, self.k.NB, GR, GR]
        return self.tmp[4][:].unsqueeze(2).broadcast_to(shape), self.tmp[4][:].unsqueeze(3).broadcast_to(shape)

    def better(self):
        self.tt(self.greater[:], *self.pairs(), ALU.is_gt)

    def as_good(self):
        self.tt(self.equal[:], *self.pairs(), ALU.is_equal)
        self.chain.settle()

    def as_good_earlier(self):
        earlier = self.k.earlier[:].rearrange("p (g h) -> p g h", h=GR).unsqueeze(1)
        self.tt(self.equal[:], self.equal[:], earlier.broadcast_to([P, self.k.NB, GR, GR]), ALU.mult)
        self.chain.settle()

    def ahead(self):
        self.tt(self.greater[:], self.greater[:], self.equal[:], ALU.add)
        self.chain.settle()

    def keep(self):
        self.chain.step(self.dve.tensor_reduce(self.rank[:], self.greater[:], X, ALU.add))
        self.chain.settle()
        self.chain.step(self.dve.tensor_scalar(self.rank[:], self.rank[:], float(TOPG), None, ALU.is_lt))
        self.chain.settle()

    def mask(self):
        self.tt(self.groups(self.masked), self.groups(self.biased),
                self.rank[:].unsqueeze(3).broadcast_to([P, self.k.NB, GR, EG]), ALU.mult)
        self.chain.settle()

    def largest(self, lo, hi):
        for b in range(lo, hi):
            self.chain.step(self.dve.max(self.top8[:, b, :], self.masked[:, b, :]))
        self.chain.settle()

    def take_out(self, lo, hi):
        for b in range(lo, hi):
            self.chain.step(self.dve.match_replace(self.rest[:, b, :], self.top8[:, b, :], self.masked[:, b, :],
                                                   -3.0e38))
        self.chain.settle()

    def chosen(self):
        self.tt(self.rest[:], self.rest[:], self.masked[:], ALU.not_equal)
        self.chain.settle()
        self.tt(self.rest[:], self.rest[:], self.k.sc[:], ALU.mult)
        self.chain.settle()

    def normalise(self):
        dve, chain, wsum = self.dve, self.chain, self.wsum
        chain.step(dve.tensor_reduce(wsum[:], self.rest[:], X, ALU.add))
        chain.settle()
        chain.step(dve.tensor_scalar(wsum[:], wsum[:], 1e-20, None, ALU.add))
        chain.settle()
        chain.step(dve.reciprocal(wsum[:], wsum[:]))
        chain.settle()
        chain.step(dve.tensor_scalar(wsum[:], wsum[:], ROUTED_SCALE, self.k.tg[:, TG_F1:TG_F1 + 1],
                                     ALU.mult, ALU.mult))
        chain.settle()

    def weights(self):
        self.dve.tensor_tensor(self.k.comb[:, :, SHARED:], self.rest[:],
                               self.wsum[:].unsqueeze(2).broadcast_to([P, self.k.NB, E]),
                               ALU.mult).then_inc(self.routed, 1)


def experts(k):
    nc, a, NB = k.nc, k.a, k.NB
    NE = a["experts"].shape[0]
    G = BANK // P
    BL = NB // G
    PAIRS = NE // 2
    WG, WU, WD, WN = 0, D, 2 * D, 3 * D
    PARTS = 3
    with ExitStack() as c:
        sem = lambda n: c.enter_context(nc.semaphore("e_" + n))
        sb = lambda n, s, dt=F32: c.enter_context(nc.sbuf_tensor("e_" + n, s, dt))
        w_loaded = [sem("w_loaded0"), sem("w_loaded1")]
        w_high, w_split, pool_copied = sem("w_high"), sem("w_split"), sem("weights_of_tokens")
        g_ready, u_ready, y_ready = sem("g_ready"), sem("u_ready"), sem("y_ready")
        silu_done, gu_done, hi_done, lo_done, acc_done = (sem("silu_done"), sem("gu_done"), sem("hi_done"),
                                                          sem("lo_done"), sem("acc_done"))
        raw = sb("w_raw", [P, 2, WN])
        wh, wl = sb("w_high", [P, 2, WN], F32R), sb("w_low", [P, 2, WN], F32R)
        ce = sb("token_weight", [P, 2, NB])
        silu, gu = sb("silu", [P, 2, BANK]), sb("gu", [P, 2, BANK])
        guh, gul = sb("gu_high", [P, 2, BANK], F32R), sb("gu_low", [P, 2, BANK], F32R)
        route_chain, routed, stored = sem("route_chain"), sem("routed"), sem("stored")
        routing = Routing(k, nc.vector, Chain(nc.vector, route_chain), routed, sb)
        block = c.enter_context(nc.Block())

        def sweep(eng, body):
            body(0, True, False)
            with eng.Fori(1, PAIRS - 1) as it:
                body(it, False, False)
            body(PAIRS - 1, False, True)

        @block.sync
        def _(sp):
            def load(e, ep):
                sp.dma_start(raw[:, ep], a["experts"][e]).then_inc(w_loaded[ep], 16)

            load(0, 0)
            load(1, 1)
            with sp.Fori(0, PAIRS - 1) as it:
                for ep in range(2):
                    sp.wait_ge(w_split, (it * 2 + ep + 1) * PARTS)
                    load(it * 2 + ep + 2, ep)
            for blk in range(BL):
                sp.wait_ge(acc_done, (NE - 1) * BL + blk + 3)
                at = slice(blk * G, (blk + 1) * G)
                sp.dma_start(a["out"][at].rearrange("b p d -> p b d"), k.xs[:, at, :]).then_inc(stored, 16)
            sp.wait_ge(stored, 16 * BL)

        @block.gpsimd
        def _(pool):
            def token_weights(e, ep):
                pool.tensor_copy(ce[:, ep, :], k.comb[:, :, e]).then_inc(pool_copied, 1)

            def split(e, ep, c):
                at = slice(c * D, (c + 1) * D)
                pool.wait_ge(w_high, e * PARTS + c + 1)
                pool.tensor_tensor(wl[:, ep, at], raw[:, ep, at], wh[:, ep, at].bitcast(F32),
                                   ALU.subtract).then_inc(w_split, 1)

            def low(s, par):
                pool.wait_ge(hi_done, s + 1)
                pool.tensor_tensor(gul[:, par], gu[:, par], guh[:, par].bitcast(F32), ALU.subtract)\
                    .then_inc(lo_done, 1)

            pool.sem_inc(lo_done, 2)
            token_weights(0, 0)
            for c in range(PARTS):
                split(0, 0, c)

            def body(it, first, last):
                for ep in range(2):
                    e = it * 2 + ep
                    for blk in range(BL):
                        low(e * BL + blk, blk % 2)
                        if 1 <= blk <= PARTS and not (last and ep == 1):
                            if blk == 1:
                                pool.wait_ge(acc_done, e * BL + 2)
                                if not (first and ep == 1):
                                    token_weights(e + 1, 1 - ep)
                            split(e + 1, 1 - ep, blk - 1)
                if first:
                    pool.wait_ge(routed, 1)
                    token_weights(SHARED, SHARED % 2)

            sweep(pool, body)

        @block.scalar
        def _(act):
            act.sem_inc(silu_done, 2)

            def step(s, par):
                act.wait_ge(g_ready, s + 1)
                act.wait_ge(gu_done, s + 1)
                act.activation(silu[:, par], k.bank[par][:], ACT.Silu).then_inc(silu_done, 1)
                act.wait_ge(gu_done, s + 3)
                act.activation(guh[:, par], gu[:, par], ACT.Copy).then_inc(hi_done, 1)

            def high(ep, c):
                at = slice(c * D, (c + 1) * D)
                act.activation(wh[:, ep, at], raw[:, ep, at], ACT.Copy).then_inc(w_high, 1)

            act.wait_ge(w_loaded[0], 16)
            for c in range(PARTS):
                high(0, c)

            def body(it, first, last):
                for ep in range(2):
                    for blk in range(BL):
                        step((it * 2 + ep) * BL + blk, blk % 2)
                        if 1 <= blk <= PARTS and not (last and ep == 1):
                            if blk == 1:
                                act.wait_ge(acc_done, (it * 2 + ep) * BL + 2)
                                act.wait_ge(w_loaded[1 - ep], (it + 1 + ep) * 16)
                            high(1 - ep, blk - 1)

            sweep(act, body)

        @block.vector
        def _(dve):
            dve.sem_inc(gu_done, 2)
            dve.sem_inc(acc_done, 2)

            def gated(s, par):
                dve.wait_ge(silu_done, s + 3)
                dve.wait_ge(u_ready, s + 1)
                dve.wait_ge(lo_done, s + 1)
                dve.tensor_tensor(gu[:, par], silu[:, par], k.bank[2 + par][:], ALU.mult).then_inc(gu_done, 1)

            def add(e, ep, blk):
                if blk == 0:
                    dve.wait_ge(pool_copied, e + 1)
                dve.wait_ge(y_ready, e * BL + blk + 1)
                for j in range(G):
                    b = blk * G + j
                    xb = k.xs[:, b, :]
                    bank = k.bank[4 + blk % 2 * 2 + j // 2]
                    ins = dve.scalar_tensor_tensor(xb, bank[:, j % 2 * D:j % 2 * D + D], ce[:, ep, b:b + 1], xb,
                                                   ALU.mult, ALU.add)
                ins.then_inc(acc_done, 1)

            gated(0, 0)

            def body(it, first, last):
                for ep in range(2):
                    e = it * 2 + ep
                    for blk in range(BL):
                        if not (last and ep == 1 and blk == BL - 1):
                            gated(e * BL + blk + 1, 1 - blk % 2)
                        if first:
                            routing.steps[ep * BL + blk]()
                        add(e, ep, blk)

            sweep(dve, body)

        @block.tensor
        def _(pe):
            def gate_and_up(e, ep, blk):
                s, par = e * BL + blk, blk % 2
                if blk == 0:
                    pe.wait_ge(w_split, (e + 1) * PARTS)
                at = slice(blk * BANK, blk * BANK + BANK)
                for w0, bank, free, ready in ((WG, k.bank[par], silu_done, g_ready),
                                              (WU, k.bank[2 + par], gu_done, u_ready)):
                    pe.wait_ge(free, s + 1)
                    for kk in range(K2):
                        w = slice(w0 + kk * P, w0 + kk * P + P)
                        ins = three_passes(pe, bank[:], wh[:, ep, w], wl[:, ep, w], k.hTh[:, kk, at], k.hTl[:, kk, at],
                                           kk == 0, kk == K2 - 1)
                    ins.then_inc(ready, 1)

            def down(e, ep, blk):
                s, par = e * BL + blk, blk % 2
                pe.wait_ge(hi_done, s + 1)
                pe.wait_ge(lo_done, s + 3)
                pe.wait_ge(acc_done, s + 1)
                for j in range(G):
                    out = k.bank[4 + par * 2 + j // 2][:, j % 2 * D:j % 2 * D + D]
                    t = slice(j * P, j * P + P)
                    ins = three_passes(pe, out, guh[:, par, t], gul[:, par, t], wh[:, ep, WD:WN], wl[:, ep, WD:WN],
                                       True, True)
                ins.then_inc(y_ready, 1)

            gate_and_up(0, 0, 0)

            def body(it, first, last):
                for ep in range(2):
                    e = it * 2 + ep
                    for blk in range(BL):
                        if blk < BL - 1:
                            gate_and_up(e, ep, blk + 1)
                        elif not (last and ep == 1):
                            gate_and_up(e + 1, 1 - ep, 0)
                        down(e, ep, blk)

            sweep(pe, body)


def layouts(i):
    import numpy as np

    f = {n: np.asarray(v) for n, v in i.items()}
    B = f["x"].shape[0]
    col = lambda v, p: np.ascontiguousarray(v.reshape(-1, p).T)
    rows = lambda v: np.ascontiguousarray(np.broadcast_to(v, (P, v.size)))
    halves = lambda v: v.reshape(64, 2, 8).transpose(1, 0, 2).reshape(P, 8)
    chunks = lambda v: v.reshape(-1, P, v.shape[-1]).transpose(1, 0, 2)
    per_expert = lambda w: w.transpose(0, 2, 1).reshape(w.shape[0], K2, P, P).transpose(0, 2, 1, 3).reshape(-1, P, D)
    gate = np.concatenate([f["L1_ffn_sh_gate"].reshape(2, P, D), f["L1_ffn_w_gate"]])
    up = np.concatenate([f["L1_ffn_sh_up"].reshape(2, P, D), f["L1_ffn_w_up"]])
    down = np.concatenate([f["L1_ffn_sh_down"].T.reshape(2, P, D), f["L1_ffn_w_down"].transpose(0, 2, 1)])
    tri = np.tril(np.ones((8, 8), np.float32), -1).reshape(-1)
    eye64 = np.eye(64, dtype=np.float32)
    win = chunks(f["L0_ffn_Win"])
    return {
        "x": f["x"],
        "ctx": f["ctx_1024"].reshape(B // 2, 2, P, D),
        "ctxT": f["ctx_1024"].reshape(B // 2, 2, P, K2, P).transpose(0, 4, 3, 1, 2),
        "ident": np.eye(P, dtype=np.float32),
        "eye2": np.concatenate([eye64, eye64]),
        "head_rows": np.repeat(np.eye(4, dtype=np.float32), 32, axis=0) * np.float32(32 ** -0.5),
        "gates": rows(np.concatenate([f["g_xattn"], f["g_ffn"], f["L1_xattn_gate"]])),
        "w1c": halves(f["L0_ffn_W1"]), "b1c": halves(f["L0_ffn_b1"]), "w2c": halves(f["L0_ffn_W2"]),
        "w2row": f["L0_ffn_W2"], "b1row": f["L0_ffn_b1"], "b2c": f["L0_ffn_b2"].reshape(64, 1),
        "binc": np.tile(f["L0_ffn_bin_"], 2).reshape(P, 1),
        "win": np.concatenate([win, win], axis=2),
        "wout0": np.concatenate([f["L0_ffn_Wout"], f["L0_ffn_bout"].reshape(1, D)]),
        "attn_w": np.concatenate([chunks(f["L1_xattn_" + n]).reshape(P, -1) for n in ("w_kv", "w_q", "w_out")], axis=1),
        "gammaT": col(f["L1_xattn_ln_gamma"], P), "betaT": col(f["L1_xattn_ln_beta"], P),
        "b_out": rows(f["L1_xattn_b_out"]),
        "gate_wT": chunks(f["L1_ffn_gate_w"].T), "gate_bias": rows(f["L1_ffn_gate_bias"]), "earlier": rows(tri),
        "experts": np.concatenate([per_expert(gate), per_expert(up), down], axis=2),
    }


def kernel(**inputs):
    import numpy as np
    import concourse.bacc as bacc
    from concourse.bass_utils import run_bass_kernel_spmd

    nc = bacc.Bacc("TRN2", target_bir_lowering=False, num_devices=1)
    arrays, aps = {}, {}
    for name, v in layouts(inputs).items():
        v = np.ascontiguousarray(v)
        arrays["in_" + name] = v
        aps[name] = nc.dram_tensor("in_" + name, v.shape, mybir.dt.from_np(v.dtype), kind="ExternalInput").ap()
    aps["out"] = nc.dram_tensor("out_x", inputs["x"].shape, F32, kind="ExternalOutput").ap()
    build(nc, aps)
    return run_bass_kernel_spmd(nc, [arrays], core_ids=[0]).results[0]["out_x"]
```

```python
from contextlib import ExitStack

import concourse.bass as bass
from concourse import mybir

F32 = mybir.dt.float32
F32R = mybir.dt.float32r
ALU = mybir.AluOpType
ACT = mybir.ActivationFunctionType
X = mybir.AxisListType.X

P = 128
D = 256
K2 = D // P
BANK = 512
EPS = 1e-5
E, GR, TOPG, SHARED = 32, 8, 4, 2
EG = E // GR
ROUTED_SCALE = 2.5


class Chain:

    def __init__(self, eng, sem):
        self.eng, self.sem, self.base, self.n = eng, sem, 0, 0

    def step(self, ins):
        ins.then_inc(self.sem, 1)
        self.n += 1
        return ins

    def settle(self):
        self.eng.wait_ge(self.sem, self.base + self.n)

    def enter_loop(self, it, per):
        self.before, self.base, self.n = self.base + self.n, self.base + self.n + it * per, 0
        self.per = per

    def leave_loop(self, trips):
        assert self.n == self.per, (self.n, self.per)
        self.base, self.n = self.before + trips * self.per, 0


def build(nc, a):
    NB = a["x"].shape[0]
    NT = NB * P
    with ExitStack() as ctx:
        k = Kernel(nc, a, NB, ctx)
        k.early = EarlyNorm(k, lambda n: ctx.enter_context(nc.semaphore(n)),
                            lambda n, s: ctx.enter_context(nc.sbuf_tensor(n, s, F32)))
        with ExitStack() as inner:
            k.folding = Folding(k, lambda n: inner.enter_context(nc.semaphore(n)),
                                lambda n, s: inner.enter_context(nc.sbuf_tensor(n, s, F32)))
            attention0(k)
            k.awh = inner.enter_context(nc.sbuf_tensor("attn_w_high", [P, a["attn_w"].shape[1]], F32R))
            k.awl = inner.enter_context(nc.sbuf_tensor("attn_w_low", [P, a["attn_w"].shape[1]], F32R))
            relu_ffn(k)
            attention1(k)
        with ExitStack() as inner:
            k.hTh = inner.enter_context(nc.sbuf_tensor("hT_high", [P, K2, NT], F32R))
            k.hTl = inner.enter_context(nc.sbuf_tensor("hT_low", [P, K2, NT], F32R))
            k.sc = inner.enter_context(nc.sbuf_tensor("scores", [P, NB, E], F32))
            k.bias = inner.enter_context(nc.sbuf_tensor("gate_bias", [P, E], F32))
            k.earlier = inner.enter_context(nc.sbuf_tensor("earlier", [P, GR * GR], F32))
            k.weights = ExpertWeights(k, lambda n: inner.enter_context(nc.semaphore(n)),
                                      lambda n, s, dt=F32: inner.enter_context(nc.sbuf_tensor(n, s, dt)))
            router(k)
            experts(k)


class Kernel:
    def __init__(self, nc, a, NB, ctx):
        self.nc, self.a, self.NB = nc, a, NB

        def sb(name, shape, dt=F32):
            return ctx.enter_context(nc.sbuf_tensor(name, shape, dt))

        self.bank = [ctx.enter_context(nc.psum_tensor(f"bank{i}", [P, BANK], F32)) for i in range(8)]
        self.xs = sb("x_resident", [P, NB, D])
        self.ident = sb("identity", [P, P])
        self.gates = sb("gates_raw", [P, 5])
        self.tg = sb("gates_tanh", [P, 6])
        self.minus_half, self.eps, self.zero = sb("minus_half", [P, 1]), sb("eps", [P, 1]), sb("zero", [P, 1])
        self.diag = sb("w2_diagonals", [P, 8, 64])
        self.w1 = sb("w1_columns", [P, 8])
        self.negb1 = sb("minus_b1", [P, 8])
        self.bin = sb("bin_column", [P, 1])
        self.gbias = sb("g_bias", [64, 1])
        self.win = sb("win", [P, K2, P])
        self.wout0 = sb("wout_and_bout", [65, D])
        self.comb = sb("combine", [P, NB, SHARED + E])


TG_X0, TG_X1, TG_F0, TG_F1, TG_GATE, TG_X1GATE = range(6)


def rstd_steps(pool, k, n, mv, veps, rstd, stats_ready, veps_done, rstd_ready):
    pool.wait_ge(stats_ready, n + 1)
    pool.tensor_tensor(veps, mv[:, 1:2], k.eps[:], ALU.add).then_inc(veps_done, 1)
    pool.wait_ge(veps_done, n + 1)
    pool.tensor_tensor(rstd, veps, k.minus_half[:], ALU.pow).then_inc(rstd_ready, 1)


def three_passes(pe, out, ah, al, bh, bl, first, last):
    pe.matmul(out, ah, bh, start=first, stop=False)
    pe.matmul(out, al, bh, start=False, stop=False)
    return pe.matmul(out, ah, bl, start=False, stop=last)


class Folding:

    def __init__(self, k, sem, sb):
        self.k, self.loaded, self.done = k, sem("const_loaded"), sem("folded")
        self.eye2, self.w2, self.b1c = sb("eye2", [P, 64]), sb("w2c", [P, 8]), sb("b1c", [P, 8])
        self.w2row, self.b1row, self.prod = sb("w2row", [64, 16]), sb("b1row", [64, 16]), sb("prod", [64, 16])
        self.b2c, self.w2b1 = sb("b2c", [64, 1]), sb("w2b1", [64, 1])
        self.loads = [(self.eye2, "eye2"), (k.w1, "w1c"), (self.b1c, "b1c"), (self.w2, "w2c"),
                      (self.w2row, "w2row"), (self.b1row, "b1row"), (self.b2c, "b2c"), (k.bin, "binc"),
                      (k.win, "win"), (k.wout0, "wout0")]
        self.steps = 8 + 5

    def load(self, sp):
        for dst, name in self.loads:
            sp.dma_start(dst[:], self.k.a[name]).then_inc(self.loaded, 16)

    def fold(self, dve):
        k, chain = self.k, Chain(dve, self.done)
        dve.wait_ge(self.loaded, 16 * len(self.loads))
        for j in range(8):
            chain.step(dve.tensor_scalar(k.diag[:, j, :], self.eye2[:], self.w2[:, j:j + 1], None, ALU.mult))
        chain.step(dve.tensor_scalar(k.negb1[:], self.b1c[:], -1.0, None, ALU.mult))
        chain.step(dve.tensor_tensor(self.prod[:], self.w2row[:], self.b1row[:], ALU.mult))
        chain.settle()
        chain.step(dve.tensor_reduce(self.w2b1[:], self.prod[:], X, ALU.add))
        chain.settle()
        chain.step(dve.tensor_tensor(k.gbias[:], self.w2b1[:], self.b2c[:], ALU.add))
        chain.step(dve.tensor_tensor(k.tg[:, TG_X1GATE:TG_X1GATE + 1], k.tg[:, TG_X1:TG_X1 + 1],
                                     k.tg[:, TG_GATE:TG_GATE + 1], ALU.mult))
        chain.settle()
        assert chain.n == self.steps


def moments(dve, src, stats, mv, stats_ready):
    dve.bn_stats(stats, src)
    dve.drain()
    dve.bn_aggr(mv, stats).then_inc(stats_ready, 1)


def apply_norm(dve, src, dst, mv, rstd, rstd_ready, n):
    dve.wait_ge(rstd_ready, n + 1)
    return dve.tensor_scalar(dst, src, mv[:, 0:1], rstd, ALU.subtract, ALU.mult)


class EarlyNorm:
    FFN, ATTENTION_X, ATTENTION_NORMED, ROUTER = range(4)

    def __init__(self, k, sem, sb):
        self.k, G = k, BANK // P
        self.stats_done, self.veps_done, self.rstd_done, self.ready = (sem("early_stats_done"), sem("early_veps_done"),
                                                                    sem("early_rstd_done"), sem("early_ready"))
        self.xn, self.stats = sb("early_xn", [P, G, D]), sb("early_stats", [P, G, 6])
        self.mv = sb("early_mv", [P, G, 2])
        self.veps, self.rstd = sb("early_veps", [P, G]), sb("early_rstd", [P, G])

    def first_moments(self, dve, src, n):
        for j in range(n):
            dve.bn_stats(self.stats[:, j, :], src[:, j, :])
        dve.drain()
        for j in range(n):
            ins = dve.bn_aggr(self.mv[:, j, :], self.stats[:, j, :])
        ins.then_inc(self.stats_done, 1)

    def first_rstd(self, pool, use, n):
        pool.wait_ge(self.stats_done, use + 1)
        pool.tensor_tensor(self.veps[:, 0:n], self.mv[:, 0:n, 1], self.k.eps[:].broadcast_to([P, n]), ALU.add)\
            .then_inc(self.veps_done, 1)
        pool.wait_ge(self.veps_done, use + 1)
        pool.tensor_tensor(self.rstd[:, 0:n], self.veps[:, 0:n], self.k.minus_half[:].broadcast_to([P, n]), ALU.pow)\
            .then_inc(self.rstd_done, 1)

    def first_normed(self, dve, use, src, dst, n):
        dve.wait_ge(self.rstd_done, use + 1)
        for j in range(n):
            ins = dve.tensor_scalar(dst[:, j, :], src[:, j, :], self.mv[:, j, 0:1], self.rstd[:, j:j + 1],
                                    ALU.subtract, ALU.mult)
        ins.then_inc(self.ready, 1)


def attention0(k):
    nc, a, NB = k.nc, k.a, k.NB
    H, DH = 8, 32
    U = 4
    trips = NB // U - 1
    with ExitStack() as c:
        sem = lambda n: c.enter_context(nc.semaphore("a0_" + n))
        sb = lambda n, s, dt=F32: c.enter_context(nc.sbuf_tensor("a0_" + n, s, dt))
        x_loaded, consts_loaded, tanh_done, consts_set = (sem("x_loaded"), sem("consts_loaded"), sem("tanh_done"),
                                                          sem("consts_set"))
        ctx_loaded = [sem(f"ctx_loaded{i}") for i in range(U)]
        stats_ready, veps_done, rstd_ready = sem("stats_ready"), sem("veps_done"), sem("rstd_ready")
        xn_ready, t_ready, q_copied = sem("xn_ready"), sem("t_ready"), sem("q_copied")
        s_ready, max_ready, exp_done = sem("s_ready"), sem("max_ready"), sem("exp_done")
        pt_ready, pt_copied = sem("pt_ready"), sem("pt_copied")
        ov_ready, ov_copied, added = sem("ov_ready"), sem("ov_copied"), sem("added")
        dve_chain = sem("dve_chain")
        ctxT = sb("ctxT", [P, U, K2, P])
        cv = sb("ctx", [P, U, D])
        xn = sb("xn", [P, 2, D])
        qT = sb("qT", [P, 2, K2, 4, P])
        head_rows = sb("head_rows", [P, 4])
        pr = sb("probs", [P, 2, H, P])
        pT = sb("probsT", [P, 2, H, P])
        stats, mv, veps, rstd = sb("stats", [P, 6]), sb("mv", [P, 2]), sb("veps", [P, 1]), sb("rstd", [P, 1])
        nmax, rsum = sb("minus_max", [P, 2, H]), sb("row_sum", [P, 2, H])
        rinv = sb("inverse_sum", [P, 2, H])
        upd = sb("update", [P, 2, D])
        consts = [(k.ident, "ident"), (head_rows, "head_rows"), (k.gates, "gates")]
        S, BT, BP0, BP1, BO = k.bank[0:4], k.bank[4], k.bank[5], k.bank[6], k.bank[7]
        block = c.enter_context(nc.Block())

        @block.sync
        def _(sp):
            def x_chunk(n):
                sp.dma_start(k.xs[:, bass.ds(n * U, U), :],
                             a["x"][bass.ds(n * U, U)].rearrange("b p d -> p b d")).then_inc(x_loaded, 16)

            def context(pair, half, slot):
                sp.dma_start(ctxT[:, slot], a["ctxT"][pair, :, :, half, :]).then_inc(ctx_loaded[slot], 16)
                sp.dma_start(cv[:, slot], a["ctx"][pair, half]).then_inc(ctx_loaded[slot], 16)

            x_chunk(0)
            for dst, name in consts:
                sp.dma_start(dst[:], a[name]).then_inc(consts_loaded, 16)
            for j in range(U):
                context(j // 2, j % 2, j)
            sp.wait_ge(x_loaded, 16)
            x_chunk(1)
            k.folding.load(sp)

            def body(it, more_x):
                if more_x:
                    sp.wait_ge(x_loaded, it * 16 + 32)
                    x_chunk(it + 2)
                for j in range(U):
                    sp.wait_ge(ov_ready, it * U + j + 1)
                    context(it * 2 + 2 + j // 2, j % 2, j)

            with sp.Fori(0, trips - 1) as it:
                body(it, True)
            body(trips - 1, False)

        @block.gpsimd
        def _(pool):
            def inverse_deviation(n):
                rstd_steps(pool, k, n, mv, veps[:], rstd[:], stats_ready, veps_done, rstd_ready)

            pool.memset(k.minus_half[:], -0.5).then_inc(consts_set, 1)
            pool.memset(k.eps[:], EPS).then_inc(consts_set, 1)
            pool.memset(k.zero[:], 0.0).then_inc(consts_set, 1)
            pool.wait_ge(consts_set, 3)
            pool.sem_inc(added, 1)
            for n in range(4):
                inverse_deviation(n)

            def body(it, last):
                for j in range(U):
                    b = it * U + j
                    if not last:
                        inverse_deviation(b + 4)
                    pool.wait_ge(ov_copied, b + 2)
                    xb = k.xs[:, b, :]
                    pool.tensor_tensor(xb, xb, upd[:, j % 2, :], ALU.add).then_inc(added, 1)

            with pool.Fori(0, trips) as it:
                body(it, False)
            k.early.first_rstd(pool, EarlyNorm.FFN, U)
            body(trips, True)

        @block.vector
        def _(dve):
            chain = Chain(dve, dve_chain)

            def measure(b, x_count):
                dve.wait_ge(x_loaded, x_count)
                moments(dve, k.xs[:, b, :], stats[:], mv[:], stats_ready)

            def apply(b, par):
                apply_norm(dve, k.xs[:, b, :], xn[:, par, :], mv, rstd[:], rstd_ready, b).then_inc(xn_ready, 1)

            def norm(b, par, x_count):
                measure(b, x_count)
                apply(b, par)

            def queries(b, par):
                dve.wait_ge(t_ready, b + 1)
                for kk in range(K2):
                    ins = dve.tensor_tensor(qT[:, par, kk],
                                            BT[:, kk * P:kk * P + P].unsqueeze(1).broadcast_to([P, 4, P]),
                                            head_rows[:].unsqueeze(2).broadcast_to([P, 4, P]), ALU.mult)
                ins.then_inc(q_copied, 1)

            def maxima(b, par):
                for kk in range(K2):
                    dve.wait_ge(s_ready, b * K2 + kk + 1)
                    dve.tensor_reduce(nmax[:, par, kk * 4:kk * 4 + 4],
                                      S[par * 2 + kk][:].rearrange("p (j t) -> p j t", j=4),
                                      X, ALU.max, negate=True).then_inc(max_ready, 1)

            def inverse_sums(b, par):
                dve.wait_ge(exp_done, b + 1)
                chain.step(dve.reciprocal(rinv[:, par, :], rsum[:, par, :]))

            def output(b, par):
                chain.settle()
                dve.wait_ge(ov_ready, b + 1)
                dve.wait_ge(added, b + 1)
                dve.scalar_tensor_tensor(upd[:, par, :].rearrange("p (h e) -> p h e", h=H),
                                         BO[:, 0:D].rearrange("p (h e) -> p h e", h=H), k.tg[:, TG_X0:TG_X0 + 1],
                                         rinv[:, par, :].unsqueeze(2).broadcast_to([P, H, DH]),
                                         ALU.mult, ALU.mult).then_inc(ov_copied, 1)

            dve.sem_inc(ov_copied, 1)
            norm(0, 0, 16)
            norm(1, 1, 16)
            dve.wait_ge(consts_loaded, 16 * len(consts))
            queries(0, 0)
            norm(2, 0, 16)
            queries(1, 1)
            norm(3, 1, 16)
            maxima(0, 0)
            queries(2, 0)
            maxima(1, 1)
            dve.wait_ge(tanh_done, 1)

            def body(it, last):
                for j in range(U):
                    b, par = it * U + j, j % 2
                    if not last or j + 3 < U:
                        queries(b + 3, 1 - par)
                    if not last:
                        measure(b + 4, it * 16 + 32)
                    inverse_sums(b, par)
                    if not last or j + 2 < U:
                        maxima(b + 2, par)
                    if not last:
                        apply(b + 4, par)
                    output(b, par)

            with dve.Fori(0, trips) as it:
                chain.enter_loop(it, U)
                body(it, False)
            chain.leave_loop(trips)
            dve.wait_ge(added, U + 1)
            k.early.first_moments(dve, k.xs[:, 0:U, :], U)
            body(trips, True)
            k.early.first_normed(dve, EarlyNorm.FFN, k.xs[:, 0:U, :], k.early.xn, U)

        @block.scalar
        def _(act):
            def exponentials(b, par, heads):
                act.wait_ge(max_ready, b * K2 + heads[0] // 4 + 1)
                for h in heads:
                    kk, j = divmod(h, 4)
                    ins = act.activation(pr[:, par, h, :], S[par * 2 + kk][:, j * P:j * P + P], ACT.Exp,
                                         bias=nmax[:, par, h:h + 1], accum_out=rsum[:, par, h:h + 1])
                return ins

            act.wait_ge(consts_loaded, 16 * len(consts))
            act.activation(k.tg[:, 0:5], k.gates[:], ACT.Tanh).then_inc(tanh_done, 1)
            exponentials(0, 0, range(4))
            exponentials(0, 0, range(4, H)).then_inc(exp_done, 1)

            def body(it, last):
                for j in range(U):
                    b, par = it * U + j, j % 2
                    if not last or j + 1 < U:
                        exponentials(b + 1, 1 - par, range(4))
                        exponentials(b + 1, 1 - par, range(4, H)).then_inc(exp_done, 1)
                    for n in range(2):
                        act.wait_ge(pt_ready, b * 2 + 1 + n)
                        act.activation(pT[:, par, 4 * n:4 * n + 4, :], (BP0, BP1)[n][:], ACT.Copy)\
                           .then_inc(pt_copied, 1)

            with act.Fori(0, trips) as it:
                body(it, False)
            body(trips, True)

        @block.tensor
        def _(pe):
            def transposed_queries(b, par):
                pe.wait_ge(xn_ready, b + 1)
                pe.wait_ge(q_copied, b)
                for kk in range(K2):
                    ins = pe.transpose(BT[:, kk * P:kk * P + P],
                                       xn[:, par, kk * P:kk * P + P], k.ident[:])
                ins.then_inc(t_ready, 1)

            def scores(b, par, slot, loads):
                pe.wait_ge(ctx_loaded[slot], loads)
                pe.wait_ge(q_copied, b + 1)
                for kk in range(K2):
                    for j in range(4):
                        ins = pe.matmul(S[par * 2 + kk][:, j * P:j * P + P], qT[:, par, kk, j, :],
                                        ctxT[:, slot, kk, :], start=True, stop=True)
                    ins.then_inc(s_ready, 1)

            pe.wait_ge(consts_loaded, 16 * len(consts))
            transposed_queries(0, 0)
            transposed_queries(1, 1)
            scores(0, 0, 0, 32)
            transposed_queries(2, 0)
            scores(1, 1, 1, 32)

            def body(it, last):
                for j in range(U):
                    b, par = it * U + j, j % 2
                    if not last or j + 3 < U:
                        transposed_queries(b + 3, 1 - par)
                    pe.wait_ge(exp_done, b + 1)
                    for h in range(H):
                        bank = (BP0, BP1)[h // 4]
                        ins = pe.transpose(bank[:, h % 4 * P:h % 4 * P + P], pr[:, par, h, :], k.ident[:])
                        if h % 4 == 3:
                            ins.then_inc(pt_ready, 1)
                    if not last or j + 2 < U:
                        scores(b + 2, par, (j + 2) % U, (it + (j + 2) // U) * 32 + 32)
                    pe.wait_ge(pt_copied, b * 2 + 2)
                    pe.wait_ge(ov_copied, b + 1)
                    for h in range(H):
                        ins = pe.matmul(BO[:, h * DH:h * DH + DH],
                                        pT[:, par, h, :], cv[:, j, h * DH:h * DH + DH], start=True, stop=True)
                    ins.then_inc(ov_ready, 1)

            with pe.Fori(0, trips) as it:
                body(it, False)
            body(trips, True)


def relu_ffn(k):
    nc, NB = k.nc, k.NB
    G = BANK // P
    NBLK, M = NB // G, 64
    LOOPED = NBLK - 3
    with ExitStack() as c:
        sem = lambda n: c.enter_context(nc.semaphore("f0_" + n))
        sb = lambda n, s: c.enter_context(nc.sbuf_tensor("f0_" + n, s, F32))
        stats_ready, veps_done, rstd_ready = sem("stats_ready"), sem("veps_done"), sem("rstd_ready")
        xn_ready, xt_ready, xt_copied = sem("xn_ready"), sem("xt_ready"), sem("xt_copied")
        s_ready, s_copied, h_ready, g_step = sem("s_ready"), sem("s_copied"), sem("h_ready"), sem("g_step")
        g_copied, o_ready, o_added = sem("g_copied"), sem("o_ready"), sem("o_added")
        ones_set = sem("ones_set")
        xn, xT = sb("xn", [P, G, D]), sb("xT", [P, K2, BANK])
        s, h = sb("s", [P, BANK]), sb("h", [P, 8, BANK])
        gT = sb("gT", [M + 1, BANK])
        stats, mv = sb("stats", [P, G, 6]), sb("mv", [P, G, 2])
        veps, rstd = sb("veps", [P, G]), sb("rstd", [P, G])
        half = sb("half", [P, G])
        half_set = sem("half_set")
        w_loaded, w_high, w_split = [sem("w_loaded0"), sem("w_loaded1")], sem("w_high"), sem("w_split")
        WCH = k.a["attn_w"].shape[1] // NBLK
        raw = sb("w_raw", [P, 2, WCH])
        BX, BS, BG, BOUT = k.bank[0:2], k.bank[2], k.bank[3], k.bank[4:6]
        block = c.enter_context(nc.Block())

        def steps(eng, body):
            with eng.Fori(0, LOOPED) as t:
                body(t, 0)
            for t in range(LOOPED, NBLK):
                body(t, t - LOOPED + 1)

        @block.gpsimd
        def _(pool):
            pool.memset(gT[M:M + 1, :], 1.0).then_inc(ones_set, 1)
            pool.wait_ge(ones_set, 1)
            pool.memset(half[:], -0.5).then_inc(half_set, 1)
            pool.wait_ge(half_set, 1)

            def split(t, par, loads):
                at = bass.ds(t * WCH, WCH)
                pool.wait_ge(w_loaded[par], loads * 16)
                pool.tensor_copy(k.awh[:, at], raw[:, par, :]).then_inc(w_high, 1)
                pool.wait_ge(w_high, t + 1)
                pool.tensor_tensor(k.awl[:, at], raw[:, par, :], k.awh[:, at].bitcast(F32),
                                   ALU.subtract).then_inc(w_split, 1)

            def inverse_deviations(t):
                pool.wait_ge(stats_ready, t)
                pool.tensor_tensor(veps[:], mv[:, :, 1], k.eps[:].broadcast_to([P, G]), ALU.add).then_inc(veps_done, 1)
                pool.wait_ge(veps_done, t)
                pool.tensor_tensor(rstd[:], veps[:], half[:], ALU.pow).then_inc(rstd_ready, 1)

            def body(it, last):
                for par in range(2):
                    if not (last and par == 1):
                        inverse_deviations(it * 2 + par + 1)
                    split(it * 2 + par, par, it + 1)

            with pool.Fori(0, NBLK // 2 - 1) as it:
                body(it, False)
            body(NBLK // 2 - 1, True)
            k.early.first_rstd(pool, EarlyNorm.ATTENTION_X, 2)
            k.early.first_rstd(pool, EarlyNorm.ATTENTION_NORMED, 2)

        @block.sync
        def _(sp):
            def load(t, par):
                sp.dma_start(raw[:, par, :], k.a["attn_w"][:, bass.ds(t * WCH, WCH)]).then_inc(w_loaded[par], 16)

            load(0, 0)
            load(1, 1)
            with sp.Fori(0, NBLK // 2 - 1) as it:
                for par in range(2):
                    sp.wait_ge(w_split, it * 2 + par + 1)
                    load(it * 2 + par + 2, par)

        @block.vector
        def _(dve):
            def norm(t):
                for j in range(G):
                    dve.bn_stats(stats[:, j, :], k.xs[:, t * G + j, :])
                dve.drain()
                for j in range(G):
                    ins = dve.bn_aggr(mv[:, j, :], stats[:, j, :])
                ins.then_inc(stats_ready, 1)
                dve.wait_ge(rstd_ready, t)
                for j in range(G):
                    ins = dve.tensor_scalar(xn[:, j, :], k.xs[:, t * G + j, :], mv[:, j, 0:1], rstd[:, j:j + 1],
                                            ALU.subtract, ALU.mult)
                ins.then_inc(xn_ready, 1)

            def hidden(t, used):
                dve.wait_ge(s_ready, t + 1)
                dve.wait_ge(h_ready, t * 8)
                dve.tensor_scalar(s[:], BS[:], k.bin[:], None, ALU.add).then_inc(s_copied, 1)
                dve.wait_ge(s_copied, t + 1)
                for j in range(8):
                    if used is not None:
                        dve.wait_ge(g_step, used + j + 1)
                    dve.tensor_scalar(h[:, j, :], s[:], k.w1[:, j:j + 1], k.negb1[:, j:j + 1],
                                      ALU.mult, ALU.max).then_inc(h_ready, 1)

            dve.sem_inc(o_added, 1)
            norm(1)
            k.folding.fold(dve)
            hidden(0, None)
            dve.wait_ge(xt_ready, 2)
            norm(2)

            def body(t, tail):
                if tail < 3:
                    hidden(t + 1, t * 8)
                if tail < 1:
                    dve.wait_ge(xt_ready, t + 3)
                    norm(t + 3)
                first, once, twice = k.xs[:, 0:2, :], k.early.xn[:, 2:4, :], k.early.xn[:, 0:2, :]
                if tail == 1:
                    k.early.first_moments(dve, first, 2)
                elif tail == 2:
                    k.early.first_normed(dve, EarlyNorm.ATTENTION_X, first, once, 2)
                    dve.wait_ge(k.early.ready, EarlyNorm.ATTENTION_X + 1)
                    k.early.first_moments(dve, once, 2)
                elif tail == 3:
                    k.early.first_normed(dve, EarlyNorm.ATTENTION_NORMED, once, twice, 2)
                dve.wait_ge(o_ready, t + 1)
                for j in range(G):
                    xb = k.xs[:, t * G + j, :]
                    ins = dve.scalar_tensor_tensor(xb, BOUT[j // 2][:, j % 2 * D:j % 2 * D + D],
                                                   k.tg[:, TG_F0:TG_F0 + 1], xb, ALU.mult, ALU.add)
                ins.then_inc(o_added, 1)

            steps(dve, body)

        @block.scalar
        def _(act):
            def xt_copy(t):
                act.wait_ge(xt_ready, t + 1)
                for kk in range(K2):
                    ins = act.activation(xT[:, kk, :], BX[kk][:], ACT.Copy)
                ins.then_inc(xt_copied, 1)

            xt_copy(0)
            xt_copy(1)

            def body(t, tail):
                act.wait_ge(g_step, t * 8 + 8)
                act.activation(gT[0:M, :], BG[0:M, :], ACT.Identity, bias=k.gbias[:]).then_inc(g_copied, 1)
                if tail < 2:
                    xt_copy(t + 2)

            steps(act, body)

        @block.tensor
        def _(pe):
            def transposes(t, src=xn):
                if src is xn:
                    pe.wait_ge(xn_ready, t)
                else:
                    pe.wait_ge(k.early.ready, EarlyNorm.FFN + 1)
                for kk in range(K2):
                    for j in range(G):
                        ins = pe.transpose(BX[kk][:, j * P:j * P + P], src[:, j, kk * P:kk * P + P], k.ident[:])
                ins.then_inc(xt_ready, 1)

            def first_product(t):
                pe.wait_ge(xt_copied, t + 1)
                pe.wait_ge(s_copied, t)
                for kk in range(K2):
                    ins = pe.matmul(BS[:], k.win[:, kk, :], xT[:, kk, :], start=kk == 0, stop=kk == K2 - 1)
                ins.then_inc(s_ready, 1)

            transposes(0, k.early.xn)
            first_product(0)
            transposes(1)
            pe.wait_ge(ones_set, 1)
            pe.wait_ge(k.folding.done, k.folding.steps)

            def body(t, tail):
                if tail < 3:
                    first_product(t + 1)
                for j in range(8):
                    pe.wait_ge(h_ready, t * 8 + j + 1)
                    pe.matmul(BG[0:M, :], k.diag[:, j, :], h[:, j, :], start=j == 0, stop=j == 7).then_inc(g_step, 1)
                if tail < 2:
                    transposes(t + 2)
                pe.wait_ge(g_copied, t + 1)
                pe.wait_ge(o_added, t + 1)
                for j in range(G):
                    ins = pe.matmul(BOUT[j // 2][:, j % 2 * D:j % 2 * D + D], gT[:, j * P:j * P + P], k.wout0[:],
                                    start=True, stop=True)
                ins.then_inc(o_ready, 1)

            steps(pe, body)


def attention1(k):
    nc, a, NB = k.nc, k.a, k.NB
    H, DH = 16, 64
    SCALE = DH ** -0.5
    NP = NB // 2
    trips = NP // 2 - 1
    INNER = H * DH
    KC = INNER // P
    FILL = ["XT", "K0", "K1", "Q0", "Q1", "K2", "K3", "Q2", "Q3", "V0", "V1", "V2", "V3"]
    NF, NKQ = len(FILL), FILL.index("V0")
    PER6, PER7 = (NF + 1) // 2, NF // 2
    fills = lambda uu: range(3 * uu, 3 * uu + 3 + uu // 3)
    with ExitStack() as c:
        sem = lambda n: c.enter_context(nc.semaphore("a1_" + n))
        sb = lambda n, s, dt=F32: c.enter_context(nc.sbuf_tensor("a1_" + n, s, dt))
        w_loaded, boadd_ready = sem("w_loaded"), sem("boadd_ready")
        ctx_loaded = [sem("ctx_loaded0"), sem("ctx_loaded1")]
        stats_ready, veps_done, rstd_ready = sem("stats_ready"), sem("veps_done"), sem("rstd_ready")
        xn_ready, proj_ready = sem("xn_ready"), sem("proj_ready")
        copied = [sem("copied6"), sem("copied7")]
        s_ready, max_ready, exp_done = sem("s_ready"), sem("max_ready"), sem("exp_done")
        pt_ready, pt0_copied, pt1_copied = sem("pt_ready"), sem("pt0_copied"), sem("pt1_copied")
        scaled, ov_ready, ot_copied = sem("scaled"), sem("ov_ready"), sem("ot_copied")
        w_ready, w_copied, biased, dve_chain = sem("w_ready"), sem("w_copied"), sem("biased"), sem("dve_chain")
        at_q, at_out = K2 * 2 * INNER, K2 * 3 * INNER
        wkv, wq, wout = ([w[:, lo:hi].rearrange("p (k n) -> p k n", k=kc) for w in (k.awh, k.awl)]
                         for lo, hi, kc in ((0, at_q, K2), (at_q, at_out, K2), (at_out, at_out + KC * D, KC)))
        gam, bet, bo = sb("gammaT", [P, K2]), sb("betaT", [P, K2]), sb("b_out", [P, D])
        raw = sb("ctxT", [P, 2, K2, 2, P])
        ctxT = [sb(n, [P, 2, K2, 2, P], F32R) for n in ("ctxT_high", "ctxT_low")]
        x1, xn, xTf = sb("x1", [P, 2, D]), sb("xn", [P, 2, D]), sb("xT", [P, K2, 2 * P])
        xT = [sb(n, [P, K2, 2 * P], F32R) for n in ("xT_high", "xT_low")]
        qT, kT = sb("qT", [P, 2, KC, 2 * P]), sb("kT", [P, 2, KC, 2 * P])
        v = sb("v", [P, 2, 2, INNER])
        pr, pT = sb("probs", [P, 2, 8, P]), sb("probsT", [P, 2, 8, P])
        oT = [sb(n, [P, KC, P], F32R) for n in ("oT_high", "oT_low")]
        ctx_high, ctx_split, xt_high, xt_split, ot_high = (sem("ctx_high"), sem("ctx_split"), sem("xt_high"),
                                                           sem("xt_split"), sem("ot_high"))
        stats, mv, veps, rstd = sb("stats", [P, 2, 6]), sb("mv", [P, 2, 2]), sb("veps", [P, 2]), sb("rstd", [P, 2])
        nmax, rsum, rinv = sb("minus_max", [P, 2, 4, 2]), sb("row_sum", [P, 2, 8]), sb("inverse_sum", [P, 2, 8])
        block = c.enter_context(nc.Block())
        weights = [(gam, "gammaT"), (bet, "betaT"), (bo, "b_out")]

        def pairs(eng, body, enter=None, leave=None):
            with eng.Fori(0, trips) as it:
                if enter:
                    enter(it)
                for half in range(2):
                    body(it * 2 + half, it, half, 2)
            if leave:
                leave()
            for half in range(2):
                body(2 * trips + half, trips, half, 1 - half)

        @block.sync
        def _(sp):
            def context(p, half):
                sp.dma_start(raw[:, half], a["ctxT"][p]).then_inc(ctx_loaded[half], 16)

            context(0, 0)
            for dst, name in weights:
                sp.dma_start(dst[:], a[name]).then_inc(w_loaded, 16)
            context(1, 1)
            with sp.Fori(0, trips) as it:
                for half in range(2):
                    sp.wait_ge(ctx_split, it * 2 + half + 1)
                    context(it * 2 + half + 2, half)

        @block.gpsimd
        def _(pool):
            def inverse_deviation(n, par):
                one = slice(par, par + 1)
                rstd_steps(pool, k, n, mv[:, par], veps[:, one], rstd[:, one], stats_ready, veps_done, rstd_ready)

            zeros = k.zero[:].unsqueeze(2).unsqueeze(3).broadcast_to([P, K2, 2, P])

            def split_context(q, half, loads):
                pool.wait_ge(ctx_loaded[half], loads * 16)
                pool.tensor_tensor(ctxT[0][:, half], raw[:, half], zeros, ALU.add).then_inc(ctx_high, 1)
                pool.wait_ge(ctx_high, q + 1)
                pool.tensor_tensor(ctxT[1][:, half], raw[:, half], ctxT[0][:, half].bitcast(F32),
                                   ALU.subtract).then_inc(ctx_split, 1)

            def low_input(q):
                pool.wait_ge(xt_high, q + 1)
                pool.tensor_tensor(xT[1][:], xTf[:], xT[0][:].bitcast(F32), ALU.subtract).then_inc(xt_split, 1)

            split_context(0, 0, 1)
            low_input(0)
            for n in range(4):
                inverse_deviation(n, n // 2)
            pool.wait_ge(w_loaded, 16 * len(weights))
            pool.tensor_tensor(bo[:], bo[:], k.tg[:, TG_X1GATE:TG_X1GATE + 1].broadcast_to([P, D]),
                               ALU.mult).then_inc(boadd_ready, 1)
            pool.wait_ge(boadd_ready, 1)
            split_context(1, 1, 1)

            def body(p, it, half, ahead):
                if ahead == 0:
                    k.early.first_rstd(pool, EarlyNorm.ROUTER, BANK // P)
                if ahead >= 2:
                    inverse_deviation(p * 4 + 4, 0)
                if ahead >= 1:
                    low_input(p + 1)
                if ahead >= 2:
                    for n in range(1, 4):
                        inverse_deviation(p * 4 + 4 + n, n // 2)
                    pool.wait_ge(proj_ready, (p + 1) * NF)
                    split_context(p + 2, half, it + 2)
                for j in range(2):
                    b = p * 2 + j
                    pool.wait_ge(w_copied, b + 2)
                    xb = k.xs[:, b, :]
                    pool.tensor_tensor(xb, xb, bo[:], ALU.add).then_inc(biased, 1)

            pairs(pool, body)

        def copy_projection(eng, is_act, half, i):
            bank = k.bank[6 + i % 2]
            kind, n = FILL[i][:-1], FILL[i][-1]
            if kind in "KQ":
                n = int(n)
                dst = (kT if kind == "K" else qT)[:, half, 2 * n:2 * n + 2, :]
                scale = SCALE if kind == "Q" else 1.0
                src = bank[:].rearrange("p (c t) -> p c t", c=2)
            else:
                n = int(n)
                dst, src, scale = v[:, half, n // 2, n % 2 * BANK:n % 2 * BANK + BANK], bank[:], 1.0
            if is_act:
                ins = eng.activation(dst, src, ACT.Copy, scale=scale)
            elif scale != 1.0:
                ins = eng.tensor_scalar(dst, src, scale, None, ALU.mult)
            else:
                ins = eng.tensor_copy(dst, src)
            ins.then_inc(copied[i % 2], 1)

        @block.vector
        def _(dve):
            chain = Chain(dve, dve_chain)

            def measure_x(b, par):
                moments(dve, k.xs[:, b, :], stats[:, par], mv[:, par], stats_ready)

            def measure_normed(b, par, n):
                chain.step(apply_norm(dve, k.xs[:, b, :], x1[:, par], mv[:, par], rstd[:, par:par + 1], rstd_ready, n))
                chain.settle()
                moments(dve, x1[:, par], stats[:, par], mv[:, par], stats_ready)

            def normed_input(par, n):
                apply_norm(dve, x1[:, par], xn[:, par, :], mv[:, par], rstd[:, par:par + 1], rstd_ready, n)\
                    .then_inc(xn_ready, 1)

            def proj(q, half, i):
                if i % 2 == 1:
                    dve.wait_ge(proj_ready, q * NF + i + 1)
                    copy_projection(dve, False, half, i)

            def maxima(u, par):
                dve.wait_ge(s_ready, u + 1)
                for e in range(2):
                    ins = dve.tensor_reduce(nmax[:, par, :, e],
                                            k.bank[2 * par + e][:].rearrange("p (m t) -> p m t", m=4),
                                            X, ALU.max, negate=True)
                ins.then_inc(max_ready, 1)

            def normalised(u, par):
                dve.wait_ge(exp_done, u + 1)
                chain.step(dve.reciprocal(rinv[:, par, :], rsum[:, par, :]))
                chain.settle()
                dve.tensor_tensor(pr[:, par], pr[:, par], rinv[:, par, :].unsqueeze(2).broadcast_to([P, 8, P]),
                                  ALU.mult).then_inc(scaled, 1)

            dve.sem_inc(ot_copied, 1)
            dve.sem_inc(w_copied, 1)
            proj(0, 0, 1)
            measure_x(2, 0)
            proj(0, 0, 3)
            measure_normed(2, 0, 0)
            proj(0, 0, 5)
            normed_input(0, 1)
            proj(0, 0, 7)
            measure_x(3, 1)
            maxima(0, 0)
            maxima(1, 1)
            measure_normed(3, 1, 2)
            proj(0, 0, 9)
            normed_input(1, 3)
            proj(0, 0, 11)
            normalised(0, 0)

            def body(p, it, half, ahead):
                for uu in range(4):
                    u, par = p * 4 + uu, uu % 2
                    normed = p * 2 + 4 + uu // 2 if ahead >= 2 and uu % 2 == 0 else None
                    dve.wait_ge(pt_ready, u * 2 + 1)
                    dve.tensor_copy(pT[:, par, 0:4, :], k.bank[4][:]).then_inc(pt0_copied, 1)
                    if normed is not None:
                        measure_x(normed, uu // 2)
                    if ahead == 0 and uu == 0:
                        first = k.xs[:, 0:BANK // P, :]
                        dve.wait_ge(biased, BANK // P)
                        k.early.first_moments(dve, first, BANK // P)
                    if ahead == 0 and uu == 1:
                        k.early.first_normed(dve, EarlyNorm.ROUTER, first, k.early.xn, BANK // P)
                    if ahead >= 1 or uu < 2:
                        maxima(u + 2, par)
                    if uu == 2:
                        residual(p * 2)
                    if ahead >= 2 and uu % 2 == 1:
                        if uu == 1:
                            dve.wait_ge(proj_ready, (p + 1) * NF + 1)
                        normed_input(uu // 2, (p * 2 + 2 + uu // 2) * 2 + 1)
                    low_output(u, uu)
                    if ahead >= 1:
                        proj(p + 1, 1 - half, fills(uu)[0])
                    if ahead >= 1 or uu < 3:
                        normalised(u + 1, 1 - par)
                    if ahead >= 1:
                        for i in fills(uu)[1:]:
                            proj(p + 1, 1 - half, i)
                    if normed is not None:
                        measure_normed(normed, uu // 2, normed * 2 - 4)
                residual(p * 2 + 1)

            def low_output(u, uu):
                at = slice(uu % 2 * 4, uu % 2 * 4 + 4)
                dve.wait_ge(ot_high, u + 1)
                dve.tensor_tensor(oT[1][:, at, :], k.bank[4][:].rearrange("p (c t) -> p c t", c=4),
                                  oT[0][:, at, :].bitcast(F32), ALU.subtract).then_inc(ot_copied, 1)

            def residual(b):
                dve.wait_ge(w_ready, b + 1)
                xb = k.xs[:, b, :]
                dve.scalar_tensor_tensor(xb, k.bank[5][:, 0:D], k.tg[:, TG_X1GATE:TG_X1GATE + 1], xb,
                                         ALU.mult, ALU.add).then_inc(w_copied, 1)

            pairs(dve, body, lambda it: chain.enter_loop(it, 2 * (4 + 2)), lambda: chain.leave_loop(trips))

        @block.scalar
        def _(act):
            act.wait_ge(w_loaded, 16 * len(weights))

            def proj(q, half, i):
                if i % 2 == 0:
                    act.wait_ge(proj_ready, q * NF + i + 1)
                    if i == 0:
                        for kk in range(K2):
                            ins = act.activation(xTf[:, kk, :], k.bank[6][:, kk * 2 * P:(kk + 1) * 2 * P], ACT.Identity,
                                                 bias=bet[:, kk:kk + 1], scale=gam[:, kk:kk + 1])
                        ins.then_inc(copied[0], 1)
                        act.wait_ge(copied[0], q * PER6 + 1)
                        act.activation(xT[0][:], xTf[:], ACT.Copy).then_inc(xt_high, 1)
                    else:
                        copy_projection(act, True, half, i)

            def exponentials(par, hs):
                for hh in hs:
                    m, e = divmod(hh, 2)
                    ins = act.activation(pr[:, par, hh, :], k.bank[2 * par + e][:, m * P:m * P + P], ACT.Exp,
                                         bias=nmax[:, par, m, e:e + 1], accum_out=rsum[:, par, hh:hh + 1])
                return ins

            for i in range(NKQ):
                proj(0, 0, i)
            act.wait_ge(max_ready, 1)
            exponentials(0, range(8)).then_inc(exp_done, 1)
            for i in range(NKQ, NF):
                proj(0, 0, i)

            def body(p, it, half, ahead):
                for uu in range(4):
                    u, par, octet = p * 4 + uu, uu % 2, uu % 2
                    act.wait_ge(pt_ready, u * 2 + 2)
                    act.activation(pT[:, par, 4:8, :], k.bank[5][:], ACT.Copy).then_inc(pt1_copied, 1)
                    if ahead >= 1 or uu < 3:
                        act.wait_ge(max_ready, u + 2)
                        exponentials(1 - par, range(8)).then_inc(exp_done, 1)
                    act.wait_ge(ov_ready, u + 1)
                    act.activation(oT[0][:, octet * 4:octet * 4 + 4, :], k.bank[4][:], ACT.Copy)\
                       .then_inc(ot_high, 1)
                    if ahead >= 1:
                        for i in fills(uu):
                            proj(p + 1, 1 - half, i)

            pairs(act, body)

        @block.tensor
        def _(pe):
            def proj(q, half, i, first=False):
                bank = k.bank[6 + i % 2]
                pe.wait_ge(copied[i % 2], q * (PER6, PER7)[i % 2] + i // 2)
                if i == 0:
                    if first:
                        pe.wait_ge(k.early.ready, EarlyNorm.ATTENTION_NORMED + 1)
                    else:
                        pe.wait_ge(xn_ready, q * 2)
                    src = k.early.xn if first else xn
                    for kk in range(K2):
                        for j in range(2):
                            ins = pe.transpose(bank[:, kk * 2 * P + j * P:kk * 2 * P + j * P + P],
                                               src[:, j, kk * P:kk * P + P], k.ident[:])
                    ins.then_inc(proj_ready, 1)
                    return
                kind, n = FILL[i][:-1], int(FILL[i][-1])
                if i == 1:
                    pe.wait_ge(ctx_split, q + 1)
                if kind == "Q" and n == 0:
                    pe.wait_ge(xt_split, q + 1)
                if kind == "K":
                    moving = [x[:, half].rearrange("p k b t -> p k (b t)") for x in ctxT]
                else:
                    moving = xT
                if kind in "KQ":
                    w = wkv if kind == "K" else wq
                    for j in range(2):
                        cols = slice((2 * n + j) * P, (2 * n + j + 1) * P)
                        for kk in range(K2):
                            ins = three_passes(pe, bank[:, j * 2 * P:(j + 1) * 2 * P], w[0][:, kk, cols],
                                               w[1][:, kk, cols], moving[0][:, kk, :], moving[1][:, kk, :],
                                               kk == 0, kk == K2 - 1)
                else:
                    cols = slice(INNER + n % 2 * BANK, INNER + (n % 2 + 1) * BANK)
                    for kk in range(K2):
                        ins = three_passes(pe, bank[:], ctxT[0][:, half, kk, n // 2, :],
                                           ctxT[1][:, half, kk, n // 2, :], wkv[0][:, kk, cols],
                                           wkv[1][:, kk, cols], kk == 0, kk == K2 - 1)
                ins.then_inc(proj_ready, 1)

            def scores(half, uu):
                b, octet = uu // 2, uu % 2
                for m in range(4):
                    for e in range(2):
                        r = slice(DH * e, DH * e + DH)
                        ins = pe.matmul(k.bank[2 * (uu % 2) + e][:, m * P:m * P + P],
                                        qT[r, half, octet * 4 + m, b * P:b * P + P],
                                        kT[r, half, octet * 4 + m, b * P:b * P + P], start=True, stop=True)
                ins.then_inc(s_ready, 1)

            def await_projected(q, name):
                upto = FILL.index(name) + 1
                pe.wait_ge(copied[0], q * PER6 + (upto + 1) // 2)
                pe.wait_ge(copied[1], q * PER7 + upto // 2)

            def projected():
                for cc in range(KC):
                    ins = three_passes(pe, k.bank[5][:, 0:D], oT[0][:, cc, :], oT[1][:, cc, :],
                                       wout[0][:, cc, :], wout[1][:, cc, :], cc == 0, cc == KC - 1)
                ins.then_inc(w_ready, 1)

            for i in range(NKQ):
                proj(0, 0, i, True)
            await_projected(0, "Q3")
            scores(0, 0)
            scores(0, 1)
            for i in range(NKQ, NF):
                proj(0, 0, i, True)

            def body(p, it, half, ahead):
                nxt = (p + 1, 1 - half)
                for uu in range(4):
                    u, par = p * 4 + uu, uu % 2
                    b, octet = uu // 2, uu % 2
                    pe.wait_ge(scaled, u + 1)
                    pe.wait_ge(ot_copied, u + 1)
                    for hh in range(8):
                        if hh == 4 and uu in (0, 3):
                            pe.wait_ge(w_copied, p * 2 + 1 + b)
                        ins = pe.transpose(k.bank[4 + hh // 4][:, hh % 4 * P:hh % 4 * P + P],
                                           pr[:, par, hh, :], k.ident[:])
                        if hh % 4 == 3:
                            ins.then_inc(pt_ready, 1)
                    if uu < 2:
                        scores(half, uu + 2)
                    elif ahead >= 1:
                        await_projected(p + 1, "Q1" if uu == 2 else "Q3")
                        scores(1 - half, uu - 2)
                    pe.wait_ge(pt0_copied, u + 1)
                    pe.wait_ge(pt1_copied, u + 1)
                    if uu == 2:
                        projected()
                    if uu == 0:
                        await_projected(p, "V3")
                    for hh in range(8):
                        m, e = divmod(hh, 2)
                        g = octet * 8 + hh
                        ins = pe.matmul(k.bank[4][e * DH:(e + 1) * DH, m * P:(m + 1) * P],
                                        v[:, half, b, g * DH:g * DH + DH], pT[:, par, hh, :], start=True, stop=True)
                    ins.then_inc(ov_ready, 1)
                    if uu == 3:
                        if ahead >= 1:
                            for i in fills(uu)[:-1]:
                                proj(*nxt, i)
                        pe.wait_ge(ot_copied, p * 4 + 5)
                        projected()
                        if ahead >= 1:
                            proj(*nxt, fills(uu)[-1])
                    elif ahead >= 1:
                        for i in fills(uu):
                            proj(*nxt, i)
            pairs(pe, body)


def router(k):
    nc, a, NB = k.nc, k.a, k.NB
    G = BANK // P
    NBLK = NB // G
    trips = NBLK // 2 - 1
    with ExitStack() as c:
        sem = lambda n: c.enter_context(nc.semaphore("r_" + n))
        sb = lambda n, s: c.enter_context(nc.sbuf_tensor("r_" + n, s, F32))
        loaded, xn_ready, t_ready, minus_set = sem("loaded"), sem("xn_ready"), sem("t_ready"), sem("minus_set")
        hf_copied, hi_copied, lo_done, l_ready, l_copied = (sem("hf_copied"), sem("hi_copied"), sem("lo_done"),
                                                                sem("l_ready"), sem("l_copied"))
        stats_ready, veps_done, rstd_ready = sem("stats_ready"), sem("veps_done"), sem("rstd_ready")
        sig_done, shared_set = sem("sig_done"), sem("shared_set")
        gw = sb("gate_wT", [P, K2, E])
        xn, hf = sb("xn", [P, 2, G, D]), sb("hT", [P, 2, K2, BANK])
        lg = sb("logits", [P, NB, E])
        stats, mv = sb("stats", [P, G, 6]), sb("mv", [P, G, 2])
        veps, rstd, minus = sb("veps", [P, G]), sb("rstd", [P, G]), sb("minus_halves", [P, G])
        loads = [(gw, "gate_wT"), (k.bias, "gate_bias"), (k.earlier, "earlier")]

        def sweep(eng, body):
            with eng.Fori(0, trips) as it:
                for par in range(2):
                    body(it * 2 + par, par, True)
            for par in range(2):
                body(trips * 2 + par, par, False)

        with nc.Block() as block:
            @block.sync
            def _(sp):
                for dst, name in loads:
                    sp.dma_start(dst[:], a[name]).then_inc(loaded, 16)
                for e in range(2):
                    k.weights.load(sp, e, e)

            @block.vector
            def _(dve):
                def norm(t, par):
                    for j in range(G):
                        dve.bn_stats(stats[:, j, :], k.xs[:, t * G + j, :])
                    dve.drain()
                    for j in range(G):
                        ins = dve.bn_aggr(mv[:, j, :], stats[:, j, :])
                    ins.then_inc(stats_ready, 1)
                    dve.wait_ge(rstd_ready, t)
                    for j in range(G):
                        ins = dve.tensor_scalar(xn[:, par, j, :], k.xs[:, t * G + j, :], mv[:, j, 0:1],
                                                rstd[:, j:j + 1], ALU.subtract, ALU.mult)
                    ins.then_inc(xn_ready, 1)

                def low(t, par):
                    dve.wait_ge(hi_copied, t + 1)
                    at = bass.ds(t * BANK, BANK)
                    dve.tensor_tensor(k.hTl[:, :, at], hf[:, par], k.hTh[:, :, at].bitcast(F32), ALU.subtract)\
                        .then_inc(lo_done, 1)

                def take_logits(t, par):
                    dve.wait_ge(l_ready, t + 1)
                    dve.tensor_copy(lg[:, bass.ds(t * G, G), :],
                                    k.bank[4 + par][:, 0:G * E].rearrange("p (g e) -> p g e", e=E))\
                       .then_inc(l_copied, 1)

                dve.sem_inc(l_copied, 2)
                dve.sem_inc(lo_done, 2)
                dve.tensor_copy(k.comb[:, :, 0:SHARED],
                                k.tg[:, TG_F1:TG_F1 + 1].unsqueeze(1).broadcast_to([P, NB, SHARED]))\
                   .then_inc(shared_set, 1)
                norm(1, 1)

                def body(t, par, ahead):
                    low(t, par)
                    if ahead:
                        norm(t + 2, par)
                    take_logits(t, par)

                sweep(dve, body)

            @block.gpsimd
            def _(pool):
                pool.memset(minus[:], -0.5).then_inc(minus_set, 1)
                pool.wait_ge(minus_set, 1)
                with pool.Fori(0, NBLK - 1) as t:
                    pool.wait_ge(stats_ready, t + 1)
                    pool.tensor_tensor(veps[:], mv[:, :, 1], k.eps[:].broadcast_to([P, G]), ALU.add)\
                        .then_inc(veps_done, 1)
                    pool.wait_ge(veps_done, t + 1)
                    pool.tensor_tensor(rstd[:], veps[:], minus[:], ALU.pow).then_inc(rstd_ready, 1)
                for c in range(k.weights.PARTS):
                    k.weights.low(pool, 0, 0, c)

            @block.scalar
            def _(act):
                def high(t, par):
                    act.wait_ge(t_ready, t + 1)
                    act.wait_ge(lo_done, t + 1)
                    for kk in range(K2):
                        ins = act.activation(hf[:, par, kk, :], k.bank[par * 2 + kk][:], ACT.Copy)
                    ins.then_inc(hf_copied, 1)
                    act.wait_ge(hf_copied, t + 1)
                    act.activation(k.hTh[:, :, bass.ds(t * BANK, BANK)], hf[:, par], ACT.Copy).then_inc(hi_copied, 1)

                with act.Fori(0, NBLK // 2) as it:
                    for par in range(2):
                        high(it * 2 + par, par)
                act.wait_ge(k.weights.loaded[0], 16)
                for c in range(k.weights.PARTS):
                    k.weights.high(act, 0, c)
                act.wait_ge(l_copied, NBLK + 2)
                act.activation(k.sc[:], lg[:], ACT.Sigmoid).then_inc(sig_done, 1)

            @block.tensor
            def _(pe):
                def transposed(t, par, early=False):
                    if early:
                        pe.wait_ge(k.early.ready, EarlyNorm.ROUTER + 1)
                        src = k.early.xn
                    else:
                        pe.wait_ge(xn_ready, t)
                        src = xn[:, par]
                    for kk in range(K2):
                        for j in range(G):
                            ins = pe.transpose(k.bank[par * 2 + kk][:, j * P:j * P + P],
                                               src[:, j, kk * P:kk * P + P], k.ident[:])
                    ins.then_inc(t_ready, 1)

                def logits(t, par):
                    pe.wait_ge(hf_copied, t + 1)
                    pe.wait_ge(l_copied, t + 1)
                    for j in range(G):
                        for kk in range(K2):
                            ins = pe.matmul(k.bank[4 + par][:, j * E:j * E + E], hf[:, par, kk, j * P:j * P + P],
                                            gw[:, kk, :], start=kk == 0, stop=kk == K2 - 1)
                    ins.then_inc(l_ready, 1)

                transposed(0, 0, early=True)
                transposed(1, 1)
                pe.wait_ge(loaded, 16 * len(loads))

                def body(t, par, ahead):
                    logits(t, par)
                    if ahead:
                        transposed(t + 2, par)

                sweep(pe, body)


class Routing:

    def __init__(self, k, dve, chain, routed, sb):
        self.k, self.dve, self.chain, self.routed, NB = k, dve, chain, routed, k.NB
        self.tmp = [sb(f"t{i}", [P, NB, GR]) for i in range(5)]
        self.greater, self.equal = sb("greater", [P, NB, GR, GR]), sb("equal", [P, NB, GR, GR])
        self.rank, self.top8, self.wsum = sb("rank", [P, NB, GR]), sb("top8", [P, NB, 8]), sb("wsum", [P, NB])
        self.biased, self.masked, self.rest = (sb("biased", [P, NB, E]), sb("masked", [P, NB, E]),
                                               sb("rest", [P, NB, E]))
        cut = [NB * i // 3 for i in range(4)]
        self.steps = (self.bias_and_halves, self.group_scores, self.better, self.as_good, self.as_good_earlier,
                      self.ahead, self.keep, self.mask,
                      lambda: self.largest(0, NB // 2), lambda: self.largest(NB // 2, NB),
                      lambda: self.take_out(cut[0], cut[1]), lambda: self.take_out(cut[1], cut[2]),
                      lambda: self.take_out(cut[2], cut[3]), self.chosen, self.normalise, self.weights)

    def tt(self, out, x, y, op):
        self.chain.step(self.dve.tensor_tensor(out, x, y, op))

    def groups(self, t):
        return t[:].rearrange("p b (g e) -> p b g e", e=EG)

    def bias_and_halves(self):
        k, t = self.k, self.tmp
        self.tt(self.biased[:], k.sc[:], k.bias[:].unsqueeze(1).broadcast_to([P, k.NB, E]), ALU.add)
        self.chain.settle()
        e0, e1, e2, e3 = (self.groups(self.biased)[:, :, :, i] for i in range(EG))
        self.tt(t[0][:], e0, e1, ALU.max)
        self.tt(t[1][:], e0, e1, ALU.min)
        self.tt(t[2][:], e2, e3, ALU.max)
        self.tt(t[3][:], e2, e3, ALU.min)
        self.chain.settle()

    def group_scores(self):
        t = self.tmp
        self.tt(t[4][:], t[0][:], t[2][:], ALU.add)
        self.tt(t[1][:], t[0][:], t[1][:], ALU.add)
        self.tt(t[3][:], t[2][:], t[3][:], ALU.add)
        self.chain.settle()
        self.tt(t[1][:], t[1][:], t[3][:], ALU.max)
        self.chain.settle()
        self.tt(t[4][:], t[4][:], t[1][:], ALU.max)
        self.chain.settle()

    def pairs(self):
        shape = [P, self.k.NB, GR, GR]
        return self.tmp[4][:].unsqueeze(2).broadcast_to(shape), self.tmp[4][:].unsqueeze(3).broadcast_to(shape)

    def better(self):
        self.tt(self.greater[:], *self.pairs(), ALU.is_gt)

    def as_good(self):
        self.tt(self.equal[:], *self.pairs(), ALU.is_equal)
        self.chain.settle()

    def as_good_earlier(self):
        earlier = self.k.earlier[:].rearrange("p (g h) -> p g h", h=GR).unsqueeze(1)
        self.tt(self.equal[:], self.equal[:], earlier.broadcast_to([P, self.k.NB, GR, GR]), ALU.mult)
        self.chain.settle()

    def ahead(self):
        self.tt(self.greater[:], self.greater[:], self.equal[:], ALU.add)
        self.chain.settle()

    def keep(self):
        self.chain.step(self.dve.tensor_reduce(self.rank[:], self.greater[:], X, ALU.add))
        self.chain.settle()
        self.chain.step(self.dve.tensor_scalar(self.rank[:], self.rank[:], float(TOPG), None, ALU.is_lt))
        self.chain.settle()

    def mask(self):
        self.tt(self.groups(self.masked), self.groups(self.biased),
                self.rank[:].unsqueeze(3).broadcast_to([P, self.k.NB, GR, EG]), ALU.mult)
        self.chain.settle()
        self.chain.step(self.dve.tensor_scalar(self.masked[:], self.masked[:], 0.0, None, ALU.add))
        self.chain.settle()

    def largest(self, lo, hi):
        for b in range(lo, hi):
            self.chain.step(self.dve.max(self.top8[:, b, :], self.masked[:, b, :]))
        self.chain.settle()

    def take_out(self, lo, hi):
        for b in range(lo, hi):
            self.chain.step(self.dve.match_replace(self.rest[:, b, :], self.top8[:, b, :], self.masked[:, b, :],
                                                   -3.0e38))
        self.chain.settle()

    def chosen(self):
        self.tt(self.rest[:], self.rest[:], self.masked[:], ALU.not_equal)
        self.chain.settle()
        self.tt(self.rest[:], self.rest[:], self.k.sc[:], ALU.mult)
        self.chain.settle()

    def normalise(self):
        dve, chain, wsum = self.dve, self.chain, self.wsum
        chain.step(dve.tensor_reduce(wsum[:], self.rest[:], X, ALU.add))
        chain.settle()
        chain.step(dve.tensor_scalar(wsum[:], wsum[:], 1e-20, None, ALU.add))
        chain.settle()
        chain.step(dve.reciprocal(wsum[:], wsum[:]))
        chain.settle()
        chain.step(dve.tensor_scalar(wsum[:], wsum[:], ROUTED_SCALE, self.k.tg[:, TG_F1:TG_F1 + 1],
                                     ALU.mult, ALU.mult))
        chain.settle()

    def weights(self):
        self.dve.tensor_tensor(self.k.comb[:, :, SHARED:], self.rest[:],
                               self.wsum[:].unsqueeze(2).broadcast_to([P, self.k.NB, E]),
                               ALU.mult).then_inc(self.routed, 1)


class ExpertWeights:
    PARTS = 3

    def __init__(self, k, sem, sb):
        self.k = k
        self.loaded = [sem("w_loaded0"), sem("w_loaded1")]
        self.high_done, self.low_done = sem("w_high_done"), sem("w_low_done")
        self.raw = sb("w_raw", [P, 2, self.PARTS * D])
        self.h, self.l = (sb(n, [P, 2, self.PARTS * D], F32R) for n in ("w_high", "w_low"))

    def load(self, sp, e, ep):
        sp.dma_start(self.raw[:, ep], self.k.a["experts"][e]).then_inc(self.loaded[ep], 16)

    def high(self, act, ep, c):
        at = slice(c * D, (c + 1) * D)
        act.activation(self.h[:, ep, at], self.raw[:, ep, at], ACT.Copy).then_inc(self.high_done, 1)

    def low(self, pool, e, ep, c):
        at = slice(c * D, (c + 1) * D)
        pool.wait_ge(self.high_done, e * self.PARTS + c + 1)
        pool.tensor_tensor(self.l[:, ep, at], self.raw[:, ep, at], self.h[:, ep, at].bitcast(F32),
                           ALU.subtract).then_inc(self.low_done, 1)


def experts(k):
    nc, a, NB = k.nc, k.a, k.NB
    NE = a["experts"].shape[0]
    G = BANK // P
    BL = NB // G
    PAIRS = NE // 2
    WG, WU, WD, WN = 0, D, 2 * D, 3 * D
    w = k.weights
    PARTS, wh, wl = w.PARTS, w.h, w.l
    with ExitStack() as c:
        sem = lambda n: c.enter_context(nc.semaphore("e_" + n))
        sb = lambda n, s, dt=F32: c.enter_context(nc.sbuf_tensor("e_" + n, s, dt))
        pool_copied = sem("weights_of_tokens")
        g_ready, u_ready, y_ready = sem("g_ready"), sem("u_ready"), sem("y_ready")
        silu_done, gu_done, hi_done, lo_done, acc_done = (sem("silu_done"), sem("gu_done"), sem("hi_done"),
                                                          sem("lo_done"), sem("acc_done"))
        ce = sb("token_weight", [P, 2, NB])
        silu, gu = sb("silu", [P, 2, BANK]), sb("gu", [P, 2, BANK])
        guh, gul = sb("gu_high", [P, 2, BANK], F32R), sb("gu_low", [P, 2, BANK], F32R)
        route_chain, routed, stored = sem("route_chain"), sem("routed"), sem("stored")
        routing = Routing(k, nc.vector, Chain(nc.vector, route_chain), routed, sb)
        block = c.enter_context(nc.Block())

        def sweep(eng, body):
            body(0, True, False)
            with eng.Fori(1, PAIRS - 1) as it:
                body(it, False, False)
            body(PAIRS - 1, False, True)

        @block.sync
        def _(sp):
            with sp.Fori(0, PAIRS - 1) as it:
                for ep in range(2):
                    sp.wait_ge(w.low_done, (it * 2 + ep + 1) * PARTS)
                    w.load(sp, it * 2 + ep + 2, ep)
            for blk in range(BL):
                sp.wait_ge(acc_done, (NE - 1) * BL + blk + 3)
                at = slice(blk * G, (blk + 1) * G)
                sp.dma_start(a["out"][at].rearrange("b p d -> p b d"), k.xs[:, at, :]).then_inc(stored, 16)
            sp.wait_ge(stored, 16 * BL)

        @block.gpsimd
        def _(pool):
            def token_weights(e, ep):
                pool.tensor_copy(ce[:, ep, :], k.comb[:, :, e]).then_inc(pool_copied, 1)

            def low(s, par):
                pool.wait_ge(hi_done, s + 1)
                pool.tensor_tensor(gul[:, par], gu[:, par], guh[:, par].bitcast(F32), ALU.subtract)\
                    .then_inc(lo_done, 1)

            pool.sem_inc(lo_done, 2)
            token_weights(0, 0)
            def body(it, first, last):
                for ep in range(2):
                    e = it * 2 + ep
                    for blk in range(BL):
                        low(e * BL + blk, blk % 2)
                        if 1 <= blk <= PARTS and not (last and ep == 1):
                            if blk == 1:
                                pool.wait_ge(acc_done, e * BL + 2)
                                if not (first and ep == 1):
                                    token_weights(e + 1, 1 - ep)
                            w.low(pool, e + 1, 1 - ep, blk - 1)
                if first:
                    pool.wait_ge(routed, 1)
                    token_weights(SHARED, SHARED % 2)

            sweep(pool, body)

        @block.scalar
        def _(act):
            act.sem_inc(silu_done, 2)

            def step(s, par):
                act.wait_ge(g_ready, s + 1)
                act.wait_ge(gu_done, s + 1)
                act.activation(silu[:, par], k.bank[par][:], ACT.Silu).then_inc(silu_done, 1)
                act.wait_ge(gu_done, s + 3)
                act.activation(guh[:, par], gu[:, par], ACT.Copy).then_inc(hi_done, 1)

            def body(it, first, last):
                for ep in range(2):
                    for blk in range(BL):
                        step((it * 2 + ep) * BL + blk, blk % 2)
                        if 1 <= blk <= PARTS and not (last and ep == 1):
                            if blk == 1:
                                act.wait_ge(acc_done, (it * 2 + ep) * BL + 2)
                                act.wait_ge(w.loaded[1 - ep], (it + 1 + ep) * 16)
                            w.high(act, 1 - ep, blk - 1)

            sweep(act, body)

        @block.vector
        def _(dve):
            dve.sem_inc(gu_done, 2)
            dve.sem_inc(acc_done, 2)

            def gated(s, par):
                dve.wait_ge(silu_done, s + 3)
                dve.wait_ge(u_ready, s + 1)
                dve.wait_ge(lo_done, s + 1)
                dve.tensor_tensor(gu[:, par], silu[:, par], k.bank[2 + par][:], ALU.mult).then_inc(gu_done, 1)

            def add(e, ep, blk):
                if blk == 0:
                    dve.wait_ge(pool_copied, e + 1)
                dve.wait_ge(y_ready, e * BL + blk + 1)
                for j in range(G):
                    b = blk * G + j
                    xb = k.xs[:, b, :]
                    bank = k.bank[4 + blk % 2 * 2 + j // 2]
                    ins = dve.scalar_tensor_tensor(xb, bank[:, j % 2 * D:j % 2 * D + D], ce[:, ep, b:b + 1], xb,
                                                   ALU.mult, ALU.add)
                ins.then_inc(acc_done, 1)

            gated(0, 0)

            def body(it, first, last):
                for ep in range(2):
                    e = it * 2 + ep
                    for blk in range(BL):
                        if not (last and ep == 1 and blk == BL - 1):
                            gated(e * BL + blk + 1, 1 - blk % 2)
                        if first:
                            routing.steps[ep * BL + blk]()
                        add(e, ep, blk)

            sweep(dve, body)

        @block.tensor
        def _(pe):
            def gate_and_up(e, ep, blk):
                s, par = e * BL + blk, blk % 2
                if blk == 0:
                    pe.wait_ge(w.low_done, (e + 1) * PARTS)
                at = slice(blk * BANK, blk * BANK + BANK)
                for w0, bank, free, ready in ((WG, k.bank[par], silu_done, g_ready),
                                              (WU, k.bank[2 + par], gu_done, u_ready)):
                    pe.wait_ge(free, s + 1)
                    for kk in range(K2):
                        cols = slice(w0 + kk * P, w0 + kk * P + P)
                        ins = three_passes(pe, bank[:], wh[:, ep, cols], wl[:, ep, cols],
                                           k.hTh[:, kk, at], k.hTl[:, kk, at], kk == 0, kk == K2 - 1)
                    ins.then_inc(ready, 1)

            def down(e, ep, blk):
                s, par = e * BL + blk, blk % 2
                pe.wait_ge(hi_done, s + 1)
                pe.wait_ge(lo_done, s + 3)
                pe.wait_ge(acc_done, s + 1)
                for j in range(G):
                    out = k.bank[4 + par * 2 + j // 2][:, j % 2 * D:j % 2 * D + D]
                    t = slice(j * P, j * P + P)
                    ins = three_passes(pe, out, guh[:, par, t], gul[:, par, t], wh[:, ep, WD:WN], wl[:, ep, WD:WN],
                                       True, True)
                ins.then_inc(y_ready, 1)

            gate_and_up(0, 0, 0)

            def body(it, first, last):
                for ep in range(2):
                    e = it * 2 + ep
                    for blk in range(BL):
                        if blk < BL - 1:
                            gate_and_up(e, ep, blk + 1)
                        elif not (last and ep == 1):
                            gate_and_up(e + 1, 1 - ep, 0)
                        down(e, ep, blk)

            sweep(pe, body)


def layouts(i):
    import numpy as np

    f = {n: np.asarray(v) for n, v in i.items()}
    B = f["x"].shape[0]
    col = lambda v, p: np.ascontiguousarray(v.reshape(-1, p).T)
    rows = lambda v: np.ascontiguousarray(np.broadcast_to(v, (P, v.size)))
    halves = lambda v: v.reshape(64, 2, 8).transpose(1, 0, 2).reshape(P, 8)
    chunks = lambda v: v.reshape(-1, P, v.shape[-1]).transpose(1, 0, 2)
    per_expert = lambda w: w.transpose(0, 2, 1).reshape(w.shape[0], K2, P, P).transpose(0, 2, 1, 3).reshape(-1, P, D)
    gate = np.concatenate([f["L1_ffn_sh_gate"].reshape(2, P, D), f["L1_ffn_w_gate"]])
    up = np.concatenate([f["L1_ffn_sh_up"].reshape(2, P, D), f["L1_ffn_w_up"]])
    down = np.concatenate([f["L1_ffn_sh_down"].T.reshape(2, P, D), f["L1_ffn_w_down"].transpose(0, 2, 1)])
    tri = np.tril(np.ones((8, 8), np.float32), -1).reshape(-1)
    eye64 = np.eye(64, dtype=np.float32)
    win = chunks(f["L0_ffn_Win"])
    return {
        "x": f["x"],
        "ctx": f["ctx_1024"].reshape(B // 2, 2, P, D),
        "ctxT": f["ctx_1024"].reshape(B // 2, 2, P, K2, P).transpose(0, 4, 3, 1, 2),
        "ident": np.eye(P, dtype=np.float32),
        "eye2": np.concatenate([eye64, eye64]),
        "head_rows": np.repeat(np.eye(4, dtype=np.float32), 32, axis=0) * np.float32(32 ** -0.5),
        "gates": rows(np.concatenate([f["g_xattn"], f["g_ffn"], f["L1_xattn_gate"]])),
        "w1c": halves(f["L0_ffn_W1"]), "b1c": halves(f["L0_ffn_b1"]), "w2c": halves(f["L0_ffn_W2"]),
        "w2row": f["L0_ffn_W2"], "b1row": f["L0_ffn_b1"], "b2c": f["L0_ffn_b2"].reshape(64, 1),
        "binc": np.tile(f["L0_ffn_bin_"], 2).reshape(P, 1),
        "win": np.concatenate([win, win], axis=2),
        "wout0": np.concatenate([f["L0_ffn_Wout"], f["L0_ffn_bout"].reshape(1, D)]),
        "attn_w": np.concatenate([chunks(f["L1_xattn_" + n]).reshape(P, -1) for n in ("w_kv", "w_q", "w_out")], axis=1),
        "gammaT": col(f["L1_xattn_ln_gamma"], P), "betaT": col(f["L1_xattn_ln_beta"], P),
        "b_out": rows(f["L1_xattn_b_out"]),
        "gate_wT": chunks(f["L1_ffn_gate_w"].T), "gate_bias": rows(f["L1_ffn_gate_bias"]), "earlier": rows(tri),
        "experts": np.concatenate([per_expert(gate), per_expert(up), down], axis=2),
    }


def kernel(**inputs):
    import numpy as np
    import concourse.bacc as bacc
    from concourse.bass_utils import run_bass_kernel_spmd

    nc = bacc.Bacc("TRN2", target_bir_lowering=False, num_devices=1)
    arrays, aps = {}, {}
    for name, v in layouts(inputs).items():
        v = np.ascontiguousarray(v)
        arrays["in_" + name] = v
        aps[name] = nc.dram_tensor("in_" + name, v.shape, mybir.dt.from_np(v.dtype), kind="ExternalInput").ap()
    aps["out"] = nc.dram_tensor("out_x", inputs["x"].shape, F32, kind="ExternalOutput").ap()
    build(nc, aps)
    return run_bass_kernel_spmd(nc, [arrays], core_ids=[0]).results[0]["out_x"]
```
